# Optimizing a Trainium2 kernel written in Bass

```python
import numpy as np
import jax
import jax.numpy as jnp

def _softmax(x, axis=-1):
    return jax.nn.softmax(x, axis=axis)

def _gelu(x):
    return jax.nn.gelu(x, approximate=True)

def _silu(x):
    return jax.nn.silu(x)

def _sigmoid(x):
    return jax.nn.sigmoid(x)

def _layernorm(x, axis=-1, eps=1e-05):
    m = jnp.mean(x, axis=axis, keepdims=True)
    v = jnp.var(x, axis=axis, keepdims=True)
    return (x - m) / jnp.sqrt(v + eps)

def _scatter_add(tgt, idx, src, axis=0):
    return tgt.at[idx].add(src)

def _segment_sum(src, seg, n):
    return jax.ops.segment_sum(src, seg, n)
kernel_name = 'mk_vit_tower_cls_d1_tok_img1024_r4_911b40'

def setup_inputs(seed: int=0):
    np.random.seed(seed)
    _w = jnp.asarray

    def _rec_inputs():
        import jax
        import jax.numpy as jnp
        _rk = jax.random.key(seed)
        x = jax.random.uniform(jax.random.fold_in(_rk, 1), (32, 3, 256, 256), jnp.float32, 0.0, 1)
        cls_tok = 0.02 * jax.random.normal(jax.random.fold_in(_rk, 5), (1, 1, 256), jnp.float32)
        return (x, cls_tok)
    x, cls_tok = _rec_inputs()

    def _L0_tok_setup():
        import jax, jax.numpy as jnp
        import numpy as np
        _GRAY_W = (0.2989, 0.587, 0.114)
        key = jax.random.key(seed)
        x = jax.random.uniform(key, (32, 3, 256, 256), dtype=jnp.float32)
        sx = jnp.array([[-3.0, 0.0, 3.0], [-10.0, 0.0, 10.0], [-3.0, 0.0, 3.0]], dtype=jnp.float32)
        scharr = jnp.stack([sx, sx.T])[:, None, :, :]
        return {'x': x, 'scharr': scharr}
    _L0_tok_all = _L0_tok_setup()
    _L0_tok_in = {k: v for k, v in _L0_tok_all.items() if k in ('scharr',)}
    del _L0_tok_all

    def _L0_attn_setup():
        import jax, jax.numpy as jnp
        import numpy as np
        D_MODEL = 256
        NUM_HEADS = 16
        HEAD_DIM = D_MODEL // NUM_HEADS
        LN_EPS = 1e-05

        def _layernorm(x, gamma, beta):
            mu = jnp.mean(x, axis=-1, keepdims=True)
            var = jnp.mean(jnp.square(x - mu), axis=-1, keepdims=True)
            return (x - mu) * jax.lax.rsqrt(var + LN_EPS) * gamma + beta
        key = jax.random.key(seed)
        ks = jax.random.split(key, 7)
        B, S, D = (2, 512, D_MODEL)
        x = jax.random.normal(ks[0], (B, S, D), dtype=jnp.float32)
        lim1 = 1.0 / np.sqrt(D)
        W1 = jax.random.uniform(ks[1], (D, 4 * D), minval=-lim1, maxval=lim1, dtype=jnp.float32)
        b1 = jax.random.uniform(ks[2], (4 * D,), minval=-lim1, maxval=lim1, dtype=jnp.float32)
        W2 = jax.random.uniform(ks[3], (D, D), minval=-lim1, maxval=lim1, dtype=jnp.float32)
        b2 = jax.random.uniform(ks[4], (D,), minval=-lim1, maxval=lim1, dtype=jnp.float32)
        gamma = jnp.ones((D,), dtype=jnp.float32)
        beta = jnp.zeros((D,), dtype=jnp.float32)
        return {'x': x, 'W1': W1, 'b1': b1, 'W2': W2, 'b2': b2, 'gamma': gamma, 'beta': beta}
    _L0_attn_all = _L0_attn_setup()
    _L0_attn_in = {k: v for k, v in _L0_attn_all.items() if k in ('W1', 'b1', 'W2', 'b2', 'gamma', 'beta')}
    del _L0_attn_all

    def _L0_ffn_setup():
        import jax, jax.numpy as jnp
        import numpy as np
        E, G, TOPK = (32, 16, 2)
        HID, INTER, A_INTER = (256, 512, 128)
        CAP_FACTOR = 1.25
        SCALE = 0.05

        def _stats(x):
            mean = x.mean(-1, keepdims=True)
            std = jnp.std(x, axis=-1, keepdims=True, ddof=1)
            mn = x.min(-1, keepdims=True)
            mx = x.max(-1, keepdims=True)
            l2 = jnp.linalg.norm(x, axis=-1, keepdims=True)
            sp = (jnp.abs(x) < 1e-06).astype(x.dtype).mean(-1, keepdims=True)
            return jnp.concatenate([mean, std, mn, mx, l2, sp], -1)
        key = jax.random.key(seed)
        ks = jax.random.split(key, 8)
        B, N = (4, 256)
        s = lambda k, shape, sc: jax.random.normal(k, shape, jnp.float32) * sc
        return {'x': jax.random.normal(ks[0], (B, N, HID), jnp.float32), 'r1_w': s(ks[1], (HID // 2, HID + 6), 0.02), 'r1_b': jnp.zeros((HID // 2,), jnp.float32), 'r2_w': s(ks[2], (E, HID // 2), 0.02), 'w_up': s(ks[3], (E, 2 * INTER, HID), 0.02), 'w_down': s(ks[4], (E, HID, INTER), 0.02), 'a_up': s(ks[5], (G, 2 * A_INTER, HID), 0.02), 'a_down': s(ks[6], (G, HID, A_INTER), 0.02)}
    _L0_ffn_all = _L0_ffn_setup()
    _L0_ffn_in = {k: v for k, v in _L0_ffn_all.items() if k in ('r1_w', 'r1_b', 'r2_w', 'w_up', 'w_down', 'a_up', 'a_down')}
    del _L0_ffn_all
    return {'x': x, 'cls_tok': cls_tok, 'L0_tok_scharr': _L0_tok_in['scharr'], 'L0_attn_W1': _L0_attn_in['W1'], 'L0_attn_b1': _L0_attn_in['b1'], 'L0_attn_W2': _L0_attn_in['W2'], 'L0_attn_b2': _L0_attn_in['b2'], 'L0_attn_gamma': _L0_attn_in['gamma'], 'L0_attn_beta': _L0_attn_in['beta'], 'L0_ffn_r1_w': _L0_ffn_in['r1_w'], 'L0_ffn_r1_b': _L0_ffn_in['r1_b'], 'L0_ffn_r2_w': _L0_ffn_in['r2_w'], 'L0_ffn_w_up': _L0_ffn_in['w_up'], 'L0_ffn_w_down': _L0_ffn_in['w_down'], 'L0_ffn_a_up': _L0_ffn_in['a_up'], 'L0_ffn_a_down': _L0_ffn_in['a_down']}

def reference(x, cls_tok, L0_tok_scharr, L0_attn_W1, L0_attn_b1, L0_attn_W2, L0_attn_b2, L0_attn_gamma, L0_attn_beta, L0_ffn_r1_w, L0_ffn_r1_b, L0_ffn_r2_w, L0_ffn_w_up, L0_ffn_w_down, L0_ffn_a_up, L0_ffn_a_down):
    import jax
    import jax.numpy as jnp

    def _L0_tok_ref(x, scharr):
        import jax, jax.numpy as jnp
        import numpy as np
        _GRAY_W = (0.2989, 0.587, 0.114)
        w = jnp.asarray(_GRAY_W, dtype=x.dtype)
        gray = jnp.einsum('bchw,c->bhw', x, w)[:, None]
        edges = jax.lax.conv_general_dilated(gray, scharr, window_strides=(1, 1), padding='SAME', dimension_numbers=('NCHW', 'OIHW', 'NCHW'))
        abs_edges = jnp.sqrt(jnp.square(edges))
        edge = abs_edges.sum(axis=1) / 2
        return edge

    def _L0_attn_ref(x, W1, b1, W2, b2, gamma, beta):
        import jax, jax.numpy as jnp
        import numpy as np
        D_MODEL = 256
        NUM_HEADS = 16
        HEAD_DIM = D_MODEL // NUM_HEADS
        LN_EPS = 1e-05

        def _layernorm(x, gamma, beta):
            mu = jnp.mean(x, axis=-1, keepdims=True)
            var = jnp.mean(jnp.square(x - mu), axis=-1, keepdims=True)
            return (x - mu) * jax.lax.rsqrt(var + LN_EPS) * gamma + beta
        B, S, D = x.shape
        H, Dh = (NUM_HEADS, HEAD_DIM)
        x_proj = jax.nn.silu(x @ W1 + b1)
        u, v, q, k = jnp.split(x_proj, 4, axis=-1)
        qh = q.reshape(B, S, H, Dh)
        kh = k.reshape(B, S, H, Dh)
        vh = v.reshape(B, S, H, Dh)
        scores = jnp.einsum('bqhd,bkhd->bhqk', qh, kh)
        attn = jax.nn.silu(scores) / S
        av = jnp.einsum('bhqk,bkhd->bqhd', attn, vh).reshape(B, S, D)
        y = _layernorm(av * u, gamma, beta) @ W2 + b2
        return y

    def _L0_ffn_ref(x, r1_w, r1_b, r2_w, w_up, w_down, a_up, a_down):
        import jax, jax.numpy as jnp
        import numpy as np
        E, G, TOPK = (32, 16, 2)
        HID, INTER, A_INTER = (256, 512, 128)
        CAP_FACTOR = 1.25
        SCALE = 0.05

        def _stats(x):
            mean = x.mean(-1, keepdims=True)
            std = jnp.std(x, axis=-1, keepdims=True, ddof=1)
            mn = x.min(-1, keepdims=True)
            mx = x.max(-1, keepdims=True)
            l2 = jnp.linalg.norm(x, axis=-1, keepdims=True)
            sp = (jnp.abs(x) < 1e-06).astype(x.dtype).mean(-1, keepdims=True)
            return jnp.concatenate([mean, std, mn, mx, l2, sp], -1)
        B, N, C = x.shape
        xf = x.reshape(-1, C)
        T = xf.shape[0]
        cap = int(CAP_FACTOR * T / E)
        ri = jnp.concatenate([xf, _stats(xf)], -1)
        h = jax.nn.gelu(ri @ r1_w.T + r1_b, approximate=False)
        probs = jax.nn.softmax(h @ r2_w.T, -1)
        topp, topi = jax.lax.top_k(probs, TOPK)
        wnorm = topp / topp.sum(-1, keepdims=True)
        eids = jnp.arange(E)
        hit = topi[..., None] == eids
        routed = hit.any(1)
        Wc = jnp.where(hit, wnorm[..., None], 0.0).sum(1)
        score = jnp.where(routed, probs, -jnp.inf)
        idx = jnp.argsort(-score, axis=0)[:cap].T
        valid = jnp.take_along_axis(routed.T, idx, 1)
        w = jnp.take_along_axis(Wc.T, idx, 1) * valid
        xe = xf[idx]
        up = jnp.einsum('eci,eji->ecj', xe, w_up)
        gate, upv = jnp.split(up, 2, axis=-1)
        hact = jax.nn.silu(gate) * upv
        ye = jnp.einsum('ecj,eoj->eco', hact, w_down)
        out = jnp.zeros((T, C), xf.dtype).at[idx.reshape(-1)].add((w[..., None] * ye).reshape(-1, C))
        Wmask = jnp.zeros((T, E), xf.dtype).at[idx, eids[:, None]].add(w)
        gw = SCALE * Wmask.reshape(T, G, E // G).sum(-1)
        aup = jnp.einsum('tc,gjc->tgj', xf, a_up)
        ag, av = jnp.split(aup, 2, axis=-1)
        ah = jax.nn.silu(ag) * av
        ay = jnp.einsum('tgj,goj->tgo', ah, a_down)
        out = out + jnp.einsum('tg,tgo->to', gw, ay)
        return out.reshape(B, N, C)
    h = _L0_tok_ref(x, L0_tok_scharr)
    h = jnp.concatenate([jnp.broadcast_to(cls_tok, (h.shape[0], 1, h.shape[2])), h], axis=1)
    h = h + _L0_attn_ref(_layernorm(h, axis=-1), L0_attn_W1, L0_attn_b1, L0_attn_W2, L0_attn_b2, L0_attn_gamma, L0_attn_beta)
    h = h + _L0_ffn_ref(_layernorm(h, axis=-1), L0_ffn_r1_w, L0_ffn_r1_b, L0_ffn_r2_w, L0_ffn_w_up, L0_ffn_w_down, L0_ffn_a_up, L0_ffn_a_down)
    return h

_drawn_inputs = setup_inputs


def setup_inputs(seed=0):
    import zlib

    import numpy as np

    out = dict(_drawn_inputs(seed))
    spreads = {'L0_attn_gamma': (1.0, 0.2), 'L0_attn_beta': (0.0, 0.4), 'L0_ffn_r1_b': (0.0, 0.8)}
    factors = {'cls_tok': 5.783,
     'L0_attn_b2': 4.421,
     'L0_ffn_r1_w': 8.0,
     'L0_ffn_r2_w': 8.0,
     'L0_ffn_w_up': 8.0,
     'L0_ffn_w_down': 8.0,
     'L0_ffn_a_up': 8.0,
     'L0_ffn_a_down': 8.0}
    for name, (base, spread) in spreads.items():
        noise = np.random.default_rng([zlib.crc32(name.encode()), seed]).standard_normal(out[name].shape)
        drawn = base * np.exp(spread * noise) if base else spread * noise
        out[name] = jnp.asarray(drawn.astype(out[name].dtype))
    for name, factor in factors.items():
        out[name] = (out[name] * factor).astype(out[name].dtype)
    return out
```

```python
from contextlib import ExitStack

import numpy as np

import concourse.bass as bass
from concourse import mybir

P = 128
C3 = 3
D = 256
R = 256
S = R + 1
H = 16
DH = D // H
NE = 32
HID = 128
NST = 8
INTER = 512
AINTER = 128
NG = 16
SLOTS = 384
ROW = 260
LN_EPS = 1e-5
GRAY = (0.2989, 0.587, 0.114)
CAP_FACTOR = 1.25
OOB = 1 << 20

CI = 0
CSH = CI + 128
CMK = CSH + 192
CMV = CMK + 256
CBE = CMV + 512
CLE = CBE + 128
CIE = CLE + 128
CSB = CIE + 32
CTK = CSB + 1
CTJ = CTK + 4
CTM = CTJ + 8
CTI = CTM + 32
CFI = CTI + 65
CRS = CFI + 3
NC_ = CRS + 1


def constants(nb):
    c = np.zeros((P, NC_), np.float32)
    p = np.arange(P)
    c[:, CI:CI + 128] = np.eye(128)
    for dy in range(3):
        for r in range(64):
            c[r + dy, CSH + dy * 64 + r] = 1
    for a in range(2):
        for copy in range(3):
            c[p, CMK + a * 128 + copy * 32 + 8 * a + p % 8] = 1
    for tl in range(8):
        for a in range(2):
            h = a * 8 + tl
            for s in range(3):
                c[s * 32 + h, CMV + (tl * 2 + a) * 32:CMV + (tl * 2 + a) * 32 + DH] = 1
    ch, e = p // 32, p % 32
    c[:, CBE:CBE + 128] = e[:, None] == e[None, :]
    c[:, CLE:CLE + 128] = (e[:, None] == e[None, :]) & (ch[:, None] < ch[None, :])
    c[:, CIE:CIE + 32] = np.arange(32) - 64
    c[:, CSB] = e * SLOTS - 1 - OOB
    jn = nb // 4
    for t in range(nb):
        c[t, CTK + t // jn] = 1
        c[t, CTJ + t % jn] = 1
        c[(t // jn) * 32:(t // jn) * 32 + 32, CTM + t] = 1
    for t in range(2 * nb):
        q = (t % (2 * jn)) * 4 + t // (2 * jn)
        c[:, CTI + q] = (t // 2) * S + 1 + (t % 2) * 128 + p
    c[:nb, CTI + 2 * nb] = np.arange(nb) * S
    c[:, CRS] = 1
    c[5, CRS] = 1.0 / D
    for st in range(3):
        c[:, CFI + st] = nb * S + st * P + p
    return c


def build(nc, x, cls_rows, w1, b1uv, b1qk, w2, b2, gb, taps, r1w, r1s, r1b, r2w, wexp, wadp, consts, out,
          NB=32, CAP=321):
    f32, f32r, i32, u32 = mybir.dt.float32, mybir.dt.float32r, mybir.dt.int32, mybir.dt.uint32
    ALU, ACT, AX = mybir.AluOpType, mybir.ActivationFunctionType, mybir.AxisListType

    NT = 2 * NB
    NTOK = NB * S
    JN = NB // 4
    CH = JN * S
    ctx = ExitStack()
    with ctx:
        names = set()

        def sb(name, shape, dt=f32):
            return ctx.enter_context(nc.sbuf_tensor(name, shape, dt))

        def sem(name):
            assert name not in names
            names.add(name)
            return ctx.enter_context(nc.semaphore(name))

        def dram(name, shape, dt=f32):
            return nc.dram_tensor(name, shape, dt, kind="Internal").ap()

        xf_dram = dram("xf_dram", [NT, P, D])
        pre_dram = dram("pre_dram", [NB, P, R])
        cls_av = dram("cls_av", [NB, D])
        routed_rows = dram("routed_rows", [NE * SLOTS, ROW])

        cst = sb("cst", [P, NC_])
        ident = cst[:, CI:CI + 128]
        stats8 = sb("stats8", [P, 2, NST])
        n05 = sb("n05", [P, 6])
        r1b_c = sb("r1b_c", [P, 1])
        r2w_sb = sb("r2w_sb", [P, NE])
        cls_xf = sb("cls_xf", [P, D])
        pre_cls = sb("pre_cls", [P, P])
        eps1 = LN_EPS

        ph1 = ExitStack()

        def s1(name, shape, dt=f32):
            return ph1.enter_context(nc.sbuf_tensor(name, shape, dt))

        w1s = s1("w1s", [P, 2, 2, 1024], f32r)
        w2s = s1("w2s", [P, 2, 2, D], f32r)
        r1ws = s1("r1ws", [P, 2, 2, HID], f32r)
        r1st = s1("r1st", [96, HID])
        band = s1("band", [96, 2, 3, 128], f32r)
        b1uv_sb = s1("b1uv_sb", [P, 512])
        b1qk_sb = s1("b1qk_sb", [P, 4])
        bias2 = s1("bias2", [P, D])
        kc = s1("kc", [P, 2, 2, 128], f32r)
        qc = s1("qc", [P, 2, 2, 128], f32r)
        vc = s1("vc", [96, 4, 128], f32r)
        uvc = s1("uvc", [P, 512])
        ccv = s1("ccv", [P, D])
        halo = s1("halo", [96, 8, 258], f32r)
        qs = [s1(f"qs{i}", [96, 8, D], f32r) for i in range(2)]
        ks = [s1(f"ks{i}", [96, 2, 8, D], f32r) for i in range(2)]
        uvp = s1("uvp", [P, 2, 512])
        stt = s1("stt", [96, D])
        ones = s1("ones", [P, 1])
        bn = {k: s1("bn" + k, [P, 2, 6]) for k in "azhx"}
        mv = {k: s1("mv" + k, [P, 2, 2]) for k in "azhx"}
        ve = {k: s1("ve" + k, [P, 2]) for k in "azh"}
        rs = {k: s1("rs" + k, [P, 2]) for k in "azh"}
        spare = s1("spare", [1, 1])
        sq = s1("sq", [P, 2, 2])

        ps_s = [ctx.enter_context(nc.psum_tensor(f"ps_s{i}", [P, 2, 2, D], f32)) for i in range(2)]
        ps_av = [ctx.enter_context(nc.psum_tensor(f"ps_av{i}", [P, 512], f32)) for i in range(2)]
        ps_f = [ctx.enter_context(nc.psum_tensor(f"ps_f{i}", [P, 512], f32)) for i in range(2)]

        def wait(eng, s, value):
            if isinstance(value, int) and value <= 0:
                return
            eng.wait_ge(s, value)

        def mm3(o, lhs, rhs, first, last):
            lh, ll = lhs
            rh, rl = rhs
            nc.tensor.matmul(o, lh, rh, start=first, stop=False)
            nc.tensor.matmul(o, ll, rh, start=False, stop=False)
            return nc.tensor.matmul(o, lh, rl, start=False, stop=last)


        staging = ExitStack()
        stage = staging.enter_context(nc.sbuf_tensor("stage", [P, 6184], f32))
        w1f = stage[:, 0:2048].rearrange("p (k n) -> p k n", k=2)
        w2f = stage[:, 2048:2560].rearrange("p (k n) -> p k n", k=2)
        r1f = stage[:, 2560:2816].rearrange("p (k n) -> p k n", k=2)
        tapf = stage[:, 2816:2834]
        gbf = stage[:, 2834:2838]
        b2f = stage[:, 2840:3096]
        betaf = stage[:, 3096:3352].rearrange("p (k n) -> p k n", k=2)
        w2g = stage[:, 3352:3864].rearrange("p (k n) -> p k n", k=2)
        bandf = stage[:, 3864:4248].rearrange("p (x n) -> p x n", x=3)
        clsf = stage[:, 4248:4504]
        clsn = stage[:, 4504:4760]
        clst = stage[:, 4760:5016].rearrange("p (k n) -> p k n", k=2)
        qkcf = stage[:, 5016:5144].rearrange("p (m n) -> p m n", m=4)
        kqf = stage[:, 5144:5656].rearrange("p (m a n) -> p m a n", m=2, a=2)
        vcf = stage[:, 5656:6168]
        sccf = stage[:, 6168:6184]
        fill = staging.enter_context(nc.sbuf_tensor("fill", [P, 3, ROW], f32))
        loaded, r1s_loaded, filled = sem("loaded"), sem("r1s_loaded"), sem("filled")
        su_dve, su_act, su_pool, su_pe = sem("su_dve"), sem("su_act"), sem("su_pool"), sem("su_pe")
        with nc.Block() as block:
            loads = [
                (cst[:, :], consts), (w1f, w1.rearrange("(k p) n -> p k n", p=P)), (w2f, w2.rearrange("(k p) n -> p k n", p=P)),
                (r1f, r1w.rearrange("(k p) n -> p k n", p=P)), (tapf, taps), (gbf, gb), (b2f, b2), (clsf, cls_rows),
                (b1uv_sb[:, :], b1uv), (b1qk_sb[:, :], b1qk), (r1b_c[:, :], r1b), (r2w_sb[:, :], r2w),
            ]

            @block.sync
            def _(sp):
                for o, i in loads:
                    sp.dma_start(o, i).then_inc(loaded, 16)
                sp.wait_ge(su_dve, 3)
                for st in range(3):
                    sp.dma_start(routed_rows.rearrange("(e n p) w -> n p e w", n=3, p=P)[st],
                                 fill[:, st, :].unsqueeze(1).to_broadcast([P, NE, ROW])).then_inc(filled, 16)
                sp.dma_start(out[NTOK:NTOK + SLOTS, :].rearrange("(n p) w -> p n w", p=P), fill[:, :, 0:D]).then_inc(filled, 16)
                sp.wait_ge(filled, 64)
                sp.wait_ge(su_pool, 1)
                sp.dma_start(r1st[0:6, :], r1s).then_inc(r1s_loaded, 16)
                sp.wait_ge(r1s_loaded, 16)

            @block.gpsimd
            def _(pool):
                nc.gpsimd.memset(r1st[:, :], 0.0).then_inc(su_pool, 1)
                nc.gpsimd.memset(stt[:, :], 0.0)
                nc.gpsimd.memset(stats8[:, :, :], 0.0)
                nc.gpsimd.memset(n05[:, 0:2], -0.5)
                nc.gpsimd.memset(n05[:, 2:6], 0.5)
                nc.gpsimd.memset(ones[:, :], 1.0)
                nc.gpsimd.memset(halo[:, :, :].bitcast(f32), 0.0)
                for i in range(2):
                    nc.gpsimd.memset(ks[i][:, :, :, :].bitcast(f32), 0.0)
                    nc.gpsimd.memset(qs[i][:, :, :].bitcast(f32), 0.0)
                nc.gpsimd.memset(vcf, 0.0).then_inc(su_pool, 1)
                pool.wait_ge(su_dve, 3)
                pool.wait_ge(su_pool, 2)
                nc.gpsimd.tensor_tensor(rs["z"][:, 0:1], ve["z"][:, 0:1], n05[:, 0:1], ALU.pow).then_inc(su_pool, 1)

            @block.vector
            def _(dve):
                tally = [0]

                def link(ins):
                    tally[0] += 1
                    ins.then_inc(su_dve, 1)
                    dve.wait_ge(su_dve, tally[0])

                dve.wait_ge(loaded, 16 * len(loads))
                nc.vector.memset(fill[:, :, :], 0.0)
                link(nc.vector.bn_stats(bn["z"][:, 0, :], clsf))
                link(nc.vector.bn_aggr(mv["z"][:, 0, :], bn["z"][:, 0, :]))
                nc.vector.tensor_copy(fill[:, :, ROW - 1].bitcast(i32), cst[:, CFI:CFI + 3])
                link(nc.vector.tensor_scalar(ve["z"][:, 0:1], mv["z"][:, 0, 1:2], LN_EPS, None, ALU.add))
                link(nc.vector.tensor_copy(w1s[:, 0, :, :], w1f))
                dve.wait_ge(su_pool, 3)
                link(nc.vector.tensor_scalar(clsn, clsf, mv["z"][:, 0, 0:1], rs["z"][:, 0:1], ALU.subtract, ALU.mult))
                for kt in range(2):
                    nc.vector.tensor_scalar(betaf[:, kt, :], ident, 0.0, gbf[:, 2 + kt:3 + kt], ALU.mult, ALU.add)
                    last = nc.vector.tensor_scalar(w2g[:, kt, :], w2f[:, kt, :], gbf[:, kt:kt + 1], None, ALU.mult)
                link(last)
                nc.vector.tensor_copy(w2s[:, 0, :, :], w2g)
                link(nc.vector.tensor_copy(r1ws[:, 0, :, :], r1f))
                nc.vector.tensor_tensor(w1s[:, 1, :, :], w1f, w1s[:, 0, :, :].bitcast(f32), ALU.subtract)
                nc.vector.tensor_tensor(w2s[:, 1, :, :], w2g, w2s[:, 0, :, :].bitcast(f32), ALU.subtract)
                nc.vector.tensor_tensor(r1ws[:, 1, :, :], r1f, r1ws[:, 0, :, :].bitcast(f32), ALU.subtract)
                for dy in range(3):
                    for dx in range(3):
                        for o in range(2):
                            dst = bandf[0:96, dx, 64 * o:64 * o + 64]
                            shift = cst[0:96, CSH + 64 * dy:CSH + 64 * dy + 64]
                            tap = tapf[0:96, o * 9 + dy * 3 + dx:o * 9 + dy * 3 + dx + 1]
                            if dy == 0:
                                last = nc.vector.tensor_scalar(dst, shift, tap, None, ALU.mult)
                            else:
                                last = nc.vector.scalar_tensor_tensor(dst, shift, tap, dst, ALU.mult, ALU.add)
                    link(last)
                link(nc.vector.tensor_copy(band[:, 0, :, :], bandf[0:96]))
                nc.vector.tensor_tensor(band[:, 1, :, :], bandf[0:96], band[:, 0, :, :].bitcast(f32), ALU.subtract)
                dve.wait_ge(su_pe, 1)
                link(nc.vector.tensor_copy(clst, ps_f[0][:, 0:256].rearrange("p (k n) -> p k n", k=2)))
                dve.wait_ge(su_pe, 3)
                nc.vector.tensor_tensor(uvp[:, 0, :], ps_f[1][:, :], b1uv_sb[:, :], ALU.add)
                link(nc.vector.tensor_tensor(bias2[:, :], ps_av[0][:, 0:256], b2f, ALU.add))
                dve.wait_ge(su_act, 1)
                for m, src in enumerate((2, 0)):
                    for a in range(2):
                        last = nc.vector.tensor_scalar(kqf[:, m, a, :], cst[:, CMK + 128 * a:CMK + 128 * a + 128],
                                                       qkcf[:, src + a, 0:1], None, ALU.mult)
                dve.wait_ge(su_pool, 2)
                link(nc.vector.tensor_tensor(
                    vcf[0:96, :].rearrange("p (tl a x) -> p tl a x", tl=8, a=2)[:, :, :, 0:16],
                    cst[0:96, CMV:CMV + 512].rearrange("p (tl a x) -> p tl a x", tl=8, a=2)[:, :, :, 0:16],
                    uvc[0:96, 256:512].rearrange("p (a tl d) -> p tl a d", a=2, tl=8), ALU.mult))
                nc.vector.tensor_copy(kc[:, 0, :, :], kqf[:, 0, :, :])
                nc.vector.tensor_copy(qc[:, 0, :, :], kqf[:, 1, :, :])
                link(nc.vector.tensor_copy(vc[:, :, :].rearrange("p t c -> p (t c)"), vcf[0:96, :]))
                nc.vector.tensor_tensor(kc[:, 1, :, :], kqf[:, 0, :, :], kc[:, 0, :, :].bitcast(f32), ALU.subtract)
                nc.vector.tensor_tensor(qc[:, 1, :, :], kqf[:, 1, :, :], qc[:, 0, :, :].bitcast(f32), ALU.subtract)
                vrow = vc[32:64, :, :].rearrange("p t c -> p (t c)")
                nc.vector.tensor_tensor(vrow, vcf[32:64, :], vrow.bitcast(f32), ALU.subtract)
                dve.wait_ge(r1s_loaded, 16)
                nc.vector.tensor_scalar(r1st[:, :], r1st[:, :], cst[0:96, CRS:CRS + 1], None, ALU.mult)
                dve.wait_ge(su_act, 2)
                link(nc.vector.tensor_tensor(ccv[0:32, :].rearrange("p (h d) -> p h d", d=DH),
                                             uvc[0:32, 256:512].rearrange("p (h d) -> p h d", d=DH),
                                             sccf[0:32, :].unsqueeze(2).to_broadcast([32, H, DH]), ALU.mult))

            @block.tensor
            def _(pe):
                pe.wait_ge(su_dve, 5)
                for kt in range(2):
                    last = nc.tensor.transpose(ps_f[0][:, 128 * kt:128 * kt + 128], clsn[:, 128 * kt:128 * kt + 128], ident)
                last.then_inc(su_pe, 1)
                pe.wait_ge(su_dve, 12)
                for m in range(4):
                    for kt in range(2):
                        last = nc.tensor.matmul(ps_s[0][:, 0, 0, 32 * m:32 * m + 32], w1f[:, kt, 512 + 128 * m:640 + 128 * m],
                                                clst[:, kt, 0:32], start=kt == 0, stop=kt == 1)
                last.then_inc(su_pe, 1)
                for kt in range(2):
                    nc.tensor.matmul(ps_f[1][:, :], clst[:, kt, :], w1f[:, kt, 0:512], start=kt == 0, stop=kt == 1)
                for kt in range(2):
                    last = nc.tensor.matmul(ps_av[0][:, 0:256], betaf[:, kt, :], w2f[:, kt, :], start=kt == 0, stop=kt == 1)
                last.then_inc(su_pe, 1)
                pe.wait_ge(su_dve, 14)
                for a in range(2):
                    last = nc.tensor.matmul(ps_av[1][0:32, 0:16], qkcf[:, a, :], kqf[:, 0, a, 0:16], start=a == 0, stop=a == 1)
                last.then_inc(su_pe, 1)

            @block.scalar
            def _(act):
                act.wait_ge(su_pe, 2)
                act.wait_ge(loaded, 16 * len(loads))
                for m in range(4):
                    nc.scalar.activation(qkcf[:, m, :], ps_s[0][:, 0, 0, 32 * m:32 * m + 32], ACT.Silu, bias=b1qk_sb[:, m:m + 1])
                act.wait_ge(su_dve, 13)
                nc.scalar.activation(uvc[:, :], uvp[:, 0, :], ACT.Silu).then_inc(su_act, 1)
                act.wait_ge(su_pe, 4)
                nc.scalar.activation(sccf[0:32, :], ps_av[1][0:32, 0:16], ACT.Silu).then_inc(su_act, 1)

        staging.close()

        xb = s1("xb", [P, 2, C3, D])
        g = s1("g", [P, 2, D])
        ghl = s1("ghl", [P, 4, D], f32r)
        absx = s1("absx", [P, 2, D])
        absy = s1("absy", [P, 2, D])
        h0 = s1("h0", [P, 2, D])
        h0b = [s1(f"h0b{i}", [P, 2, D]) for i in range(4)]
        xn = s1("xn", [P, 2, D])
        xt = s1("xt", [P, 2, 2, D], f32r)
        qk = s1("qk", [P, 4, D])
        qkh = s1("qkh", [P, 4, D], f32r)
        qkl = s1("qkl", [P, 4, D], f32r)
        uv = [s1(f"uv{i}", [P, 2, 512]) for i in range(2)]
        at = [s1(f"at{i}", [P, 2, 2, D]) for i in range(4)]
        clc = s1("clc", [96, 512])
        cls_s = s1("cls_s", [96, D], f32r)
        va = s1("va", [P, 2, D])
        va2 = s1("va2", [P, D])
        crow = s1("crow", [1, D])
        avs = s1("avs", [P, 4, D])
        y = s1("y", [P, 2, D])
        z = s1("z", [P, 2, D])
        zt = s1("zt", [P, 2, 2, D], f32r)
        h2 = s1("h2", [P, 2, D])
        xf = s1("xf", [P, 2, D])
        axf = s1("axf", [P, 2, D])
        xft = s1("xft", [P, 2, 2, D], f32r)
        pre = s1("pre", [P, R])
        x_loaded, gray_a, gray_sum, gray_hi, gray_split = (sem(n) for n in ("x_loaded", "gray_a", "gray_sum", "gray_hi", "gray_split"))
        halo_loaded, conv_done, abs_done, h0_done, h0b_done = (sem(n) for n in ("halo_loaded", "conv_done", "abs_done", "h0_done", "h0b_done"))
        stat_a, ve_a, rs_a, xn_done, xt_ps, xt_hi, xt_done = (sem(n) for n in ("stat_a", "ve_a", "rs_a", "xn_done", "xt_ps", "xt_hi", "xt_done"))
        qk_ps, qk_act, qk_hi, qk_lo, stacked, uv_ps, uv_sum, uv_act = (sem(n) for n in ("qk_ps", "qk_act", "qk_hi", "qk_lo", "stacked", "uv_ps", "uv_sum", "uv_act"))
        cls_ps, cls_act, cls_hi, cls_ready, scores, attn, av_ps, av_out = (sem(n) for n in ("cls_ps", "cls_act", "cls_hi", "cls_ready", "scores", "attn", "av_ps", "av_out"))
        va_done, va_sum, crow_done, crow_out, avt_ps, y_done = (sem(n) for n in ("va_done", "va_sum", "crow_done", "crow_out", "avt_ps", "y_done"))
        stat_z, ve_z, rs_z, z_done, zt_ps, zt_hi, zt_done, w2_ps, h2_done, h2_out = (sem(n) for n in ("stat_z", "ve_z", "rs_z", "z_done", "zt_ps", "zt_hi", "zt_done", "w2_ps", "h2_done", "h2_out"))
        stat_h, ve_h, rs_h, xf_done, xf_out, axf_done = (sem(n) for n in ("stat_h", "ve_h", "rs_h", "xf_done", "xf_out", "axf_done"))
        stat_x, mean_sq, var_sq, sq_root, st_done, xft_ps, xft_hi, xft_done, stt_done, r1_ps, pre_done = (sem(n) for n in ("stat_x", "mean_sq", "var_sq", "sq_root", "st_done", "xft_ps", "xft_hi", "xft_done", "stt_done", "r1_ps", "pre_done"))
        pre_out = sem("pre_out")
        bna, bnz, bnh, bnx = (sem(n) for n in ("bna", "bnz", "bnh", "bnx"))

        def has(m):
            return not isinstance(m, int) or 0 <= m < NB

        def steps(eng, body):
            n0, per = 3, 4
            loops = max(0, (NB - 4 - n0) // per)
            for n in range(-3, n0):
                body(n, n % 4)
            if loops > 0:
                with eng.Fori(0, loops) as i:
                    for k in range(per):
                        body(i * per + (n0 + k), (n0 + k) % 4)
            for n in range(n0 + per * loops, NB + 2):
                body(n, n % 4)

        def av_count(m, t):
            return 4 * m + t + 1

        def st_count(m):
            return 4 * (m + 1) + 4 if not (isinstance(m, int) and m == NB - 1) else 4 * NB + 1

        UNITS = ["E", "G0", "D0", "D1", "B0", "A0", "B1", "B2", "D2", "B3", "D3", "A1", "B4", "D4"]
        LAG = {"E": 0, "G": -2, "D": -1, "B": 1, "A": 2}
        READ = {"E": (cls_act, 1, 1), "G0": (pre_done, 1, 1), "D0": (y_done, 2, 1), "D1": (y_done, 2, 2),
                "B0": (xt_done, 1, 1), "A0": (abs_done, 2, 1), "A1": (abs_done, 2, 2),
                "B1": (qk_act, 2, 1), "B2": (qk_act, 2, 2), "B3": (uv_sum, 2, 1), "B4": (uv_sum, 2, 2),
                "D2": (zt_done, 1, 1), "D3": (h2_done, 1, 1), "D4": (xft_done, 1, 1)}

        def bank_free(pe, n, unit):
            k = UNITS.index(unit) - 2
            for _ in range(14):
                step, u = (n, UNITS[k]) if k >= 0 else (n - 1, UNITS[k + 14])
                m = step + LAG[u[0]]
                if has(m):
                    s, per, ev = READ[u]
                    pe.wait_ge(s, m * per + ev)
                    return
                k -= 2
                if k < -14:
                    return

        def bank(unit):
            return ps_f[UNITS.index(unit) % 2]

        images = ExitStack()
        block = images.enter_context(nc.Block())

        @block.tensor
        def _(pe):
            def conv(n, m, hf, unit):
                if hf == 0:
                    pe.wait_ge(halo_loaded, 64 * (m + 1))
                bank_free(pe, n, unit)
                for par in range(2):
                    o = bank(unit)[:, 256 * par:256 * par + 256]
                    j = 2 * hf + par
                    for dx in range(3):
                        last = mm3(o, (band[:, 0, dx, :], band[:, 1, dx, :]),
                                   (halo[:, j, dx:dx + 256], halo[:, 4 + j, dx:dx + 256]), dx == 0, dx == 2)
                last.then_inc(conv_done, 1)

            def transposes(n, unit, src, ready, value, done):
                pe.wait_ge(ready, value)
                bank_free(pe, n, unit)
                for hf in range(2):
                    for kt in range(2):
                        last = nc.tensor.transpose(bank(unit)[:, kt * 256 + hf * 128:kt * 256 + hf * 128 + 128],
                                                   src[:, hf, kt * 128:kt * 128 + 128], ident)
                last.then_inc(done, 1)

            def proj_qk(n, m, kind, unit):
                bank_free(pe, n, unit)
                if kind == 0:
                    pe.wait_ge(xt_done, m + 1)
                for a in range(2):
                    col = 512 + 256 * kind + 128 * a
                    for kt in range(2):
                        last = mm3(bank(unit)[:, 256 * a:256 * a + 256],
                                   (w1s[:, 0, kt, col:col + 128], w1s[:, 1, kt, col:col + 128]),
                                   (xt[:, 0, kt, :], xt[:, 1, kt, :]), kt == 0, kt == 1)
                last.then_inc(qk_ps, 1)

            def proj_uv(n, m, hf, unit):
                bank_free(pe, n, unit)
                for kt in range(2):
                    last = mm3(bank(unit)[:, :],
                               (xt[:, 0, kt, hf * 128:hf * 128 + 128], xt[:, 1, kt, hf * 128:hf * 128 + 128]),
                               (w1s[:, 0, kt, 0:512], w1s[:, 1, kt, 0:512]), kt == 0, kt == 1)
                last.then_inc(uv_ps, 1)

            def cls_scores(n, m):
                pe.wait_ge(qk_hi, 2 * m + 2)
                pe.wait_ge(qk_lo, 2 * m + 2)
                bank_free(pe, n, "E")
                for kind, st in ((0, kc), (1, qc)):
                    for a in range(2):
                        last = mm3(bank("E")[:, 256 * kind:256 * kind + 256], (st[:, 0, a, :], st[:, 1, a, :]),
                                   (qkh[:, 2 * kind + a, :], qkl[:, 2 * kind + a, :]), a == 0, a == 1)
                last.then_inc(cls_ps, 1)

            def score(n, r, m, gq):
                if gq == 0:
                    pe.wait_ge(stacked, 192 * (m + 1))
                wait(pe, attn, 8 * m + gq - 1)
                for a in range(2):
                    for kt in range(2):
                        last = nc.tensor.matmul(ps_s[gq % 2][:, a, kt, :], ks[r % 2][:, a, gq, kt * 128:kt * 128 + 128],
                                                qs[r % 2][:, gq, :], start=True, stop=True)
                last.then_inc(scores, 1)

            def weighted(n, r, m, t):
                if t == 0:
                    pe.wait_ge(cls_ready, m + 1)
                    pe.wait_ge(uv_act, 2 * m + 2)
                pe.wait_ge(attn, 8 * m + 2 * t + 2)
                wait(pe, av_out, 4 * m + t - 1)
                if t == 0:
                    wait(pe, crow_done, m)
                if t == 1:
                    wait(pe, stt_done, m - 1)
                o = ps_av[t % 2]
                nc.tensor.matmul(o[:, 0:256], vc[:, t, :], cls_s[:, :], start=True, stop=False, skip_group_check=True)
                for kt in range(2):
                    for j in range(4):
                        l2, a = j // 2, j % 2
                        h = a * 8 + 2 * t + l2
                        last = nc.tensor.matmul(o[32 * j:32 * j + 16, 0:256], uv[r % 2][:, kt, 256 + h * 16:256 + h * 16 + 16],
                                                at[(2 * t + l2) % 4][:, a, kt, :], start=False, stop=kt == 1,
                                                skip_group_check=True)
                if t == 0:
                    for kt in range(2):
                        last = nc.tensor.transpose(o[:, 256 + 16 * kt:272 + 16 * kt],
                                                   clc[0:16, 256 + 128 * kt:384 + 128 * kt], ident[0:16, 0:16])
                if t == 2:
                    pe.wait_ge(va_sum, m + 1)
                    last = nc.tensor.matmul(o[0:1, 256:512], ones[:, 0:1], va2[:, :], start=True, stop=True)
                return last

            def body(n, r):
                a, b, c, d, e = n + 2, n + 1, n, n - 1, n - 2
                if has(c):
                    cls_scores(n, c)
                    score(n, r, c, 0)
                    score(n, r, c, 1)
                if has(e):
                    pe.wait_ge(xft_done, e + 1)
                    pe.wait_ge(stt_done, e + 1)
                    bank_free(pe, n, "G0")
                    o = bank("G0")[:, 0:256]
                    for kt in range(2):
                        mm3(o, (r1ws[:, 0, kt, :], r1ws[:, 1, kt, :]), (xft[:, 0, kt, :], xft[:, 1, kt, :]), kt == 0, False)
                    nc.tensor.matmul(o, r1st[:, :], stt[:, :], start=False, stop=True).then_inc(r1_ps, 1)
                if has(d):
                    pe.wait_ge(av_out, 4 * d + 4)
                    for hf in range(2):
                        u = ("D0", "D1")[hf]
                        bank_free(pe, n, u)
                        for t in range(4):
                            last = nc.tensor.transpose(bank(u)[:, 128 * t:128 * t + 128], avs[:, t, hf * 128:hf * 128 + 128], ident)
                        last.then_inc(avt_ps, 1)
                if has(b):
                    transposes(n, "B0", xn, xn_done, b + 1, xt_ps)
                if has(c):
                    score(n, r, c, 2)
                if has(a):
                    conv(n, a, 0, "A0")
                if has(c):
                    weighted(n, r, c, 0).then_inc(av_ps, 1)
                if has(b):
                    proj_qk(n, b, 0, "B1")
                if has(c):
                    score(n, r, c, 3)
                if has(b):
                    proj_qk(n, b, 1, "B2")
                if has(d):
                    transposes(n, "D2", z, z_done, d + 1, zt_ps)
                if has(c):
                    score(n, r, c, 4)
                    weighted(n, r, c, 1).then_inc(av_ps, 1)
                if has(b):
                    proj_uv(n, b, 0, "B3")
                if has(c):
                    score(n, r, c, 5)
                if has(d):
                    pe.wait_ge(zt_done, d + 1)
                    bank_free(pe, n, "D3")
                    for hf in range(2):
                        for kt in range(2):
                            last = mm3(bank("D3")[:, 256 * hf:256 * hf + 256],
                                       (zt[:, 0, kt, hf * 128:hf * 128 + 128], zt[:, 1, kt, hf * 128:hf * 128 + 128]),
                                       (w2s[:, 0, kt, :], w2s[:, 1, kt, :]), kt == 0, kt == 1)
                    last.then_inc(w2_ps, 1)
                if has(a):
                    conv(n, a, 1, "A1")
                if has(b):
                    proj_uv(n, b, 1, "B4")
                if has(c):
                    score(n, r, c, 6)
                    weighted(n, r, c, 2).then_inc(av_ps, 1)
                if has(d):
                    transposes(n, "D4", xf, xf_done, d + 1, xft_ps)
                if has(c):
                    score(n, r, c, 7)
                last = None
                if has(c):
                    last = weighted(n, r, c, 3)
                    if not has(d):
                        last.then_inc(av_ps, 1)
                if has(d):
                    pe.wait_ge(st_done, d + 1)
                    if not has(c):
                        pe.wait_ge(av_out, 4 * d + 4)
                    for hf in range(2):
                        last = nc.tensor.transpose(ps_av[1][0:NST, 256 + 128 * hf:384 + 128 * hf], stats8[:, hf, :], ident)
                    last.then_inc(av_ps, 1)

            steps(pe, body)

        @block.scalar
        def _(act):
            def body(n, r):
                a, b, c, d, e, gm = n + 2, n + 1, n, n - 1, n - 2, n + 3
                if has(c):
                    act.wait_ge(cls_ps, c + 1)
                    wait(act, va_done, c)
                    nc.scalar.activation(clc[:, :], bank("E")[0:96, :], ACT.Silu).then_inc(cls_act, 1)

                def silu_scores(gq):
                    act.wait_ge(scores, 8 * c + gq + 1)
                    if gq < 4:
                        wait(act, av_ps, av_count(c - 1, 3 if gq >= 2 else 2))
                    else:
                        act.wait_ge(av_ps, av_count(c, (gq - 4) // 2))
                    nc.scalar.activation(at[gq % 4][:, :, :, :].rearrange("p a k q -> p (a k q)"),
                                         ps_s[gq % 2][:, :, :, :].rearrange("p a k q -> p (a k q)"), ACT.Silu).then_inc(attn, 1)

                def abs_edges(hf):
                    act.wait_ge(conv_done, 2 * a + hf + 1)
                    if hf == 0:
                        wait(act, h0_done, a)
                    bk = bank(("A0", "A1")[hf])
                    nc.scalar.activation(absx[0:64, hf, :], bk[0:64, 0:256], ACT.Abs)
                    nc.scalar.activation(absx[64:128, hf, :], bk[0:64, 256:512], ACT.Abs)
                    nc.scalar.activation(absy[0:64, hf, :], bk[64:128, 0:256], ACT.Abs)
                    nc.scalar.activation(absy[64:128, hf, :], bk[64:128, 256:512], ACT.Abs).then_inc(abs_done, 1)

                def silu_qk(kind):
                    act.wait_ge(qk_ps, 2 * b + kind + 1)
                    wait(act, qk_hi, 2 * b + kind - 1)
                    wait(act, qk_lo, 2 * b + kind - 1)
                    bk = bank(("B1", "B2")[kind])
                    nc.scalar.activation(qk[:, 2 * kind, :], bk[:, 0:256], ACT.Silu, bias=b1qk_sb[:, 2 * kind:2 * kind + 1])
                    nc.scalar.activation(qk[:, 2 * kind + 1, :], bk[:, 256:512], ACT.Silu,
                                         bias=b1qk_sb[:, 2 * kind + 1:2 * kind + 2]).then_inc(qk_act, 1)

                def silu_uv(hf):
                    act.wait_ge(uv_sum, 2 * b + hf + 1)
                    wait(act, y_done, 2 * b - 2)
                    wait(act, av_ps, av_count(b - 2, 3))
                    wait(act, va_done, b - 1)
                    nc.scalar.activation(uv[(r + 1) % 2][:, hf, :], uvp[:, hf, :], ACT.Silu).then_inc(uv_act, 1)

                if has(c):
                    silu_scores(0)
                    silu_scores(1)
                if has(e):
                    act.wait_ge(r1_ps, e + 1)
                    wait(act, pre_out, 16 * e)
                    nc.scalar.activation(pre[:, :], bank("G0")[:, 0:256], ACT.Copy).then_inc(pre_done, 1)
                if has(gm):
                    act.wait_ge(x_loaded, 32 * (gm + 1))
                    wait(act, gray_split, gm)
                    nc.scalar.activation(g[:, :, :], xb[:, :, 0, :], ACT.Copy,
                                         scale=float(np.float32(GRAY[0]) / 2)).then_inc(gray_a, 1)
                if has(c):
                    silu_scores(2)
                if has(a):
                    abs_edges(0)
                if has(b):
                    silu_qk(0)
                if has(c):
                    silu_scores(3)
                if has(b):
                    silu_qk(1)
                if has(c):
                    silu_scores(4)
                if has(b):
                    silu_uv(0)
                if has(c):
                    silu_scores(5)
                if has(a):
                    abs_edges(1)
                if has(b):
                    silu_uv(1)
                if has(c):
                    silu_scores(6)
                if has(d):
                    act.wait_ge(xf_done, d + 1)
                    wait(act, st_done, d)
                    nc.scalar.activation(axf[:, :, :], xf[:, :, :], ACT.Abs).then_inc(axf_done, 1)
                if has(c):
                    silu_scores(7)

            steps(act, body)

        @block.vector
        def _(dve):
            def norm_stats(src, k, done_bn, done_stat, done_ve, eps, m):
                nc.vector.bn_stats(bn[k][:, 0, :], src[:, 0, :])
                nc.vector.bn_stats(bn[k][:, 1, :], src[:, 1, :]).then_inc(done_bn, 1)
                dve.wait_ge(done_bn, m + 1)
                nc.vector.memset(spare[:, :], 0.0)
                nc.vector.bn_aggr(mv[k][:, 0, :], bn[k][:, 0, :])
                nc.vector.bn_aggr(mv[k][:, 1, :], bn[k][:, 1, :]).then_inc(done_stat, 1)
                dve.wait_ge(done_stat, m + 1)
                if done_ve is not None:
                    nc.vector.tensor_scalar(ve[k][:, :], mv[k][:, :, 1], eps, None, ALU.add).then_inc(done_ve, 1)

            def normalise(dst, src, k, done):
                nc.vector.tensor_scalar(dst[:, 0, :], src[:, 0, :], mv[k][:, 0, 0:1], rs[k][:, 0:1], ALU.subtract, ALU.mult)
                nc.vector.tensor_scalar(dst[:, 1, :], src[:, 1, :], mv[k][:, 1, 0:1], rs[k][:, 1:2], ALU.subtract,
                                        ALU.mult).then_inc(done, 1)

            def split_t(dst, src, m, hi, done):
                nc.vector.tensor_copy(dst[:, 0, :, :].rearrange("p k t -> p (k t)"), src).then_inc(hi, 1)
                dve.wait_ge(hi, m + 1)
                nc.vector.tensor_tensor(dst[:, 1, :, :].rearrange("p k t -> p (k t)"), src,
                                        dst[:, 0, :, :].rearrange("p k t -> p (k t)").bitcast(f32), ALU.subtract).then_inc(done, 1)

            def body(n, r):
                a, b, c, d, e, gm = n + 2, n + 1, n, n - 1, n - 2, n + 3
                if has(c):
                    dve.wait_ge(cls_act, c + 1)
                    wait(dve, av_ps, 4 * c)
                    nc.vector.tensor_copy(cls_s[:, :], clc[:, 0:256]).then_inc(cls_hi, 1)
                    dve.wait_ge(cls_hi, c + 1)
                    nc.vector.tensor_tensor(cls_s[64:96, :], clc[64:96, 0:256], cls_s[64:96, :].bitcast(f32),
                                            ALU.subtract).then_inc(cls_ready, 1)
                if has(d):
                    for hf in range(2):
                        dve.wait_ge(avt_ps, 2 * d + hf + 1)
                        nc.vector.tensor_tensor(
                            y[:, hf, :].rearrange("p (a tl d) -> p tl a d", a=2, tl=8),
                            bank(("D0", "D1")[hf])[:, :].rearrange("p (tl a x) -> p tl a x", tl=8, a=2)[:, :, :, 0:16],
                            uv[(r - 1) % 2][:, hf, 0:256].rearrange("p (a tl d) -> p tl a d", a=2, tl=8),
                            ALU.mult).then_inc(y_done, 1)
                    dve.wait_ge(y_done, 2 * d + 2)
                    norm_stats(y, "z", bnz, stat_z, ve_z, LN_EPS * S * S, d)
                if has(b):
                    dve.wait_ge(xt_ps, b + 1)
                    wait(dve, uv_ps, 2 * b)
                    split_t(xt, bank("B0")[:, :], b, xt_hi, xt_done)
                if has(d):
                    dve.wait_ge(rs_z, d + 1)
                    wait(dve, zt_ps, d)
                    normalise(z, y, "z", z_done)
                if has(gm):
                    dve.wait_ge(gray_a, gm + 1)
                    nc.vector.scalar_tensor_tensor(g[:, :, :], xb[:, :, 1, :], float(np.float32(GRAY[1]) / 2), g[:, :, :],
                                                   ALU.mult, ALU.add).then_inc(gray_sum, 1)
                    dve.wait_ge(gray_sum, 2 * gm + 1)
                    nc.vector.scalar_tensor_tensor(g[:, :, :], xb[:, :, 2, :], float(np.float32(GRAY[2]) / 2), g[:, :, :],
                                                   ALU.mult, ALU.add).then_inc(gray_sum, 1)
                    dve.wait_ge(gray_sum, 2 * gm + 2)
                    wait(dve, halo_loaded, 64 * gm)
                    nc.vector.tensor_copy(ghl[:, 0:2, :], g[:, :, :]).then_inc(gray_hi, 1)
                    dve.wait_ge(gray_hi, gm + 1)
                    nc.vector.tensor_tensor(ghl[:, 2:4, :], g[:, :, :], ghl[:, 0:2, :].bitcast(f32),
                                            ALU.subtract).then_inc(gray_split, 1)

                def av_read(t):
                    dve.wait_ge(av_ps, av_count(c, t))
                    if t == 0:
                        wait(dve, avt_ps, 2 * c)
                        wait(dve, va_sum, c)
                        nc.vector.tensor_tensor(
                            va[:, :, :].rearrange("p k (h d) -> p k h d", d=DH),
                            uv[r % 2][:, :, 256:512].rearrange("p k (h d) -> p k h d", d=DH),
                            ps_av[0][:, 256:288].rearrange("p (k h) -> p k h", k=2).unsqueeze(3).to_broadcast([P, 2, H, DH]),
                            ALU.mult).then_inc(va_done, 1)
                    nc.vector.tensor_copy(avs[:, t, :], ps_av[t % 2][:, 0:256]).then_inc(av_out, 1)

                def qk_split(kind):
                    dve.wait_ge(qk_act, 2 * b + kind + 1)
                    wait(dve, stacked, 192 * b)
                    wait(dve, cls_ps, b)
                    nc.vector.tensor_copy(qkh[:, 2 * kind:2 * kind + 2, :], qk[:, 2 * kind:2 * kind + 2, :]).then_inc(qk_hi, 1)

                if has(c):
                    av_read(0)
                if has(b):
                    qk_split(0)
                    qk_split(1)
                if has(d):
                    dve.wait_ge(zt_ps, d + 1)
                    wait(dve, w2_ps, d)
                    split_t(zt, bank("D2")[:, :], d, zt_hi, zt_done)
                if has(b):
                    dve.wait_ge(uv_ps, 2 * b + 1)
                    wait(dve, uv_act, 2 * b)
                    nc.vector.tensor_tensor(uvp[:, 0, :], bank("B3")[:, :], b1uv_sb[:, :], ALU.add).then_inc(uv_sum, 1)
                if has(c):
                    av_read(1)
                if has(d):
                    dve.wait_ge(w2_ps, d + 1)
                    dve.wait_ge(h0b_done, d + 1)
                    wait(dve, h2_out, 32 * d)
                    nc.vector.tensor_tensor(h2[:, :, :], bank("D3")[:, :].rearrange("p (a q) -> p a q", a=2), h0b[(r - 1) % 4][:, :, :],
                                            ALU.add).then_inc(h2_done, 1)
                    dve.wait_ge(h2_done, d + 1)
                    norm_stats(h2, "h", bnh, stat_h, ve_h, LN_EPS, d)
                if has(b):
                    dve.wait_ge(uv_ps, 2 * b + 2)
                    nc.vector.tensor_tensor(uvp[:, 1, :], bank("B4")[:, :], b1uv_sb[:, :], ALU.add).then_inc(uv_sum, 1)
                if has(d):
                    dve.wait_ge(rs_h, d + 1)
                    wait(dve, xft_ps, d)
                    wait(dve, xf_out, 32 * d)
                    normalise(xf, h2, "h", xf_done)
                    dve.wait_ge(xf_done, d + 1)
                    norm_stats(xf, "x", bnx, stat_x, None, 0.0, d)
                    wait(dve, av_ps, st_count(d - 1))
                    nc.vector.tensor_copy(stats8[:, :, 0:1], mv["x"][:, :, 0:1])
                    nc.vector.tensor_tensor(sq[:, :, 1:2], mv["x"][:, :, 0:1], mv["x"][:, :, 0:1], ALU.mult)
                    nc.vector.tensor_scalar(sq[:, :, 0:1], mv["x"][:, :, 1:2], float(D) / (D - 1), None, ALU.mult).then_inc(mean_sq, 1)
                    nc.vector.tensor_reduce(stats8[:, :, 2:3], xf[:, :, :], AX.X, ALU.min)
                    nc.vector.tensor_reduce(stats8[:, :, 3:4], xf[:, :, :], AX.X, ALU.max)
                    dve.wait_ge(mean_sq, d + 1)
                    nc.vector.tensor_tensor(sq[:, :, 1:2], sq[:, :, 1:2], mv["x"][:, :, 1:2], ALU.add).then_inc(var_sq, 1)
                if has(a):
                    dve.wait_ge(abs_done, 2 * a + 2)
                    wait(dve, h0b_done, a)
                    nc.vector.tensor_tensor(h0[:, :, :], absx[:, :, :], absy[:, :, :], ALU.add).then_inc(h0_done, 1)
                    dve.wait_ge(h0_done, a + 1)
                    norm_stats(h0, "a", bna, stat_a, ve_a, LN_EPS, a)
                if has(c):
                    av_read(2)
                    wait(dve, crow_out, 16 * c)
                    nc.vector.tensor_copy(crow[0:1, :], ps_av[0][0:1, 256:512]).then_inc(crow_done, 1)
                if has(d):
                    dve.wait_ge(axf_done, d + 1)
                    for hf in range(2):
                        nc.vector.tensor_scalar(axf[:, hf, :], axf[:, hf, :], 1e-6, None, ALU.is_lt, ALU.add,
                                                accum_out=stats8[:, hf, 5:6])
                    dve.wait_ge(sq_root, d + 1)
                    nc.vector.tensor_copy(stats8[:, :, 1:2], sq[:, :, 0:1])
                    nc.vector.tensor_scalar(stats8[:, :, 4:5], sq[:, :, 1:2], float(D) ** 0.5, None, ALU.mult).then_inc(st_done, 1)
                if has(a):
                    dve.wait_ge(rs_a, a + 1)
                    wait(dve, xt_ps, a)
                    normalise(xn, h0, "a", xn_done)
                if has(d):
                    dve.wait_ge(xft_ps, d + 1)
                    wait(dve, r1_ps, d)
                    split_t(xft, bank("D4")[:, :], d, xft_hi, xft_done)
                if has(c):
                    av_read(3)
                if has(d):
                    dve.wait_ge(av_ps, st_count(d))
                    nc.vector.tensor_copy(stt[0:NST, :], ps_av[1][0:NST, 256:512]).then_inc(stt_done, 1)

            steps(dve, body)

        @block.gpsimd
        def _(pool):
            def rsqrt(k, ready, done, m):
                pool.wait_ge(ready, m + 1)
                nc.gpsimd.tensor_tensor(rs[k][:, :], ve[k][:, :], n05[:, 0:2], ALU.pow).then_inc(done, 1)

            def body(n, r):
                a, b, c, d = n + 2, n + 1, n, n - 1
                if has(d):
                    wait(pool, z_done, d)
                    rsqrt("z", ve_z, rs_z, d)
                if has(c):
                    pool.wait_ge(va_done, c + 1)
                    wait(pool, av_ps, av_count(c - 1, 2))
                    nc.gpsimd.tensor_tensor(va2[:, :], va[:, 0, :], va[:, 1, :], ALU.add).then_inc(va_sum, 1)
                if has(b):
                    for kind in range(2):
                        pool.wait_ge(qk_hi, 2 * b + kind + 1)
                        nc.gpsimd.tensor_tensor(qkl[:, 2 * kind:2 * kind + 2, :], qk[:, 2 * kind:2 * kind + 2, :],
                                                qkh[:, 2 * kind:2 * kind + 2, :].bitcast(f32), ALU.subtract).then_inc(qk_lo, 1)
                if has(d):
                    wait(pool, xf_done, d)
                    rsqrt("h", ve_h, rs_h, d)
                    pool.wait_ge(var_sq, d + 1)
                    nc.gpsimd.tensor_tensor(sq[:, :, :], sq[:, :, :], n05[:, 2:6].rearrange("p (a b) -> p a b", a=2),
                                            ALU.pow).then_inc(sq_root, 1)
                if has(a):
                    wait(pool, xn_done, a)
                    rsqrt("a", ve_a, rs_a, a)
                    pool.wait_ge(h0_done, a + 1)
                    wait(pool, h2_done, a - 3)
                    nc.gpsimd.tensor_tensor(h0b[(r + 2) % 4][:, :, :], h0[:, :, :],
                                            bias2[:, :].unsqueeze(1).to_broadcast([P, 2, D]), ALU.add).then_inc(h0b_done, 1)

            steps(pool, body)

        @block.sync
        def _(sp):
            def load_x(m):
                wait(sp, gray_split, m)
                for hf in range(2):
                    sp.dma_start(xb[:, hf, :, :], x[bass.ds(m, 1), :, hf * 128:hf * 128 + 128, :].rearrange(
                        "o c p w -> p (o c) w")).then_inc(x_loaded, 16)

            def body(n, r):
                a, b, c, d, e, gm = n + 2, n + 1, n, n - 1, n - 2, n + 3
                if isinstance(n, int) and n == -3:
                    load_x(0)
                nx = n + 4
                if has(nx) and (not isinstance(nx, int) or nx > 0):
                    load_x(nx)
                if has(b):
                    for kind, (dst, slots) in enumerate(((qs, "hhl"), (ks, "hlh"))):
                        sp.wait_ge(qk_hi, 2 * b + kind + 1)
                        sp.wait_ge(qk_lo, 2 * b + kind + 1)
                        for a2 in range(2):
                            for s, part in enumerate(slots):
                                row = 48 * a2 + 16 * s
                                o = dst[(r + 1) % 2]
                                o = o[row:row + 16, :, :] if kind == 0 else o[row:row + 16, a2, :, :]
                                sp.dma_start(o.bitcast(f32), (qkh if part == "h" else qkl)[:, 2 * kind + a2, :].bitcast(f32)).then_inc(stacked, 16)
                if has(gm):
                    wait(sp, conv_done, 2 * gm)
                    sp.wait_ge(gray_split, gm + 1)
                    for out_ap, in_ap in (
                        (halo[1:66, 0:8:2, 1:257], ghl[0:65, :, :]),
                        (halo[0:65, 1:8:2, 1:257], ghl[63:128, :, :]),
                        (halo[65:66, 1:8:4, 1:257], ghl[0:1, 1:4:2, :]),
                        (halo[0:1, 2:8:4, 1:257], ghl[127:128, 0:4:2, :]),
                    ):
                        sp.dma_start(out_ap.bitcast(f32), in_ap.bitcast(f32)).then_inc(halo_loaded, 16)
                if has(d):
                    sp.wait_ge(h2_done, d + 1)
                    for hf in range(2):
                        sp.dma_start(out[bass.ds(d * S + 1 + 128 * hf, 128), :], h2[:, hf, :]).then_inc(h2_out, 16)
                    sp.wait_ge(xf_done, d + 1)
                    for hf in range(2):
                        sp.dma_start(xf_dram[bass.ds(2 * d + hf, 1), :, :].rearrange("o p w -> (o p) w"), xf[:, hf, :]).then_inc(xf_out, 16)
                if has(e):
                    sp.wait_ge(pre_done, e + 1)
                    sp.dma_start(pre_dram[bass.ds(e, 1), :, :].rearrange("o p t -> (o p) t"), pre[:, :]).then_inc(pre_out, 16)
                if has(c):
                    sp.wait_ge(crow_done, c + 1)
                    sp.dma_start(cls_av[bass.ds(c, 1), :], crow[0:1, :]).then_inc(crow_out, 16)

            steps(sp, body)
            sp.wait_ge(h2_out, 32 * NB)
            sp.wait_ge(xf_out, 32 * NB)
            sp.wait_ge(crow_out, 16 * NB)
            sp.wait_ge(pre_out, 16 * NB)
        images.close()

        def chain(eng, s):
            tally = [0]

            def link(ins, value=None):
                tally[0] += 1
                assert value is None or value == tally[0], (value, tally[0])
                ins.then_inc(s, 1)
                eng.wait_ge(s, tally[0])
            link.tally = tally
            return link

        classes = ExitStack()
        block = classes.enter_context(nc.Block())
        cls_load, ct_dve, ct_pe, ct_pool, ct_act, cls_var, cls_out = (sem(n) for n in ("cls_load", "ct_dve", "ct_pe", "ct_pool", "ct_act", "cls_var", "cls_out"))
        B = slice(0, NB)
        clsr = h0[:, 0, :]
        Z_, ZT_, VH_, XF_, SQ_, ST_, XT_ = 6, 8, 11, 12, 16, 19, 21

        @block.sync
        def _(sp):
            sp.dma_start(y[B, 0, :], cls_av).then_inc(cls_load, 16)
            sp.dma_start(h0[:, 1, :], cls_rows).then_inc(cls_load, 16)
            sp.wait_ge(ct_dve, VH_)
            sp.dma_start(out[0:NTOK, :].rearrange("(b s) w -> b s w", s=S)[:, 0, :], h2[B, 0, :]).then_inc(cls_out, 16)
            sp.wait_ge(cls_out, 16)

        @block.vector
        def _(dve):
            link = chain(dve, ct_dve)
            nc.vector.memset(z[:, 0, :], 0.0)
            nc.vector.memset(xf[:, 0, :], 0.0)
            nc.vector.memset(stats8[:, 0, :], 0.0)
            dve.wait_ge(cls_load, 32)
            nc.vector.tensor_tensor(clsr, h0[:, 1, :], bias2[:, :], ALU.add)
            link(nc.vector.tensor_tensor(y[B, 0, :], y[B, 0, :], ccv[B, :], ALU.add))
            link(nc.vector.tensor_tensor(y[B, 0, :], y[B, 0, :], uvc[B, 0:256], ALU.mult))
            link(nc.vector.bn_stats(bn["z"][B, 0, :], y[B, 0, :]))
            link(nc.vector.bn_aggr(mv["z"][B, 0, :], bn["z"][B, 0, :]))
            link(nc.vector.tensor_scalar(ve["z"][B, 0:1], mv["z"][B, 0, 1:2], LN_EPS * S * S, None, ALU.add), 5)
            dve.wait_ge(ct_pool, 1)
            link(nc.vector.tensor_scalar(z[B, 0, :], y[B, 0, :], mv["z"][B, 0, 0:1], rs["z"][B, 0:1], ALU.subtract, ALU.mult), Z_)
            dve.wait_ge(ct_pe, 1)
            zps = ps_f[0][:, 0:256].rearrange("p (k t) -> p k t", k=2)
            link(nc.vector.tensor_copy(zt[:, 0, :, 0:128], zps))
            link(nc.vector.tensor_tensor(zt[:, 1, :, 0:128], zps, zt[:, 0, :, 0:128].bitcast(f32), ALU.subtract), ZT_)
            dve.wait_ge(ct_pe, 2)
            link(nc.vector.tensor_tensor(h2[B, 0, :], ps_f[1][B, 0:256], clsr[B, :], ALU.add))
            link(nc.vector.bn_stats(bn["h"][B, 0, :], h2[B, 0, :]))
            link(nc.vector.bn_aggr(mv["h"][B, 0, :], bn["h"][B, 0, :]), VH_)
            dve.wait_ge(ct_pool, 2)
            link(nc.vector.tensor_scalar(xf[B, 0, :], h2[B, 0, :], mv["h"][B, 0, 0:1], rs["h"][B, 0:1], ALU.subtract, ALU.mult), XF_)
            nc.vector.tensor_copy(cls_xf[:, :], xf[:, 0, :])
            link(nc.vector.bn_stats(bn["x"][B, 0, :], xf[B, 0, :]))
            link(nc.vector.bn_aggr(mv["x"][B, 0, :], bn["x"][B, 0, :]))
            nc.vector.tensor_copy(stats8[B, 0, 0:1], mv["x"][B, 0, 0:1])
            nc.vector.tensor_reduce(stats8[B, 0, 2:3], xf[B, 0, :], AX.X, ALU.min)
            nc.vector.tensor_reduce(stats8[B, 0, 3:4], xf[B, 0, :], AX.X, ALU.max)
            nc.vector.tensor_scalar(sq[B, 0, 0:1], mv["x"][B, 0, 1:2], float(D) / (D - 1), None, ALU.mult)
            link(nc.vector.tensor_tensor(sq[B, 0, 1:2], mv["x"][B, 0, 0:1], mv["x"][B, 0, 0:1], ALU.mult))
            link(nc.vector.tensor_tensor(sq[B, 0, 1:2], sq[B, 0, 1:2], mv["x"][B, 0, 1:2], ALU.add), SQ_)
            dve.wait_ge(ct_act, 1)
            link(nc.vector.tensor_scalar(axf[B, 0, :], axf[B, 0, :], 1e-6, None, ALU.is_lt, ALU.add, accum_out=stats8[B, 0, 5:6]))
            dve.wait_ge(ct_pool, 3)
            link(nc.vector.tensor_copy(stats8[B, 0, 1:2], sq[B, 0, 0:1]))
            link(nc.vector.tensor_scalar(stats8[B, 0, 4:5], sq[B, 0, 1:2], float(D) ** 0.5, None, ALU.mult), ST_)
            dve.wait_ge(ct_pe, 3)
            link(nc.vector.tensor_copy(xft[:, 0, :, 0:128], zps))
            dve.wait_ge(ct_pe, 4)
            nc.vector.tensor_tensor(xft[:, 1, :, 0:128], zps, xft[:, 0, :, 0:128].bitcast(f32), ALU.subtract)
            link(nc.vector.tensor_copy(stt[0:NST, 0:128], ps_av[0][0:NST, 0:128]), XT_)
            dve.wait_ge(ct_pe, 5)
            link(nc.vector.tensor_copy(pre_cls[:, :], ps_f[1][:, 256:384]))

        @block.gpsimd
        def _(pool):
            pool.wait_ge(ct_dve, 5)
            nc.gpsimd.tensor_tensor(rs["z"][B, 0:1], ve["z"][B, 0:1], n05[B, 0:1], ALU.pow).then_inc(ct_pool, 1)
            pool.wait_ge(ct_dve, VH_)
            nc.gpsimd.tensor_scalar(ve["h"][B, 0:1], mv["h"][B, 0, 1:2], LN_EPS, None, ALU.add).then_inc(cls_var, 1)
            pool.wait_ge(cls_var, 1)
            nc.gpsimd.tensor_tensor(rs["h"][B, 0:1], ve["h"][B, 0:1], n05[B, 0:1], ALU.pow).then_inc(ct_pool, 1)
            pool.wait_ge(ct_dve, SQ_)
            nc.gpsimd.tensor_tensor(sq[B, 0, :], sq[B, 0, :], n05[B, 2:4], ALU.pow).then_inc(ct_pool, 1)

        @block.scalar
        def _(act):
            act.wait_ge(ct_dve, XF_)
            nc.scalar.activation(axf[B, 0, :], xf[B, 0, :], ACT.Abs).then_inc(ct_act, 1)

        @block.tensor
        def _(pe):
            pe.wait_ge(ct_dve, Z_)
            for kt in range(2):
                last = nc.tensor.transpose(ps_f[0][:, 128 * kt:128 * kt + 128], z[:, 0, kt * 128:kt * 128 + 128], ident)
            last.then_inc(ct_pe, 1)
            pe.wait_ge(ct_dve, ZT_)
            for kt in range(2):
                last = mm3(ps_f[1][:, 0:256], (zt[:, 0, kt, 0:128], zt[:, 1, kt, 0:128]), (w2s[:, 0, kt, :], w2s[:, 1, kt, :]), kt == 0, kt == 1)
            last.then_inc(ct_pe, 1)
            pe.wait_ge(ct_dve, XF_)
            for kt in range(2):
                last = nc.tensor.transpose(ps_f[0][:, 128 * kt:128 * kt + 128], xf[:, 0, kt * 128:kt * 128 + 128], ident)
            last.then_inc(ct_pe, 1)
            pe.wait_ge(ct_dve, ST_)
            nc.tensor.transpose(ps_av[0][0:NST, 0:128], stats8[:, 0, :], ident).then_inc(ct_pe, 1)
            pe.wait_ge(ct_dve, XT_)
            for kt in range(2):
                mm3(ps_f[1][:, 256:384], (r1ws[:, 0, kt, :], r1ws[:, 1, kt, :]), (xft[:, 0, kt, 0:128], xft[:, 1, kt, 0:128]), kt == 0, False)
            nc.tensor.matmul(ps_f[1][:, 256:384], r1st[:, :], stt[:, 0:128], start=False, stop=True).then_inc(ct_pe, 1)
        classes.close()
        ph1.close()

        TI = 2 * JN
        NQ = NT + 1
        router = ExitStack()

        def s2(name, shape, dt=f32):
            return router.enter_context(nc.sbuf_tensor(name, shape, dt))

        hid = s2("hid", [P, NQ, P])
        prob = s2("prob", [P, NQ, NE])
        work = s2("work", [P, NQ, NE])
        first = s2("first", [P, NQ, NE])
        second = s2("second", [P, NQ, NE])
        score_t = s2("score_t", [P, NQ, NE])
        top = s2("top", [P, NQ])
        den = s2("den", [P, NQ])
        v1 = s2("v1", [P, NQ])
        v2 = s2("v2", [P, NQ])
        e0m = s2("e0m", [P, NQ])
        e1m = s2("e1m", [P, NQ])
        slot_f = [s2(f"slot_f{k}", [P, NQ]) for k in range(2)]
        slot_i = [s2(f"slot_i{k}", [P, NQ], i32) for k in range(2)]
        rows = s2("rows", [P, NQ, ROW])
        score_e = s2("score_e", [P, CH])
        above = s2("above", [P, CH])
        level = s2("level", [P, CH])
        rank = s2("rank", [P, CH])
        clsk = s2("clsk", [P, P])
        cut = s2("cut", [P, 1], i32)
        cand = s2("cand", [P, 1], i32)
        bitf = s2("bitf", [P, 1])
        biti = s2("biti", [P, 1], i32)
        take = s2("take", [P, 1])
        takei = s2("takei", [P, 1], i32)
        cnt = s2("cnt", [P, 4])
        lim = s2("lim", [P, 4])
        groups = [(k, min(32, NT - 32 * k)) for k in range((NT + 31) // 32)]
        banks = [ps_av[0], ps_av[1], ps_f[0], ps_f[1]]
        iota_m = cst[:, CIE:CIE + NE].unsqueeze(1).to_broadcast([P, NQ, NE])

        def wide(t):
            return t[:, :].unsqueeze(2).to_broadcast([P, NQ, NE])

        def tiles(k, n):
            return ps_s[k][:, :, :, :].rearrange("p a k q -> p (a k q)")[:, 0:n * NE].rearrange("p (t e) -> p t e", e=NE)

        def flat(t):
            return t[:, :, :].rearrange("p t e -> p (t e)")

        block_stack = ExitStack()
        block = block_stack.enter_context(nc.Block())
        pre_load, rows_load, rt_act, rt_pe, rt_dve, scattered = (sem(n) for n in ("pre_load", "rows_load", "rt_act", "rt_pe", "rt_dve", "scattered"))
        BITS = 30
        D_PRE, D_LOG, D_SCO, D_SE, D_SEA = 1, 3, 21, 22, 24
        PER = 5
        D_CNT = D_SEA + PER * BITS + 1
        D_SEL, D_V, D_SLOT = D_CNT + 4, D_CNT + 8, D_CNT + 12
        E_PRE = 4
        P_LOG, P_SE, P_SEC = 1, 2, 3
        P_CNT, P_SEL, P_V = P_SEC + BITS + 1, P_SEC + BITS + 2, P_SEC + BITS + 3

        @block.sync
        def _(sp):
            for c in range(4):
                sp.dma_start(hid[:, c * TI:(c + 1) * TI, :].rearrange("p (m h) t -> p m (h t)", h=2),
                             pre_dram[c * JN:(c + 1) * JN].rearrange("m p t -> p m t")).then_inc(pre_load, 16)
            for c in range(4):
                sp.dma_start(rows[:, c:NT:4, 0:D], xf_dram[c * TI:(c + 1) * TI].rearrange("t p w -> p t w")).then_inc(rows_load, 16)
            sp.wait_ge(rows_load, 64)

        @block.scalar
        def _(act):
            act.wait_ge(rt_dve, D_PRE)
            nc.scalar.activation(hid[:, NT, :], pre_cls[:, :], ACT.Gelu, bias=r1b_c[:, 0:1])
            act.wait_ge(pre_load, 64)
            for c in range(4):
                nc.scalar.activation(hid[:, c * TI:(c + 1) * TI, :], hid[:, c * TI:(c + 1) * TI, :], ACT.Gelu,
                                     bias=r1b_c[:, 0:1]).then_inc(rt_act, 1)
            act.wait_ge(rt_dve, D_LOG)
            nc.scalar.activation(prob[:, :, :], work[:, :, :], ACT.Exp).then_inc(rt_act, 1)

        @block.tensor
        def _(pe):
            for c in range(4):
                pe.wait_ge(rt_act, c + 1)
                for i in range(TI):
                    q = 4 * i + c
                    nc.tensor.matmul(tiles(q // 32, 32)[:, q % 32, :], hid[:, c * TI + i, :], r2w_sb[:, :], start=True, stop=True)
            nc.tensor.matmul(ps_f[0][:, 0:NE], hid[:, NT, :], r2w_sb[:, :], start=True, stop=True).then_inc(rt_pe, 1)
            pe.wait_ge(rt_dve, D_SCO)
            for i in range(TI):
                last = nc.tensor.transpose(banks[i // 4][:, 128 * (i % 4):128 * (i % 4) + 128],
                                           score_t[:, 4 * i:4 * i + 4, :].rearrange("p c e -> p (c e)"), ident)
            last.then_inc(rt_pe, 1)
            pe.wait_ge(rt_dve, D_SE)
            nc.tensor.matmul(ps_s[0][:, 0, 0, 0:JN], clsk[0:32, :], cst[0:32, CTJ:CTJ + JN], start=True, stop=True).then_inc(rt_pe, 1)
            with pe.Fori(0, BITS) as b:
                pe.wait_ge(rt_dve, b * PER + (D_SEA + 2))
                nc.tensor.matmul(ps_s[1][:, 0, 0, 0:1], cst[:, CBE:CBE + 128], cnt[:, 0:1], start=True, stop=True).then_inc(rt_pe, 1)
            pe.wait_ge(rt_dve, D_CNT)
            nc.tensor.matmul(ps_s[1][:, 0, 0, 0:1], cst[:, CBE:CBE + 128], cnt[:, 1:2], start=True, stop=True)
            nc.tensor.matmul(ps_s[1][:, 0, 0, 1:2], cst[:, CLE:CLE + 128], cnt[:, 2:3], start=True, stop=True).then_inc(rt_pe, 1)
            pe.wait_ge(rt_dve, D_SEL)
            nc.tensor.matmul(ps_s[1][:, 0, 0, 2:3], cst[:, CLE:CLE + 128], cnt[:, 3:4], start=True, stop=True).then_inc(rt_pe, 1)
            pe.wait_ge(rt_dve, D_V)
            for i in range(TI):
                at_ = S * (i // 2) + 1 + 128 * (i % 2)
                nc.tensor.transpose(tiles((4 * i) // 32, 32)[:, (4 * i) % 32:(4 * i) % 32 + 4, :].rearrange("p c e -> p (c e)"),
                                    level[:, at_:at_ + 128], ident)
            nc.tensor.matmul(ps_av[0][0:NB, 0:NE], clsk[:, 0:NB], cst[:, CBE:CBE + NE], start=True, stop=True).then_inc(rt_pe, 1)

        @block.vector
        def _(dve):
            link = chain(dve, rt_dve)
            for k in range(2):
                nc.vector.memset(slot_f[k][:, NT:NQ], float(OOB))
            nc.vector.memset(cut[:, :], 0)
            nc.vector.memset(bitf[:, :], float(1 << (BITS - 1)))
            link(nc.vector.memset(biti[:, :], 1 << (BITS - 1)), D_PRE)
            dve.wait_ge(rt_pe, P_LOG)
            for k, n in groups:
                nc.vector.tensor_reduce(top[:, 32 * k:32 * k + n], tiles(k, n), AX.X, ALU.max)
            link(nc.vector.tensor_reduce(top[:, NT:NQ], ps_f[0][:, 0:NE], AX.X, ALU.max))
            for k, n in groups:
                nc.vector.tensor_tensor(work[:, 32 * k:32 * k + n, :], tiles(k, n),
                                        top[:, 32 * k:32 * k + n].unsqueeze(2).to_broadcast([P, n, NE]), ALU.subtract)
            link(nc.vector.tensor_tensor(work[:, NT, :], ps_f[0][:, 0:NE], top[:, NT:NQ].to_broadcast([P, NE]), ALU.subtract), D_LOG)
            dve.wait_ge(rt_act, 5)
            link(nc.vector.tensor_reduce(den[:, :], prob[:, :, :], AX.X, ALU.add))
            link(nc.vector.reciprocal(den[:, :], den[:, :]))
            link(nc.vector.tensor_tensor(prob[:, :, :], prob[:, :, :], wide(den), ALU.mult))
            link(nc.vector.tensor_reduce(v1[:, :], prob[:, :, :], AX.X, ALU.max))
            link(nc.vector.tensor_tensor(work[:, :, :], prob[:, :, :], wide(v1), ALU.is_equal))
            link(nc.vector.tensor_tensor(work[:, :, :], work[:, :, :], iota_m, ALU.mult))
            link(nc.vector.tensor_reduce(e0m[:, :], work[:, :, :], AX.X, ALU.min))
            link(nc.vector.tensor_tensor(first[:, :, :], iota_m, wide(e0m), ALU.is_equal))
            link(nc.vector.scalar_tensor_tensor(flat(score_t), flat(first), -2.0, flat(prob), ALU.mult, ALU.add))
            link(nc.vector.tensor_reduce(v2[:, :], score_t[:, :, :], AX.X, ALU.max))
            link(nc.vector.tensor_tensor(work[:, :, :], score_t[:, :, :], wide(v2), ALU.is_equal))
            link(nc.vector.tensor_tensor(work[:, :, :], work[:, :, :], iota_m, ALU.mult))
            link(nc.vector.tensor_reduce(e1m[:, :], work[:, :, :], AX.X, ALU.min))
            link(nc.vector.tensor_tensor(second[:, :, :], iota_m, wide(e1m), ALU.is_equal))
            link(nc.vector.tensor_tensor(work[:, :, :], first[:, :, :], second[:, :, :], ALU.add))
            nc.vector.tensor_tensor(den[:, :], v1[:, :], v2[:, :], ALU.add)
            link(nc.vector.tensor_tensor(prob[:, :, :], prob[:, :, :], work[:, :, :], ALU.mult))
            nc.vector.reciprocal(top[:, :], den[:, :])
            link(nc.vector.scalar_tensor_tensor(flat(score_t), flat(work), -1.0, flat(prob), ALU.add, ALU.add))
            nc.vector.tensor_tensor(rows[:, :, D], v1[:, :], top[:, :], ALU.mult)
            nc.vector.tensor_tensor(rows[:, :, D + 1], v2[:, :], top[:, :], ALU.mult)
            nc.vector.tensor_scalar(rows[:, :, D + 2], e0m[:, :], 64.0, None, ALU.add)
            nc.vector.tensor_copy(rows[:, :, D + 3].bitcast(i32), cst[:, CTI:CTI + NQ])
            link(nc.vector.tensor_copy(rows[:, NT, 0:D], cls_xf[:, :]), D_SCO)
            link(nc.vector.tensor_tensor(clsk[0:32, :].rearrange("p (c e) -> p c e", c=4),
                                         score_t[0:32, NT, :].unsqueeze(1).to_broadcast([32, 4, NE]),
                                         cst[0:32, CTK:CTK + 4].unsqueeze(2).to_broadcast([32, 4, NE]), ALU.mult), D_SE)
            dve.wait_ge(rt_pe, P_SE)
            se = score_e[:, :].rearrange("p (j s) -> p j s", s=S)
            for b in range((TI + 3) // 4):
                last = nc.vector.tensor_copy(se[:, 2 * b:2 * b + 2, 1:S], banks[b][:, :].rearrange("p (j s) -> p j s", j=2))
            link(last)
            dve.wait_ge(rt_pe, P_SEC)
            link(nc.vector.tensor_copy(se[:, :, 0], ps_s[0][:, 0, 0, 0:JN]), D_SEA)
            with dve.Fori(0, BITS) as b:
                n = b * PER + D_SEA

                def step(ins, k):
                    ins.then_inc(rt_dve, 1)
                    dve.wait_ge(rt_dve, n + k)

                step(nc.vector.tensor_tensor(cand[:, :], cut[:, :], biti[:, :], ALU.bitwise_or), 1)
                step(nc.vector.tensor_scalar(above[:, :], score_e[:, :], cand[:, 0:1].bitcast(f32), None, ALU.is_ge, ALU.add,
                                             accum_out=cnt[:, 0:1]), 2)
                dve.wait_ge(rt_pe, b + (P_SEC + 1))
                step(nc.vector.tensor_scalar(takei[:, :], ps_s[1][:, 0, 0, 0:1], float(CAP), bitf[:, 0:1], ALU.is_ge, ALU.mult), 3)
                nc.vector.tensor_scalar(biti[:, :], bitf[:, :], 0.5, None, ALU.mult)
                step(nc.vector.tensor_tensor(cut[:, :], cut[:, :], takei[:, :], ALU.bitwise_or), 4)
                step(nc.vector.tensor_scalar(bitf[:, :], bitf[:, :], 0.5, None, ALU.mult), 5)
            link.tally[0] += PER * BITS
            nc.vector.tensor_scalar(above[:, :], score_e[:, :], cut[:, 0:1].bitcast(f32), None, ALU.is_gt, ALU.add, accum_out=cnt[:, 1:2])
            link(nc.vector.tensor_scalar(level[:, :], score_e[:, :], cut[:, 0:1].bitcast(f32), None, ALU.is_equal, ALU.add,
                                         accum_out=cnt[:, 2:3]))
            dve.wait_ge(rt_pe, P_CNT)
            nc.vector.tensor_scalar(lim[:, 0:1], ps_s[1][:, 0, 0, 0:1], -1.0, float(CAP), ALU.mult, ALU.add)
            link(nc.vector.tensor_copy(lim[:, 1:2], ps_s[1][:, 0, 0, 1:2]))
            link(nc.vector.tensor_tensor_scan(rank[:, :], level[:, :], level[:, :], lim[:, 1:2], ALU.add, ALU.bypass))
            link(nc.vector.scalar_tensor_tensor(level[:, :], rank[:, :], lim[:, 0:1], level[:, :], ALU.is_le, ALU.mult))
            link(nc.vector.scalar_tensor_tensor(above[:, :], above[:, :], 0.0, level[:, :], ALU.add, ALU.add, accum_out=cnt[:, 3:4]), D_SEL)
            dve.wait_ge(rt_pe, P_SEL)
            link(nc.vector.tensor_copy(lim[:, 2:3], ps_s[1][:, 0, 0, 2:3]))
            link(nc.vector.tensor_tensor_scan(rank[:, :], above[:, :], above[:, :], lim[:, 2:3], ALU.add, ALU.bypass))
            link(nc.vector.scalar_tensor_tensor(level[:, :], rank[:, :], cst[:, CSB:CSB + 1], above[:, :], ALU.add, ALU.mult))
            link(nc.vector.tensor_tensor(clsk[:, 0:NB].rearrange("p (c j) -> p c j", c=4),
                                         level[:, :].rearrange("p (j s) -> p j s", s=S)[:, :, 0].unsqueeze(1).to_broadcast([P, 4, JN]),
                                         cst[:, CTM:CTM + NB].rearrange("p (c j) -> p c j", c=4), ALU.mult), D_V)
            dve.wait_ge(rt_pe, P_V)
            for onehot, wk in ((first, work), (second, prob)):
                for g_, n in groups:
                    nc.vector.tensor_tensor(wk[:, 32 * g_:32 * g_ + n, :], tiles(g_, n), onehot[:, 32 * g_:32 * g_ + n, :], ALU.mult)
                last = nc.vector.tensor_tensor(wk[0:NB, NT, :], ps_av[0][0:NB, 0:NE], onehot[0:NB, NT, :], ALU.mult)
            link(last)
            for k, wk in enumerate((work, prob)):
                nc.vector.tensor_reduce(slot_f[k][:, 0:NT], wk[:, 0:NT, :], AX.X, ALU.add)
                last = nc.vector.tensor_reduce(v1[0:NB, k:k + 1], wk[0:NB, NT, :], AX.X, ALU.add)
            link(last)
            for k in range(2):
                nc.vector.tensor_scalar(slot_f[k][:, 0:NT], slot_f[k][:, 0:NT], float(OOB), None, ALU.add)
                last = nc.vector.tensor_scalar(slot_f[k][0:NB, NT:NQ], v1[0:NB, k:k + 1], float(OOB), None, ALU.add)
            link(last)
            for k in range(2):
                last = nc.vector.tensor_copy(slot_i[k][:, :], slot_f[k][:, :])
            link(last, D_SLOT)

        @block.gpsimd
        def _(pool):
            pool.wait_ge(rows_load, 64)
            pool.wait_ge(rt_dve, D_SLOT)
            for q in range(NQ):
                for k in range(2):
                    nc.gpsimd.indirect_dma_start(
                        out=routed_rows, out_offset=bass.IndirectOffsetOnAxis(ap=slot_i[k][:, q:q + 1], axis=0),
                        in_=rows[:, q, :], in_offset=None, bounds_check=NE * SLOTS - 1, oob_is_err=False).then_inc(scattered, 16)
            pool.wait_ge(scattered, 32 * NQ)
        block_stack.close()
        router.close()

        CW = CAP + CAP % 2
        slot_tiles = [(s0, min(P, CW - s0)) for s0 in range(0, CW, P)]
        ST = len(slot_tiles)
        WUP, WDN = 2 * 1024, 2 * 1024 + 4 * D
        WAU = WDN + 2 * 2 * AINTER
        WCOL = WAU + D
        experts = ExitStack()

        def s3(name, shape, dt=f32):
            return experts.enter_context(nc.sbuf_tensor(name, shape, dt))

        raw = [s3(f"raw{i}", [P, WCOL]) for i in range(2)]
        whi = [s3(f"whi{i}", [P, WCOL], f32r) for i in range(2)]
        wlo = [s3(f"wlo{i}", [P, WCOL], f32r) for i in range(2)]
        xe = [s3(f"xe{i}", [P, ST, ROW]) for i in range(2)]
        xet = [s3(f"xet{i}", [P, 2, 2, CW], f32r) for i in range(2)]
        hs = [s3(f"hs{i}", [P, 2, 5, CW], f32r) for i in range(2)]
        sg = [s3(f"sg{i}", [P, CW]) for i in range(2)]
        hm = [s3(f"hm{i}", [P, CW]) for i in range(2)]
        ye = [s3(f"ye{i}", [P, ST, D]) for i in range(2)]
        weight = [s3(f"weight{i}", [P, ST]) for i in range(2)]
        is0 = [s3(f"is0{i}", [P, ST]) for i in range(2)]
        wd = [s3(f"wd{i}", [P, ST]) for i in range(2)]
        tok = [s3(f"tok{i}", [P, ST], i32) for i in range(2)]
        spare = s3("spare_pool", [1, 2 * ST])
        enum = s3("enum", [P, 1])
        w_load = [sem("w_load0"), sem("w_load1")]
        xe_load = [sem("xe_load0"), sem("xe_load1")]
        w_hi, w_lo_up, w_lo_dn, xet_ps, xet_hi, xet_done = (sem(n) for n in ("w_hi", "w_lo_up", "w_lo_dn", "xet_ps", "xet_hi", "xet_done"))
        up_ps, gate_act, h_done, h_hi, h_lo, down_ps, ye_done = (sem(n) for n in ("up_ps", "gate_act", "h_done", "h_hi", "h_lo", "down_ps", "ye_done"))
        is_first, w_diff, w_part, w_ready, tok_ready, added = (sem(n) for n in ("is_first", "w_diff", "w_part", "w_ready", "tok_ready", "added"))
        enum_set = sem("enum_set")

        def there(m):
            return not isinstance(m, int) or 0 <= m < NE

        def expert_steps(eng, body):
            for n in range(-1, 4):
                body(n, n % 2)
            with eng.Fori(0, (NE - 6) // 2) as i:
                for k in range(2):
                    body(i * 2 + (4 + k), k)
            for n in range(NE - 2, NE + 1):
                body(n, n % 2)

        def half(m, r):
            return m // 2 if isinstance(m, int) else (m - r) // 2

        block_stack = ExitStack()
        block = block_stack.enter_context(nc.Block())

        def load_count(m, r, per):
            return (m // 2 + 1) * per if isinstance(m, int) else (m + (2 - r)) * (per // 2)

        @block.sync
        def _(sp):
            def load(m, r):
                if there(m):
                    wait(sp, w_hi, 2 * (m - 1))
                    wait(sp, w_lo_up, m - 1)
                    wait(sp, w_lo_dn, m - 1)
                    sp.dma_start(raw[r][:, 0:WDN], wexp[bass.ds(m, 1)].rearrange("o p w -> (o p) w")).then_inc(w_load[r], 16)
                    g_ = half(m, r)
                    sp.dma_start(raw[r][:, WDN:WCOL], wadp[bass.ds(g_, 1)].rearrange("o p w -> (o p) w")).then_inc(w_load[r], 16)
                    wait(sp, xet_ps, m - 1)
                    wait(sp, w_ready, m - 1)
                    wait(sp, tok_ready, m - 1)
                    sp.dma_start(xe[r][:, :, :], routed_rows[bass.ds(m * SLOTS, ST * P), :].rearrange(
                        "(n p) w -> p n w", p=P)).then_inc(xe_load[r], 16)

            def body(n, r):
                if isinstance(n, int) and n == -1:
                    load(0, 0)
                    load(1, 1)
                elif not isinstance(n, int) or n >= 0:
                    load(n + 2, r)

            expert_steps(sp, body)

        @block.tensor
        def _(pe):
            def up(n, r, j):
                if j == 0:
                    pe.wait_ge(w_hi, 2 * n + 2)
                    pe.wait_ge(w_lo_up, n + 1)
                    pe.wait_ge(w_lo_dn, n + 1)
                    pe.wait_ge(xet_done, n + 1)
                b = (5 * r + j) % 2
                wait(pe, h_done, 5 * n + j - 1)
                for part in range(2):
                    for kt in range(2):
                        if j < 4:
                            col = kt * 1024 + part * INTER + j * 128
                        else:
                            col = WDN + kt * 2 * AINTER + part * AINTER
                        last = mm3(ps_s[b][:, part, :, :].rearrange("p k q -> p (k q)")[:, 0:CW],
                                   (whi[r][:, col:col + 128], wlo[r][:, col:col + 128]),
                                   (xet[r][:, 0, kt, :], xet[r][:, 1, kt, :]), kt == 0, kt == 1)
                last.then_inc(up_ps, 1)

            def down(m, r):
                pe.wait_ge(h_lo, 5 * m + 5)
                for st, (s0, w) in enumerate(slot_tiles):
                    wait(pe, ye_done, ST * m + st - 1)
                    for j in range(5):
                        col = WUP + j * D if j < 4 else WAU
                        last = mm3(ps_av[(ST * r + st) % 2][0:w, 0:D], (hs[r][:, 0, j, s0:s0 + w], hs[r][:, 1, j, s0:s0 + w]),
                                   (whi[r][:, col:col + D], wlo[r][:, col:col + D]), j == 0, j == 4)
                    last.then_inc(down_ps, 1)

            def body(n, r):
                if there(n):
                    up(n, r, 0)
                    up(n, r, 1)
                if there(n - 1):
                    down(n - 1, 1 - r)
                if there(n):
                    up(n, r, 2)
                    up(n, r, 3)
                if there(n + 1):
                    pe.wait_ge(xe_load[1 - r], load_count(n + 1, 1 - r, 16))
                    wait(pe, xet_done, n + 1)
                    for kt in range(2):
                        for st, (s0, w) in enumerate(slot_tiles):
                            last = nc.tensor.transpose(ps_f[kt][:, s0:s0 + w], xe[1 - r][0:w, st, kt * 128:kt * 128 + 128], ident[0:w, 0:w])
                    last.then_inc(xet_ps, 1)
                if there(n):
                    up(n, r, 4)

            expert_steps(pe, body)

        @block.scalar
        def _(act):
            def gate(n, r, j):
                act.wait_ge(up_ps, 5 * n + j + 1)
                wait(act, h_done, 5 * n + j - 1)
                b = (5 * r + j) % 2
                nc.scalar.activation(sg[b][:, :], ps_s[b][:, 0, :, :].rearrange("p k q -> p (k q)")[:, 0:CW], ACT.Silu).then_inc(gate_act, 1)

            def split(n, r, lo, hi, first_part):
                if there(n):
                    if first_part:
                        act.wait_ge(w_load[r], load_count(n, r, 32))
                        wait(act, down_ps, ST * (n - 1))
                    nc.scalar.activation(whi[r][:, lo:hi], raw[r][:, lo:hi], ACT.Copy).then_inc(w_hi, 1)

            def body(n, r):
                if there(n):
                    gate(n, r, 0)
                    gate(n, r, 1)
                if there(n - 1):
                    act.wait_ge(w_ready, n)
                    wait(act, added, 16 * ST * (n - 2))
                    for st, (s0, w) in enumerate(slot_tiles):
                        act.wait_ge(down_ps, ST * (n - 1) + st + 1)
                        nc.scalar.activation(ye[1 - r][0:w, st, :], ps_av[(ST * (1 - r) + st) % 2][0:w, 0:D], ACT.Copy,
                                             scale=weight[1 - r][0:w, st:st + 1]).then_inc(ye_done, 1)
                split(n + 1, 1 - r, 0, WUP, True)
                if there(n):
                    gate(n, r, 2)
                split(n + 1, 1 - r, WUP, WCOL, False)
                if there(n):
                    gate(n, r, 3)
                    gate(n, r, 4)

            expert_steps(act, body)

        @block.vector
        def _(dve):
            def hidden(n, r, j):
                b = (5 * r + j) % 2
                dve.wait_ge(gate_act, 5 * n + j + 1)
                wait(dve, down_ps, ST * (n - 1))
                o = ps_s[b][:, 1, :, :].rearrange("p k q -> p (k q)")[:, 0:CW]
                wait(dve, h_lo, 5 * n + j - 1)
                if j < 4:
                    nc.vector.tensor_tensor(hm[b][:, :], o, sg[b][:, :], ALU.mult).then_inc(h_done, 1)
                else:
                    nc.vector.scalar_tensor_tensor(hm[b][:, :], o, 0.05, sg[b][:, :], ALU.mult, ALU.mult).then_inc(h_done, 1)
                dve.wait_ge(h_done, 5 * n + j + 1)
                nc.vector.tensor_copy(hs[r][:, 0, j, :], hm[b][:, :]).then_inc(h_hi, 1)
                dve.wait_ge(h_hi, 5 * n + j + 1)
                nc.vector.tensor_tensor(hs[r][:, 1, j, :], hm[b][:, :], hs[r][:, 0, j, :].bitcast(f32), ALU.subtract).then_inc(h_lo, 1)

            def row_weight(m, r):
                dve.wait_ge(xe_load[r], load_count(m, r, 16))
                if not isinstance(m, int) or m > 0:
                    wait(dve, w_ready, m)
                    nc.vector.tensor_scalar(enum[:, :], enum[:, :], 1.0, None, ALU.add).then_inc(enum_set, 1)
                else:
                    nc.vector.memset(enum[:, :], 0.0).then_inc(enum_set, 1)
                dve.wait_ge(enum_set, m + 1)
                wait(dve, ye_done, ST * (m - 1))
                nc.vector.tensor_scalar(is0[r][:, :], xe[r][:, :, D + 2], enum[:, 0:1], None, ALU.is_equal).then_inc(is_first, 1)
                dve.wait_ge(is_first, m + 1)
                nc.vector.tensor_scalar(wd[r][:, :], is0[r][:, :], -1.0, 1.0, ALU.mult, ALU.add).then_inc(w_diff, 1)
                dve.wait_ge(w_diff, m + 1)
                nc.vector.tensor_tensor(is0[r][:, :], is0[r][:, :], xe[r][:, :, D], ALU.mult)
                nc.vector.tensor_tensor(wd[r][:, :], wd[r][:, :], xe[r][:, :, D + 1], ALU.mult).then_inc(w_part, 1)
                dve.wait_ge(w_part, m + 1)
                nc.vector.tensor_tensor(weight[r][:, :], is0[r][:, :], wd[r][:, :], ALU.add).then_inc(w_ready, 1)

            def body(n, r):
                if there(n):
                    hidden(n, r, 0)
                    hidden(n, r, 1)
                    hidden(n, r, 2)
                if there(n + 1):
                    row_weight(n + 1, 1 - r)
                    dve.wait_ge(w_hi, 2 * n + 4)
                    nc.vector.tensor_tensor(wlo[1 - r][:, WUP:WCOL], raw[1 - r][:, WUP:WCOL], whi[1 - r][:, WUP:WCOL].bitcast(f32),
                                            ALU.subtract).then_inc(w_lo_dn, 1)
                if there(n):
                    hidden(n, r, 3)
                if there(n + 1):
                    dve.wait_ge(xet_ps, n + 2)
                    for kt in range(2):
                        last = nc.vector.tensor_copy(xet[1 - r][:, 0, kt, :], ps_f[kt][:, 0:CW])
                    last.then_inc(xet_hi, 1)
                    dve.wait_ge(xet_hi, n + 2)
                    for kt in range(2):
                        last = nc.vector.tensor_tensor(xet[1 - r][:, 1, kt, :], ps_f[kt][:, 0:CW], xet[1 - r][:, 0, kt, :].bitcast(f32), ALU.subtract)
                    last.then_inc(xet_done, 1)
                    wait(dve, added, 16 * ST * n)
                    nc.vector.tensor_copy(tok[1 - r][:, :], xe[1 - r][:, :, D + 3].bitcast(i32)).then_inc(tok_ready, 1)
                if there(n):
                    hidden(n, r, 4)

            expert_steps(dve, body)

        @block.gpsimd
        def _(pool):
            last_row = pool.to_reg(NTOK + SLOTS - 1)

            def body(n, r):
                if there(n - 1):
                    pool.wait_ge(tok_ready, n)
                    wait(pool, added, 16 * ST * (n - 1))
                    for st, (s0, w) in enumerate(slot_tiles):
                        pool.wait_ge(ye_done, ST * (n - 1) + st + 1)
                        nc.gpsimd.tensor_tensor(spare[:, 2 * st + r:2 * st + r + 1], ident[0:1, 0:1], ident[0:1, 0:1], ALU.add)
                        nc.gpsimd.indirect_dma_start(
                            out=out, out_offset=bass.IndirectOffsetOnAxis(ap=tok[1 - r][0:w, st:st + 1], axis=0),
                            in_=ye[1 - r][0:w, st, :], in_offset=None, bounds_check=last_row, oob_is_err=True,
                            compute_op=ALU.add).then_inc(added, 16)
                if there(n + 1):
                    pool.wait_ge(w_hi, 2 * n + 3)
                    nc.gpsimd.tensor_tensor(wlo[1 - r][:, 0:WUP], raw[1 - r][:, 0:WUP], whi[1 - r][:, 0:WUP].bitcast(f32),
                                            ALU.subtract).then_inc(w_lo_up, 1)

            expert_steps(pool, body)
            pool.wait_ge(added, 16 * ST * NE)
        block_stack.close()
        experts.close()


def layouts(x, cls_tok, scharr, W1, b1, W2, b2, gamma, beta, r1_w, r1_b, r2_w, w_up, w_down, a_up, a_down):
    def by_lane(t):
        return t.reshape(t.shape[:-1] + (2, H // 2, DH)).swapaxes(-1, -2).reshape(t.shape[:-1] + (D,))

    def spread(t):
        return np.broadcast_to(t.reshape(1, -1), (P, t.size))

    def k_tiles(t):
        e, o, i = t.shape
        return t.transpose(0, 2, 1).reshape(e, i // P, P, o).transpose(0, 2, 1, 3).reshape(e, P, i // P * o)

    arrays = dict(
        x=x, cls_rows=spread(cls_tok),
        w1=np.concatenate([W1[:, 0:2 * D], by_lane(W1[:, 2 * D:3 * D]), by_lane(W1[:, 3 * D:4 * D])], 1),
        b1uv=spread(b1[0:2 * D]),
        b1qk=np.concatenate([by_lane(b1[2 * D:3 * D]), by_lane(b1[3 * D:4 * D])]).reshape(4, P).T,
        w2=W2, b2=spread(b2),
        gb=np.concatenate([gamma.reshape(2, P).T, beta.reshape(2, P).T], 1),
        taps=spread(scharr), r1w=r1_w.T[0:D], r1s=r1_w.T[D:], r1b=r1_b.reshape(HID, 1), r2w=r2_w.T,
        wexp=np.concatenate([k_tiles(w_up), k_tiles(w_down)], 2),
        wadp=np.concatenate([k_tiles(a_up), k_tiles(a_down)], 2),
        consts=constants(x.shape[0]))
    return {k: np.ascontiguousarray(v) for k, v in arrays.items()}


def kernel(x, cls_tok, L0_tok_scharr, L0_attn_W1, L0_attn_b1, L0_attn_W2, L0_attn_b2, L0_attn_gamma, L0_attn_beta,
           L0_ffn_r1_w, L0_ffn_r1_b, L0_ffn_r2_w, L0_ffn_w_up, L0_ffn_w_down, L0_ffn_a_up, L0_ffn_a_down):
    import concourse.bacc as bacc
    from concourse.bass_utils import run_bass_kernel_spmd

    given = (x, cls_tok, L0_tok_scharr, L0_attn_W1, L0_attn_b1, L0_attn_W2, L0_attn_b2, L0_attn_gamma, L0_attn_beta,
             L0_ffn_r1_w, L0_ffn_r1_b, L0_ffn_r2_w, L0_ffn_w_up, L0_ffn_w_down, L0_ffn_a_up, L0_ffn_a_down)
    laid = layouts(*[np.asarray(t) for t in given])
    nb = laid["x"].shape[0]
    nc = bacc.Bacc("TRN2", target_bir_lowering=False, num_devices=1)
    arrays, args = {}, []
    for name, a in laid.items():
        arrays[f"in_{name}"] = a
        args.append(nc.dram_tensor(f"in_{name}", a.shape, mybir.dt.from_np(a.dtype), kind="ExternalInput").ap())
    args.append(nc.dram_tensor("out_rows", [nb * S + SLOTS, D], mybir.dt.float32, kind="ExternalOutput").ap())
    build(nc, *args, NB=nb, CAP=int(CAP_FACTOR * nb * S / NE))
    r = run_bass_kernel_spmd(nc, [arrays], core_ids=[0])
    return r.results[0]["out_rows"][0:nb * S].reshape(nb, S, D)
```

```python
from contextlib import ExitStack

import numpy as np

import concourse.bass as bass
from concourse import mybir

P = 128
C3 = 3
D = 256
R = 256
S = R + 1
H = 16
DH = D // H
NE = 32
HID = 128
NST = 8
INTER = 512
AINTER = 128
NG = 16
SLOTS = 384
ROW = 260
LN_EPS = 1e-5
GRAY = (0.2989, 0.587, 0.114)
CAP_FACTOR = 1.25
OOB = 1 << 20

CI = 0
CSH = CI + 128
CMK = CSH + 192
CMV = CMK + 256
CBE = CMV + 512
CLE = CBE + 128
CIE = CLE + 128
CSB = CIE + 32
CTK = CSB + 1
CTJ = CTK + 4
CTM = CTJ + 8
CTI = CTM + 32
CFI = CTI + 65
CEM = CFI + 3
CIO = CEM + 96
CTN = CIO + 128
CP1 = CTN + 65
CBH = CP1 + 1
CRS = CBH + 128
NC_ = CRS + 1


def constants(nb):
    c = np.zeros((P, NC_), np.float32)
    p = np.arange(P)
    c[:, CI:CI + 128] = np.eye(128)
    for dy in range(3):
        for r in range(64):
            c[r + dy, CSH + dy * 64 + r] = 1
    for a in range(2):
        for copy in range(3):
            c[p, CMK + a * 128 + copy * 32 + 8 * a + p % 8] = 1
    for tl in range(8):
        for a in range(2):
            h = a * 8 + tl
            for s in range(3):
                c[s * 32 + h, CMV + (tl * 2 + a) * 32:CMV + (tl * 2 + a) * 32 + DH] = 1
    ch, e = p // 32, p % 32
    c[:, CBE:CBE + 128] = e[:, None] == e[None, :]
    c[:, CLE:CLE + 128] = (e[:, None] == e[None, :]) & (ch[:, None] < ch[None, :])
    c[:, CIE:CIE + 32] = np.arange(32) - 64
    c[:, CSB] = e * SLOTS - 1 - OOB
    jn = nb // 4
    for t in range(nb):
        c[t, CTK + t // jn] = 1
        c[t, CTJ + t % jn] = 1
        c[(t // jn) * 32:(t // jn) * 32 + 32, CTM + t] = 1
    for t in range(2 * nb):
        q = (t % (2 * jn)) * 4 + t // (2 * jn)
        c[:, CTI + q] = (t // 2) * S + 1 + (t % 2) * 128 + p
        c[:, CTN + q] = t
    c[:nb, CTI + 2 * nb] = np.arange(nb) * S
    c[:, CTN + 2 * nb] = 2 * nb
    c[:, CEM:CEM + 96] = ((2 * nb + 1) * P + 1 + p)[:, None] + np.tile(np.arange(3) * P, NE)[None, :]
    c[:, CIO:CIO + 128] = np.arange(128)
    c[:, CP1] = p + 1
    c[:, CBH:CBH + 128] = 0.5 * c[:, CBE:CBE + 128]
    c[:, CRS] = 1
    c[5, CRS] = 1.0 / D
    for st in range(3):
        c[:, CFI + st] = nb * S + st * P + p
    return c


def build(nc, x, cls_rows, w1, b1uv, b1qk, w2, b2, gb, taps, r1w, r1s, r1b, r2w, wexp, consts, out,
          NB=32, CAP=321):
    f32, f32r, bf16, i32 = mybir.dt.float32, mybir.dt.float32r, mybir.dt.bfloat16, mybir.dt.int32
    ALU, ACT, AX = mybir.AluOpType, mybir.ActivationFunctionType, mybir.AxisListType

    NT = 2 * NB
    NTOK = NB * S
    JN = NB // 4
    CH = JN * S
    ctx = ExitStack()
    with ctx:
        names = set()

        def sb(name, shape, dt=f32):
            return ctx.enter_context(nc.sbuf_tensor(name, shape, dt))

        def sem(name):
            assert name not in names
            names.add(name)
            return ctx.enter_context(nc.semaphore(name))

        def dram(name, shape, dt=f32):
            return nc.dram_tensor(name, shape, dt, kind="Internal").ap()

        token_rows = dram("token_rows", [(NT + 1) * P + SLOTS, ROW])
        pre_dram = dram("pre_dram", [NB, P, R])
        cls_av = dram("cls_av", [NB, D])

        cst = sb("cst", [P, NC_])
        ident = cst[:, CI:CI + 128]
        stats8 = sb("stats8", [P, 2, NST])
        n05 = sb("n05", [P, 6])
        r1b_c = sb("r1b_c", [P, 1])
        r2w_sb = sb("r2w_sb", [P, NE])
        slot_token = sb("slot_token", [P, 3 * NE], i32)
        pre_cls = sb("pre_cls", [P, P])

        ph1 = ExitStack()

        def s1(name, shape, dt=f32):
            return ph1.enter_context(nc.sbuf_tensor(name, shape, dt))

        w1s = s1("w1s", [P, 2, 2, 1024], f32r)
        w2s = s1("w2s", [P, 2, 2, D], f32r)
        r1ws = s1("r1ws", [P, 2, 2, HID], f32r)
        r1st = s1("r1st", [96, HID])
        band = s1("band", [96, 2, 3, 128], f32r)
        b1uv_sb = s1("b1uv_sb", [P, 512])
        b1qk_sb = s1("b1qk_sb", [P, 4])
        bias2 = s1("bias2", [P, D])
        kc = s1("kc", [P, 2, 2, 128], f32r)
        qc = s1("qc", [P, 2, 2, 128], f32r)
        vc = s1("vc", [96, 4, 128], f32r)
        uvc = s1("uvc", [P, 512])
        ccv = s1("ccv", [P, D])
        halo = s1("halo", [96, 8, 258], f32r)
        qs = [s1(f"qs{i}", [96, 8, D], f32r) for i in range(2)]
        ks = [s1(f"ks{i}", [96, 2, 8, D], f32r) for i in range(2)]
        uvp = s1("uvp", [P, 2, 512])
        stt = s1("stt", [96, D])
        ones = s1("ones", [P, 1])
        bn = {k: s1("bn" + k, [P, 2, 6]) for k in "azhx"}
        mv = {k: s1("mv" + k, [P, 2, 2]) for k in "azhx"}
        ve = {k: s1("ve" + k, [P, 2]) for k in "azh"}
        rs = {k: s1("rs" + k, [P, 2]) for k in "azh"}
        spare = s1("spare", [1, 1])
        sq = s1("sq", [P, 2, 2])

        ps_s = [ctx.enter_context(nc.psum_tensor(f"ps_s{i}", [P, 2, 2, D], f32)) for i in range(2)]
        ps_av = [ctx.enter_context(nc.psum_tensor(f"ps_av{i}", [P, 512], f32)) for i in range(2)]
        ps_f = [ctx.enter_context(nc.psum_tensor(f"ps_f{i}", [P, 512], f32)) for i in range(2)]

        def wait(eng, s, value):
            if isinstance(value, int) and value <= 0:
                return
            eng.wait_ge(s, value)

        def mm3(o, lhs, rhs, first, last):
            lh, ll = lhs
            rh, rl = rhs
            nc.tensor.matmul(o, lh, rh, start=first, stop=False)
            nc.tensor.matmul(o, ll, rh, start=False, stop=False)
            return nc.tensor.matmul(o, lh, rl, start=False, stop=last)


        staging = ExitStack()
        stage = staging.enter_context(nc.sbuf_tensor("stage", [P, 6184], f32))
        w1f = stage[:, 0:2048].rearrange("p (k n) -> p k n", k=2)
        w2f = stage[:, 2048:2560].rearrange("p (k n) -> p k n", k=2)
        r1f = stage[:, 2560:2816].rearrange("p (k n) -> p k n", k=2)
        tapf = stage[:, 2816:2834]
        gbf = stage[:, 2834:2838]
        b2f = stage[:, 2840:3096]
        betaf = stage[:, 3096:3352].rearrange("p (k n) -> p k n", k=2)
        w2g = stage[:, 3352:3864].rearrange("p (k n) -> p k n", k=2)
        bandf = stage[:, 3864:4248].rearrange("p (x n) -> p x n", x=3)
        clsf = stage[:, 4248:4504]
        clsn = stage[:, 4504:4760]
        clst = stage[:, 4760:5016].rearrange("p (k n) -> p k n", k=2)
        qkcf = stage[:, 5016:5144].rearrange("p (m n) -> p m n", m=4)
        kqf = stage[:, 5144:5656].rearrange("p (m a n) -> p m a n", m=2, a=2)
        vcf = stage[:, 5656:6168]
        sccf = stage[:, 6168:6184]
        fill = staging.enter_context(nc.sbuf_tensor("fill", [P, 3, ROW], f32))
        loaded, r1s_loaded, filled = sem("loaded"), sem("r1s_loaded"), sem("filled")
        su_dve, su_act, su_pool, su_pe = sem("su_dve"), sem("su_act"), sem("su_pool"), sem("su_pe")
        with nc.Block() as block:
            loads = [
                (cst[:, :], consts), (w1f, w1.rearrange("(k p) n -> p k n", p=P)), (w2f, w2.rearrange("(k p) n -> p k n", p=P)),
                (r1f, r1w.rearrange("(k p) n -> p k n", p=P)), (tapf, taps), (gbf, gb), (b2f, b2), (clsf, cls_rows),
                (b1uv_sb[:, :], b1uv), (b1qk_sb[:, :], b1qk), (r1b_c[:, :], r1b), (r2w_sb[:, :], r2w),
            ]

            @block.sync
            def _(sp):
                for o, i in loads:
                    sp.dma_start(o, i).then_inc(loaded, 16)
                sp.wait_ge(su_dve, 3)
                sp.dma_start(token_rows[(NT + 1) * P:(NT + 1) * P + SLOTS, :].rearrange("(n p) w -> p n w", p=P), fill[:, :, :]).then_inc(filled, 16)
                sp.dma_start(out[NTOK:NTOK + SLOTS, :].rearrange("(n p) w -> p n w", p=P), fill[:, :, 0:D]).then_inc(filled, 16)
                sp.wait_ge(filled, 32)
                sp.wait_ge(su_pool, 1)
                sp.dma_start(r1st[0:6, :], r1s).then_inc(r1s_loaded, 16)
                sp.wait_ge(r1s_loaded, 16)

            @block.gpsimd
            def _(pool):
                nc.gpsimd.memset(r1st[:, :], 0.0).then_inc(su_pool, 1)
                nc.gpsimd.memset(stt[:, :], 0.0)
                nc.gpsimd.memset(stats8[:, :, :], 0.0)
                nc.gpsimd.memset(n05[:, 0:2], -0.5)
                nc.gpsimd.memset(n05[:, 2:6], 0.5)
                nc.gpsimd.memset(ones[:, :], 1.0)
                nc.gpsimd.memset(halo[:, :, :].bitcast(f32), 0.0)
                for i in range(2):
                    nc.gpsimd.memset(ks[i][:, :, :, :].bitcast(f32), 0.0)
                    nc.gpsimd.memset(qs[i][:, :, :].bitcast(f32), 0.0)
                nc.gpsimd.memset(vcf, 0.0).then_inc(su_pool, 1)
                pool.wait_ge(su_dve, 3)
                pool.wait_ge(su_pool, 2)
                nc.gpsimd.tensor_tensor(rs["z"][:, 0:1], ve["z"][:, 0:1], n05[:, 0:1], ALU.pow).then_inc(su_pool, 1)

            @block.vector
            def _(dve):
                tally = [0]

                def link(ins):
                    tally[0] += 1
                    ins.then_inc(su_dve, 1)
                    dve.wait_ge(su_dve, tally[0])

                dve.wait_ge(loaded, 16 * len(loads))
                nc.vector.memset(fill[:, :, :], 0.0)
                link(nc.vector.bn_stats(bn["z"][:, 0, :], clsf))
                link(nc.vector.bn_aggr(mv["z"][:, 0, :], bn["z"][:, 0, :]))
                nc.vector.tensor_copy(fill[:, :, ROW - 1].bitcast(i32), cst[:, CFI:CFI + 3])
                link(nc.vector.tensor_scalar(ve["z"][:, 0:1], mv["z"][:, 0, 1:2], LN_EPS, None, ALU.add))
                link(nc.vector.tensor_copy(w1s[:, 0, :, :], w1f))
                dve.wait_ge(su_pool, 3)
                link(nc.vector.tensor_scalar(clsn, clsf, mv["z"][:, 0, 0:1], rs["z"][:, 0:1], ALU.subtract, ALU.mult))
                for kt in range(2):
                    nc.vector.tensor_scalar(betaf[:, kt, :], ident, 0.0, gbf[:, 2 + kt:3 + kt], ALU.mult, ALU.add)
                    last = nc.vector.tensor_scalar(w2g[:, kt, :], w2f[:, kt, :], gbf[:, kt:kt + 1], None, ALU.mult)
                link(last)
                nc.vector.tensor_copy(w2s[:, 0, :, :], w2g)
                link(nc.vector.tensor_copy(r1ws[:, 0, :, :], r1f))
                nc.vector.tensor_tensor(w1s[:, 1, :, :], w1f, w1s[:, 0, :, :].bitcast(f32), ALU.subtract)
                nc.vector.tensor_tensor(w2s[:, 1, :, :], w2g, w2s[:, 0, :, :].bitcast(f32), ALU.subtract)
                nc.vector.tensor_tensor(r1ws[:, 1, :, :], r1f, r1ws[:, 0, :, :].bitcast(f32), ALU.subtract)
                for dy in range(3):
                    for dx in range(3):
                        for o in range(2):
                            dst = bandf[0:96, dx, 64 * o:64 * o + 64]
                            shift = cst[0:96, CSH + 64 * dy:CSH + 64 * dy + 64]
                            tap = tapf[0:96, o * 9 + dy * 3 + dx:o * 9 + dy * 3 + dx + 1]
                            if dy == 0:
                                last = nc.vector.tensor_scalar(dst, shift, tap, None, ALU.mult)
                            else:
                                last = nc.vector.scalar_tensor_tensor(dst, shift, tap, dst, ALU.mult, ALU.add)
                    link(last)
                link(nc.vector.tensor_copy(band[:, 0, :, :], bandf[0:96]))
                nc.vector.tensor_tensor(band[:, 1, :, :], bandf[0:96], band[:, 0, :, :].bitcast(f32), ALU.subtract)
                dve.wait_ge(su_pe, 1)
                link(nc.vector.tensor_copy(clst, ps_f[0][:, 0:256].rearrange("p (k n) -> p k n", k=2)))
                dve.wait_ge(su_pe, 3)
                nc.vector.tensor_tensor(uvp[:, 0, :], ps_f[1][:, :], b1uv_sb[:, :], ALU.add)
                link(nc.vector.tensor_tensor(bias2[:, :], ps_av[0][:, 0:256], b2f, ALU.add))
                dve.wait_ge(su_act, 1)
                for m, src in enumerate((2, 0)):
                    for a in range(2):
                        last = nc.vector.tensor_scalar(kqf[:, m, a, :], cst[:, CMK + 128 * a:CMK + 128 * a + 128],
                                                       qkcf[:, src + a, 0:1], None, ALU.mult)
                dve.wait_ge(su_pool, 2)
                link(nc.vector.tensor_tensor(
                    vcf[0:96, :].rearrange("p (tl a x) -> p tl a x", tl=8, a=2)[:, :, :, 0:16],
                    cst[0:96, CMV:CMV + 512].rearrange("p (tl a x) -> p tl a x", tl=8, a=2)[:, :, :, 0:16],
                    uvc[0:96, 256:512].rearrange("p (a tl d) -> p tl a d", a=2, tl=8), ALU.mult))
                nc.vector.tensor_copy(kc[:, 0, :, :], kqf[:, 0, :, :])
                nc.vector.tensor_copy(qc[:, 0, :, :], kqf[:, 1, :, :])
                link(nc.vector.tensor_copy(vc[:, :, :].rearrange("p t c -> p (t c)"), vcf[0:96, :]))
                nc.vector.tensor_tensor(kc[:, 1, :, :], kqf[:, 0, :, :], kc[:, 0, :, :].bitcast(f32), ALU.subtract)
                nc.vector.tensor_tensor(qc[:, 1, :, :], kqf[:, 1, :, :], qc[:, 0, :, :].bitcast(f32), ALU.subtract)
                vrow = vc[32:64, :, :].rearrange("p t c -> p (t c)")
                nc.vector.tensor_tensor(vrow, vcf[32:64, :], vrow.bitcast(f32), ALU.subtract)
                dve.wait_ge(r1s_loaded, 16)
                nc.vector.tensor_scalar(r1st[:, :], r1st[:, :], cst[0:96, CRS:CRS + 1], None, ALU.mult)
                dve.wait_ge(su_act, 2)
                link(nc.vector.tensor_tensor(ccv[0:32, :].rearrange("p (h d) -> p h d", d=DH),
                                             uvc[0:32, 256:512].rearrange("p (h d) -> p h d", d=DH),
                                             sccf[0:32, :].unsqueeze(2).to_broadcast([32, H, DH]), ALU.mult))

            @block.tensor
            def _(pe):
                pe.wait_ge(su_dve, 5)
                for kt in range(2):
                    last = nc.tensor.transpose(ps_f[0][:, 128 * kt:128 * kt + 128], clsn[:, 128 * kt:128 * kt + 128], ident)
                last.then_inc(su_pe, 1)
                pe.wait_ge(su_dve, 12)
                for m in range(4):
                    for kt in range(2):
                        last = nc.tensor.matmul(ps_s[0][:, 0, 0, 32 * m:32 * m + 32], w1f[:, kt, 512 + 128 * m:640 + 128 * m],
                                                clst[:, kt, 0:32], start=kt == 0, stop=kt == 1)
                last.then_inc(su_pe, 1)
                for kt in range(2):
                    nc.tensor.matmul(ps_f[1][:, :], clst[:, kt, :], w1f[:, kt, 0:512], start=kt == 0, stop=kt == 1)
                for kt in range(2):
                    last = nc.tensor.matmul(ps_av[0][:, 0:256], betaf[:, kt, :], w2f[:, kt, :], start=kt == 0, stop=kt == 1)
                last.then_inc(su_pe, 1)
                pe.wait_ge(su_dve, 14)
                for a in range(2):
                    last = nc.tensor.matmul(ps_av[1][0:32, 0:16], qkcf[:, a, :], kqf[:, 0, a, 0:16], start=a == 0, stop=a == 1)
                last.then_inc(su_pe, 1)

            @block.scalar
            def _(act):
                act.wait_ge(su_pe, 2)
                act.wait_ge(loaded, 16 * len(loads))
                for m in range(4):
                    nc.scalar.activation(qkcf[:, m, :], ps_s[0][:, 0, 0, 32 * m:32 * m + 32], ACT.Silu, bias=b1qk_sb[:, m:m + 1])
                act.wait_ge(su_dve, 13)
                nc.scalar.activation(uvc[:, :], uvp[:, 0, :], ACT.Silu).then_inc(su_act, 1)
                act.wait_ge(su_pe, 4)
                nc.scalar.activation(sccf[0:32, :], ps_av[1][0:32, 0:16], ACT.Silu).then_inc(su_act, 1)

        staging.close()

        xb = s1("xb", [P, 2, C3, D])
        g = s1("g", [P, 2, D])
        ghl = s1("ghl", [P, 4, D], f32r)
        absx = s1("absx", [P, 2, D])
        absy = s1("absy", [P, 2, D])
        h0 = s1("h0", [P, 2, D])
        h0b_all = s1("h0b", [P, 4, 2, D])
        h0b = [h0b_all[:, i] for i in range(4)]
        xn = s1("xn", [P, 2, D])
        xt = s1("xt", [P, 2, 2, D], f32r)
        qk = s1("qk", [P, 4, D])
        qkh = s1("qkh", [P, 4, D], f32r)
        qkl = s1("qkl", [P, 4, D], f32r)
        uv_all = s1("uv", [P, 2, 2, 512])
        uv = [uv_all[:, i] for i in range(2)]
        at_all = s1("at", [P, 4, 2, 2, D])
        at = [at_all[:, i] for i in range(4)]
        clc = s1("clc", [96, 512])
        cls_s = s1("cls_s", [96, D], f32r)
        va = s1("va", [P, 2, D])
        va2 = s1("va2", [P, D])
        crow = s1("crow", [1, D])
        avs = s1("avs", [P, 4, D])
        y = s1("y", [P, 2, D])
        z = s1("z", [P, 2, D])
        zt = s1("zt", [P, 2, 2, D], f32r)
        h2 = s1("h2", [P, 2, D])
        xf = s1("xf", [P, 2, D])
        axf = s1("axf", [P, 2, D])
        xft = s1("xft", [P, 2, 2, D], f32r)
        pre = s1("pre", [P, R])
        x_loaded, gray_a, gray_sum, gray_hi, gray_split = (sem(n) for n in ("x_loaded", "gray_a", "gray_sum", "gray_hi", "gray_split"))
        halo_loaded, conv_done, abs_done, h0_done, h0b_done = (sem(n) for n in ("halo_loaded", "conv_done", "abs_done", "h0_done", "h0b_done"))
        stat_a, ve_a, rs_a, xn_done, xt_ps, xt_hi, xt_done = (sem(n) for n in ("stat_a", "ve_a", "rs_a", "xn_done", "xt_ps", "xt_hi", "xt_done"))
        qk_ps, qk_act, qk_hi, qk_lo, stacked, uv_ps, uv_sum, uv_act = (sem(n) for n in ("qk_ps", "qk_act", "qk_hi", "qk_lo", "stacked", "uv_ps", "uv_sum", "uv_act"))
        cls_ps, cls_act, cls_hi, cls_ready, scores, attn, av_ps, av_out = (sem(n) for n in ("cls_ps", "cls_act", "cls_hi", "cls_ready", "scores", "attn", "av_ps", "av_out"))
        va_done, va_sum, crow_done, crow_out, avt_ps, y_done = (sem(n) for n in ("va_done", "va_sum", "crow_done", "crow_out", "avt_ps", "y_done"))
        stat_z, ve_z, rs_z, z_done, zt_ps, zt_hi, zt_done, w2_ps, h2_done, h2_out = (sem(n) for n in ("stat_z", "ve_z", "rs_z", "z_done", "zt_ps", "zt_hi", "zt_done", "w2_ps", "h2_done", "h2_out"))
        stat_h, ve_h, rs_h, xf_done, xf_out, axf_done = (sem(n) for n in ("stat_h", "ve_h", "rs_h", "xf_done", "xf_out", "axf_done"))
        stat_x, mean_sq, var_sq, sq_root, st_done, xft_ps, xft_hi, xft_done, stt_done, r1_ps, pre_done = (sem(n) for n in ("stat_x", "mean_sq", "var_sq", "sq_root", "st_done", "xft_ps", "xft_hi", "xft_done", "stt_done", "r1_ps", "pre_done"))
        pre_out = sem("pre_out")
        bna, bnz, bnh, bnx = (sem(n) for n in ("bna", "bnz", "bnh", "bnx"))

        def has(m):
            return not isinstance(m, int) or 0 <= m < NB

        def steps(eng, body):
            n0, per = 3, 4
            loops = max(0, (NB - 4 - n0) // per)
            for n in range(-3, n0):
                body(n, n % 4)
            if loops > 0:
                with eng.Fori(0, loops) as i:
                    for k in range(per):
                        body(i * per + (n0 + k), (n0 + k) % 4)
            for n in range(n0 + per * loops, NB + 2):
                body(n, n % 4)

        def av_count(m, t):
            return 4 * m + t + 1

        def st_count(m):
            return av_count(m + 2, 1) if not isinstance(m, int) or m < NB - 2 else 4 * NB + m - (NB - 2) + 1

        UNITS = ["E", "A0", "D0", "D1", "B0", "B1", "B2", "D2", "A1", "B3", "D3", "G0", "B4", "D4"]
        LAG = {"E": 0, "G": -2, "D": -1, "B": 1, "A": 2}
        READ = {"E": (cls_act, 1, 1), "G0": (pre_done, 1, 1), "D0": (y_done, 2, 1), "D1": (y_done, 2, 2),
                "B0": (xt_done, 1, 1), "A0": (abs_done, 2, 1), "A1": (abs_done, 2, 2),
                "B1": (qk_act, 2, 1), "B2": (qk_act, 2, 2), "B3": (uv_sum, 2, 1), "B4": (uv_sum, 2, 2),
                "D2": (zt_done, 1, 1), "D3": (h2_done, 1, 1), "D4": (xft_done, 1, 1)}

        def bank_free(pe, n, unit):
            k = UNITS.index(unit) - 2
            for _ in range(14):
                step, u = (n, UNITS[k]) if k >= 0 else (n - 1, UNITS[k + 14])
                m = step + LAG[u[0]]
                if has(m):
                    s, per, ev = READ[u]
                    pe.wait_ge(s, m * per + ev)
                    return
                k -= 2
                if k < -14:
                    return

        def bank(unit):
            return ps_f[UNITS.index(unit) % 2]

        images = ExitStack()
        block = images.enter_context(nc.Block())

        @block.tensor
        def _(pe):
            def conv(n, m, hf, unit):
                if hf == 0:
                    pe.wait_ge(halo_loaded, 64 * (m + 1))
                bank_free(pe, n, unit)
                for par in range(2):
                    o = bank(unit)[:, 256 * par:256 * par + 256]
                    j = 2 * hf + par
                    for dx in range(3):
                        last = mm3(o, (band[:, 0, dx, :], band[:, 1, dx, :]),
                                   (halo[:, j, dx:dx + 256], halo[:, 4 + j, dx:dx + 256]), dx == 0, dx == 2)
                last.then_inc(conv_done, 1)

            def transposes(n, unit, src, ready, value, done):
                pe.wait_ge(ready, value)
                bank_free(pe, n, unit)
                for hf in range(2):
                    for kt in range(2):
                        last = nc.tensor.transpose(bank(unit)[:, kt * 256 + hf * 128:kt * 256 + hf * 128 + 128],
                                                   src[:, hf, kt * 128:kt * 128 + 128], ident)
                last.then_inc(done, 1)

            def proj_qk(n, m, kind, unit):
                bank_free(pe, n, unit)
                if kind == 0:
                    pe.wait_ge(xt_done, m + 1)
                for a in range(2):
                    col = 512 + 256 * kind + 128 * a
                    for kt in range(2):
                        last = mm3(bank(unit)[:, 256 * a:256 * a + 256],
                                   (w1s[:, 0, kt, col:col + 128], w1s[:, 1, kt, col:col + 128]),
                                   (xt[:, 0, kt, :], xt[:, 1, kt, :]), kt == 0, kt == 1)
                last.then_inc(qk_ps, 1)

            def proj_uv(n, m, hf, unit):
                bank_free(pe, n, unit)
                for kt in range(2):
                    last = mm3(bank(unit)[:, :],
                               (xt[:, 0, kt, hf * 128:hf * 128 + 128], xt[:, 1, kt, hf * 128:hf * 128 + 128]),
                               (w1s[:, 0, kt, 0:512], w1s[:, 1, kt, 0:512]), kt == 0, kt == 1)
                last.then_inc(uv_ps, 1)

            def cls_scores(n, m):
                pe.wait_ge(qk_hi, 2 * m + 2)
                pe.wait_ge(qk_lo, 2 * m + 2)
                bank_free(pe, n, "E")
                for kind, st in ((0, kc), (1, qc)):
                    for a in range(2):
                        last = mm3(bank("E")[:, 256 * kind:256 * kind + 256], (st[:, 0, a, :], st[:, 1, a, :]),
                                   (qkh[:, 2 * kind + a, :], qkl[:, 2 * kind + a, :]), a == 0, a == 1)
                last.then_inc(cls_ps, 1)

            def score(n, r, m, gq):
                if gq == 0:
                    pe.wait_ge(stacked, 192 * (m + 1))
                wait(pe, attn, 8 * m + gq - 1)
                for a in range(2):
                    for kt in range(2):
                        last = nc.tensor.matmul(ps_s[gq % 2][:, a, kt, :], ks[r % 2][:, a, gq, kt * 128:kt * 128 + 128],
                                                qs[r % 2][:, gq, :], start=True, stop=True)
                last.then_inc(scores, 1)

            def weighted(n, r, m, t):
                if t == 0:
                    pe.wait_ge(cls_ready, m + 1)
                    pe.wait_ge(uv_act, 2 * m + 2)
                pe.wait_ge(attn, 8 * m + 2 * t + 2)
                wait(pe, av_out, 4 * m + t - 1)
                if t == 0:
                    wait(pe, crow_done, m)
                if t == 1:
                    wait(pe, stt_done, m - 2)
                o = ps_av[t % 2]
                nc.tensor.matmul(o[:, 0:256], vc[:, t, :], cls_s[:, :], start=True, stop=False, skip_group_check=True)
                for kt in range(2):
                    for j in range(4):
                        l2, a = j // 2, j % 2
                        h = a * 8 + 2 * t + l2
                        last = nc.tensor.matmul(o[32 * j:32 * j + 16, 0:256], uv[r % 2][:, kt, 256 + h * 16:256 + h * 16 + 16],
                                                at[(2 * t + l2) % 4][:, a, kt, :], start=False, stop=kt == 1,
                                                skip_group_check=True)
                if t == 0:
                    for kt in range(2):
                        last = nc.tensor.transpose(o[:, 256 + 16 * kt:272 + 16 * kt],
                                                   clc[0:16, 256 + 128 * kt:384 + 128 * kt], ident[0:16, 0:16])
                if t == 2:
                    pe.wait_ge(va_sum, m + 1)
                    last = nc.tensor.matmul(o[0:1, 256:512], ones[:, 0:1], va2[:, :], start=True, stop=True)
                return last

            def body(n, r):
                a, b, c, d, e = n + 2, n + 1, n, n - 1, n - 2
                if has(c):
                    cls_scores(n, c)
                    score(n, r, c, 0)
                    score(n, r, c, 1)
                if has(a):
                    conv(n, a, 0, "A0")
                if has(d):
                    pe.wait_ge(av_out, 4 * d + 4)
                    for hf in range(2):
                        u = ("D0", "D1")[hf]
                        bank_free(pe, n, u)
                        for t in range(4):
                            last = nc.tensor.transpose(bank(u)[:, 128 * t:128 * t + 128], avs[:, t, hf * 128:hf * 128 + 128], ident)
                        last.then_inc(avt_ps, 1)
                        if hf == 0 and has(c):
                            score(n, r, c, 2)
                if has(b):
                    transposes(n, "B0", xn, xn_done, b + 1, xt_ps)
                if has(c) and not has(d):
                    score(n, r, c, 2)
                if has(c):
                    weighted(n, r, c, 0).then_inc(av_ps, 1)
                if has(c):
                    score(n, r, c, 3)
                if has(b):
                    proj_qk(n, b, 0, "B1")
                if has(b):
                    proj_qk(n, b, 1, "B2")
                if has(d):
                    transposes(n, "D2", z, z_done, d + 1, zt_ps)
                last = None
                if has(c):
                    score(n, r, c, 4)
                    last = weighted(n, r, c, 1)
                if has(e):
                    pe.wait_ge(st_done, e + 1)
                    if not has(c):
                        wait(pe, stt_done, e)
                    for hf in range(2):
                        last = nc.tensor.transpose(ps_av[1][0:NST, 256 + 128 * hf:384 + 128 * hf], stats8[:, hf, :], ident)
                if last is not None:
                    last.then_inc(av_ps, 1)
                if has(a):
                    conv(n, a, 1, "A1")
                if has(c):
                    score(n, r, c, 5)
                if has(b):
                    proj_uv(n, b, 0, "B3")
                if has(d):
                    pe.wait_ge(zt_done, d + 1)
                    bank_free(pe, n, "D3")
                    for hf in range(2):
                        for kt in range(2):
                            last = mm3(bank("D3")[:, 256 * hf:256 * hf + 256],
                                       (zt[:, 0, kt, hf * 128:hf * 128 + 128], zt[:, 1, kt, hf * 128:hf * 128 + 128]),
                                       (w2s[:, 0, kt, :], w2s[:, 1, kt, :]), kt == 0, kt == 1)
                    last.then_inc(w2_ps, 1)
                if has(e):
                    pe.wait_ge(xft_done, e + 1)
                    pe.wait_ge(stt_done, e + 1)
                    bank_free(pe, n, "G0")
                    o = bank("G0")[:, 0:256]
                    for kt in range(2):
                        mm3(o, (r1ws[:, 0, kt, :], r1ws[:, 1, kt, :]), (xft[:, 0, kt, :], xft[:, 1, kt, :]), kt == 0, False)
                    nc.tensor.matmul(o, r1st[:, :], stt[:, :], start=False, stop=True).then_inc(r1_ps, 1)
                if has(c):
                    score(n, r, c, 6)
                    score(n, r, c, 7)
                if has(b):
                    proj_uv(n, b, 1, "B4")
                if has(c):
                    weighted(n, r, c, 2).then_inc(av_ps, 1)
                if has(d):
                    transposes(n, "D4", xf, xf_done, d + 1, xft_ps)
                if has(c):
                    weighted(n, r, c, 3).then_inc(av_ps, 1)

            steps(pe, body)

        @block.scalar
        def _(act):
            def body(n, r):
                a, b, c, d, e, gm = n + 2, n + 1, n, n - 1, n - 2, n + 3
                if has(c):
                    act.wait_ge(cls_ps, c + 1)
                    wait(act, va_done, c)
                    nc.scalar.activation(clc[:, :], bank("E")[0:96, :], ACT.Silu).then_inc(cls_act, 1)

                def silu_scores(gq):
                    act.wait_ge(scores, 8 * c + gq + 1)
                    if gq < 4:
                        wait(act, av_ps, av_count(c - 1, 3 if gq >= 2 else 2))
                    else:
                        act.wait_ge(av_ps, av_count(c, (gq - 4) // 2))
                    nc.scalar.activation(at[gq % 4][:, :, :, :].rearrange("p a k q -> p (a k q)"),
                                         ps_s[gq % 2][:, :, :, :].rearrange("p a k q -> p (a k q)"), ACT.Silu).then_inc(attn, 1)

                def abs_edges(hf):
                    act.wait_ge(conv_done, 2 * a + hf + 1)
                    if hf == 0:
                        wait(act, h0_done, a)
                    bk = bank(("A0", "A1")[hf])
                    nc.scalar.activation(absx[0:64, hf, :], bk[0:64, 0:256], ACT.Abs)
                    nc.scalar.activation(absx[64:128, hf, :], bk[0:64, 256:512], ACT.Abs)
                    nc.scalar.activation(absy[0:64, hf, :], bk[64:128, 0:256], ACT.Abs)
                    nc.scalar.activation(absy[64:128, hf, :], bk[64:128, 256:512], ACT.Abs).then_inc(abs_done, 1)

                def silu_qk(kind):
                    act.wait_ge(qk_ps, 2 * b + kind + 1)
                    wait(act, qk_hi, 2 * b + kind - 1)
                    wait(act, qk_lo, 2 * b + kind - 1)
                    bk = bank(("B1", "B2")[kind])
                    nc.scalar.activation(qk[:, 2 * kind, :], bk[:, 0:256], ACT.Silu, bias=b1qk_sb[:, 2 * kind:2 * kind + 1])
                    nc.scalar.activation(qk[:, 2 * kind + 1, :], bk[:, 256:512], ACT.Silu,
                                         bias=b1qk_sb[:, 2 * kind + 1:2 * kind + 2]).then_inc(qk_act, 1)

                def silu_uv(hf):
                    act.wait_ge(uv_sum, 2 * b + hf + 1)
                    wait(act, y_done, 2 * b - 2)
                    wait(act, av_ps, av_count(b - 2, 3))
                    wait(act, va_done, b - 1)
                    nc.scalar.activation(uv[(r + 1) % 2][:, hf, :], uvp[:, hf, :], ACT.Silu).then_inc(uv_act, 1)

                if has(c):
                    silu_scores(0)
                    silu_scores(1)
                if has(a):
                    abs_edges(0)
                if has(gm):
                    act.wait_ge(x_loaded, 32 * (gm + 1))
                    wait(act, gray_split, gm)
                    nc.scalar.activation(g[:, :, :], xb[:, :, 0, :], ACT.Copy,
                                         scale=float(np.float32(GRAY[0]) / 2)).then_inc(gray_a, 1)
                if has(c):
                    silu_scores(2)
                if has(b):
                    silu_qk(0)
                if has(c):
                    silu_scores(3)
                if has(b):
                    silu_qk(1)
                if has(c):
                    silu_scores(4)
                if has(a):
                    abs_edges(1)
                if has(c):
                    silu_scores(5)
                if has(b):
                    silu_uv(0)
                if has(e):
                    act.wait_ge(r1_ps, e + 1)
                    wait(act, pre_out, 16 * e)
                    nc.scalar.activation(pre[:, :], bank("G0")[:, 0:256], ACT.Copy).then_inc(pre_done, 1)
                if has(c):
                    silu_scores(6)
                if has(b):
                    silu_uv(1)
                if has(c):
                    silu_scores(7)
                if has(d):
                    act.wait_ge(xf_done, d + 1)
                    wait(act, st_done, d)
                    nc.scalar.activation(axf[:, :, :], xf[:, :, :], ACT.Abs).then_inc(axf_done, 1)

            steps(act, body)

        @block.vector
        def _(dve):
            def norm_stats(src, k, done_bn, done_stat, done_ve, eps, m):
                nc.vector.bn_stats(bn[k][:, 0, :], src[:, 0, :])
                nc.vector.bn_stats(bn[k][:, 1, :], src[:, 1, :]).then_inc(done_bn, 1)
                dve.wait_ge(done_bn, m + 1)
                nc.vector.memset(spare[:, :], 0.0)
                nc.vector.bn_aggr(mv[k][:, 0, :], bn[k][:, 0, :])
                nc.vector.bn_aggr(mv[k][:, 1, :], bn[k][:, 1, :]).then_inc(done_stat, 1)
                dve.wait_ge(done_stat, m + 1)
                if done_ve is not None:
                    nc.vector.tensor_scalar(ve[k][:, :], mv[k][:, :, 1], eps, None, ALU.add).then_inc(done_ve, 1)

            def normalise(dst, src, k, done):
                nc.vector.tensor_scalar(dst[:, 0, :], src[:, 0, :], mv[k][:, 0, 0:1], rs[k][:, 0:1], ALU.subtract, ALU.mult)
                nc.vector.tensor_scalar(dst[:, 1, :], src[:, 1, :], mv[k][:, 1, 0:1], rs[k][:, 1:2], ALU.subtract,
                                        ALU.mult).then_inc(done, 1)

            def split_t(dst, src, m, hi, done):
                nc.vector.tensor_copy(dst[:, 0, :, :].rearrange("p k t -> p (k t)"), src).then_inc(hi, 1)
                dve.wait_ge(hi, m + 1)
                nc.vector.tensor_tensor(dst[:, 1, :, :].rearrange("p k t -> p (k t)"), src,
                                        dst[:, 0, :, :].rearrange("p k t -> p (k t)").bitcast(f32), ALU.subtract).then_inc(done, 1)

            def body(n, r):
                a, b, c, d, e, gm = n + 2, n + 1, n, n - 1, n - 2, n + 3
                if has(c):
                    dve.wait_ge(cls_act, c + 1)
                    wait(dve, av_ps, 4 * c)
                    nc.vector.tensor_copy(cls_s[:, :], clc[:, 0:256]).then_inc(cls_hi, 1)
                    dve.wait_ge(cls_hi, c + 1)
                    nc.vector.tensor_tensor(cls_s[64:96, :], clc[64:96, 0:256], cls_s[64:96, :].bitcast(f32),
                                            ALU.subtract).then_inc(cls_ready, 1)
                if has(d):
                    for hf in range(2):
                        dve.wait_ge(avt_ps, 2 * d + hf + 1)
                        nc.vector.tensor_tensor(
                            y[:, hf, :].rearrange("p (a tl d) -> p tl a d", a=2, tl=8),
                            bank(("D0", "D1")[hf])[:, :].rearrange("p (tl a x) -> p tl a x", tl=8, a=2)[:, :, :, 0:16],
                            uv[(r - 1) % 2][:, hf, 0:256].rearrange("p (a tl d) -> p tl a d", a=2, tl=8),
                            ALU.mult).then_inc(y_done, 1)
                if has(b):
                    dve.wait_ge(xt_ps, b + 1)
                    wait(dve, uv_ps, 2 * b)
                    split_t(xt, bank("B0")[:, :], b, xt_hi, xt_done)
                if has(d):
                    dve.wait_ge(y_done, 2 * d + 2)
                    norm_stats(y, "z", bnz, stat_z, ve_z, LN_EPS * S * S, d)
                if has(d):
                    dve.wait_ge(rs_z, d + 1)
                    wait(dve, zt_ps, d)
                    normalise(z, y, "z", z_done)
                if has(gm):
                    dve.wait_ge(gray_a, gm + 1)
                    nc.vector.scalar_tensor_tensor(g[:, :, :], xb[:, :, 1, :], float(np.float32(GRAY[1]) / 2), g[:, :, :],
                                                   ALU.mult, ALU.add).then_inc(gray_sum, 1)
                    dve.wait_ge(gray_sum, 2 * gm + 1)
                    nc.vector.scalar_tensor_tensor(g[:, :, :], xb[:, :, 2, :], float(np.float32(GRAY[2]) / 2), g[:, :, :],
                                                   ALU.mult, ALU.add).then_inc(gray_sum, 1)
                    dve.wait_ge(gray_sum, 2 * gm + 2)
                    wait(dve, halo_loaded, 64 * gm)
                    nc.vector.tensor_copy(ghl[:, 0:2, :], g[:, :, :]).then_inc(gray_hi, 1)
                    dve.wait_ge(gray_hi, gm + 1)
                    nc.vector.tensor_tensor(ghl[:, 2:4, :], g[:, :, :], ghl[:, 0:2, :].bitcast(f32),
                                            ALU.subtract).then_inc(gray_split, 1)

                def av_read(t):
                    dve.wait_ge(av_ps, av_count(c, t))
                    if t == 0:
                        wait(dve, avt_ps, 2 * c)
                        wait(dve, va_sum, c)
                        nc.vector.tensor_tensor(
                            va[:, :, :].rearrange("p k (h d) -> p k h d", d=DH),
                            uv[r % 2][:, :, 256:512].rearrange("p k (h d) -> p k h d", d=DH),
                            ps_av[0][:, 256:288].rearrange("p (k h) -> p k h", k=2).unsqueeze(3).to_broadcast([P, 2, H, DH]),
                            ALU.mult).then_inc(va_done, 1)
                    nc.vector.tensor_copy(avs[:, t, :], ps_av[t % 2][:, 0:256]).then_inc(av_out, 1)

                def qk_split(kind):
                    dve.wait_ge(qk_act, 2 * b + kind + 1)
                    wait(dve, stacked, 192 * b)
                    wait(dve, cls_ps, b)
                    nc.vector.tensor_copy(qkh[:, 2 * kind:2 * kind + 2, :], qk[:, 2 * kind:2 * kind + 2, :]).then_inc(qk_hi, 1)

                if has(c):
                    av_read(0)
                if has(b):
                    qk_split(0)
                if has(d):
                    dve.wait_ge(zt_ps, d + 1)
                    wait(dve, w2_ps, d)
                    split_t(zt, bank("D2")[:, :], d, zt_hi, zt_done)
                if has(b):
                    qk_split(1)
                if has(c):
                    av_read(1)
                if has(e):
                    dve.wait_ge(av_ps, st_count(e))
                    nc.vector.tensor_copy(stt[0:NST, :], ps_av[1][0:NST, 256:512]).then_inc(stt_done, 1)
                if has(b):
                    dve.wait_ge(uv_ps, 2 * b + 1)
                    wait(dve, uv_act, 2 * b)
                    nc.vector.tensor_tensor(uvp[:, 0, :], bank("B3")[:, :], b1uv_sb[:, :], ALU.add).then_inc(uv_sum, 1)
                if has(a):
                    dve.wait_ge(abs_done, 2 * a + 2)
                    wait(dve, h0b_done, a)
                    nc.vector.tensor_tensor(h0[:, :, :], absx[:, :, :], absy[:, :, :], ALU.add).then_inc(h0_done, 1)
                    dve.wait_ge(h0_done, a + 1)
                    norm_stats(h0, "a", bna, stat_a, ve_a, LN_EPS, a)
                if has(d):
                    dve.wait_ge(w2_ps, d + 1)
                    dve.wait_ge(h0b_done, d + 1)
                    wait(dve, h2_out, 32 * d)
                    nc.vector.tensor_tensor(h2[:, :, :], bank("D3")[:, :].rearrange("p (a q) -> p a q", a=2), h0b[(r - 1) % 4][:, :, :],
                                            ALU.add).then_inc(h2_done, 1)
                    dve.wait_ge(h2_done, d + 1)
                    norm_stats(h2, "h", bnh, stat_h, ve_h, LN_EPS, d)
                if has(a):
                    dve.wait_ge(rs_a, a + 1)
                    wait(dve, xt_ps, a)
                    normalise(xn, h0, "a", xn_done)
                if has(b):
                    dve.wait_ge(uv_ps, 2 * b + 2)
                    nc.vector.tensor_tensor(uvp[:, 1, :], bank("B4")[:, :], b1uv_sb[:, :], ALU.add).then_inc(uv_sum, 1)
                if has(d):
                    dve.wait_ge(rs_h, d + 1)
                    wait(dve, xft_ps, d)
                    wait(dve, xf_out, 32 * d)
                    normalise(xf, h2, "h", xf_done)
                    dve.wait_ge(xf_done, d + 1)
                    norm_stats(xf, "x", bnx, stat_x, None, 0.0, d)
                    wait(dve, av_ps, st_count(d - 1))
                    nc.vector.tensor_copy(stats8[:, :, 0:1], mv["x"][:, :, 0:1])
                    nc.vector.tensor_tensor(sq[:, :, 1:2], mv["x"][:, :, 0:1], mv["x"][:, :, 0:1], ALU.mult)
                    nc.vector.tensor_scalar(sq[:, :, 0:1], mv["x"][:, :, 1:2], float(D) / (D - 1), None, ALU.mult).then_inc(mean_sq, 1)
                    nc.vector.tensor_reduce(stats8[:, :, 2:3], xf[:, :, :], AX.X, ALU.min)
                    nc.vector.tensor_reduce(stats8[:, :, 3:4], xf[:, :, :], AX.X, ALU.max)
                    dve.wait_ge(mean_sq, d + 1)
                    nc.vector.tensor_tensor(sq[:, :, 1:2], sq[:, :, 1:2], mv["x"][:, :, 1:2], ALU.add).then_inc(var_sq, 1)
                if has(c):
                    av_read(2)
                    wait(dve, crow_out, 16 * c)
                    nc.vector.tensor_copy(crow[0:1, :], ps_av[0][0:1, 256:512]).then_inc(crow_done, 1)
                if has(d):
                    dve.wait_ge(xft_ps, d + 1)
                    wait(dve, r1_ps, d)
                    split_t(xft, bank("D4")[:, :], d, xft_hi, xft_done)
                if has(c):
                    av_read(3)
                if has(d):
                    dve.wait_ge(axf_done, d + 1)
                    for hf in range(2):
                        nc.vector.tensor_scalar(axf[:, hf, :], axf[:, hf, :], 1e-6, None, ALU.is_lt, ALU.add,
                                                accum_out=stats8[:, hf, 5:6])
                    dve.wait_ge(sq_root, d + 1)
                    nc.vector.tensor_copy(stats8[:, :, 1:2], sq[:, :, 0:1])
                    nc.vector.tensor_scalar(stats8[:, :, 4:5], sq[:, :, 1:2], float(D) ** 0.5, None, ALU.mult).then_inc(st_done, 1)

            steps(dve, body)

        @block.gpsimd
        def _(pool):
            def rsqrt(k, ready, done, m):
                pool.wait_ge(ready, m + 1)
                nc.gpsimd.tensor_tensor(rs[k][:, :], ve[k][:, :], n05[:, 0:2], ALU.pow).then_inc(done, 1)

            def body(n, r):
                a, b, c, d, e = n + 2, n + 1, n, n - 1, n - 2
                if has(d):
                    wait(pool, z_done, d)
                    rsqrt("z", ve_z, rs_z, d)
                if has(c):
                    pool.wait_ge(va_done, c + 1)
                    wait(pool, av_ps, av_count(c - 1, 2))
                    nc.gpsimd.tensor_tensor(va2[:, :], va[:, 0, :], va[:, 1, :], ALU.add).then_inc(va_sum, 1)
                if has(b):
                    for kind in range(2):
                        pool.wait_ge(qk_hi, 2 * b + kind + 1)
                        nc.gpsimd.tensor_tensor(qkl[:, 2 * kind:2 * kind + 2, :], qk[:, 2 * kind:2 * kind + 2, :],
                                                qkh[:, 2 * kind:2 * kind + 2, :].bitcast(f32), ALU.subtract).then_inc(qk_lo, 1)
                if has(a):
                    wait(pool, xn_done, a)
                    rsqrt("a", ve_a, rs_a, a)
                    pool.wait_ge(h0_done, a + 1)
                    wait(pool, h2_done, a - 3)
                    nc.gpsimd.tensor_tensor(h0b[(r + 2) % 4][:, :, :], h0[:, :, :],
                                            bias2[:, :].unsqueeze(1).to_broadcast([P, 2, D]), ALU.add).then_inc(h0b_done, 1)
                if has(d):
                    wait(pool, xf_done, d)
                    rsqrt("h", ve_h, rs_h, d)
                    pool.wait_ge(var_sq, d + 1)
                    nc.gpsimd.tensor_tensor(sq[:, :, :], sq[:, :, :], n05[:, 2:6].rearrange("p (a b) -> p a b", a=2),
                                            ALU.pow).then_inc(sq_root, 1)
            steps(pool, body)

        @block.sync
        def _(sp):
            def load_x(m):
                wait(sp, gray_split, m)
                for hf in range(2):
                    sp.dma_start(xb[:, hf, :, :], x[bass.ds(m, 1), :, hf * 128:hf * 128 + 128, :].rearrange(
                        "o c p w -> p (o c) w")).then_inc(x_loaded, 16)

            def body(n, r):
                a, b, c, d, e, gm = n + 2, n + 1, n, n - 1, n - 2, n + 3
                if isinstance(n, int) and n == -3:
                    load_x(0)
                nx = n + 4
                if has(nx) and (not isinstance(nx, int) or nx > 0):
                    load_x(nx)
                if has(b):
                    for kind, (dst, slots) in enumerate(((qs, "hhl"), (ks, "hlh"))):
                        sp.wait_ge(qk_hi, 2 * b + kind + 1)
                        sp.wait_ge(qk_lo, 2 * b + kind + 1)
                        for a2 in range(2):
                            for s, part in enumerate(slots):
                                row = 48 * a2 + 16 * s
                                o = dst[(r + 1) % 2]
                                o = o[row:row + 16, :, :] if kind == 0 else o[row:row + 16, a2, :, :]
                                sp.dma_start(o.bitcast(f32), (qkh if part == "h" else qkl)[:, 2 * kind + a2, :].bitcast(f32)).then_inc(stacked, 16)
                if has(gm):
                    wait(sp, conv_done, 2 * gm)
                    sp.wait_ge(gray_split, gm + 1)
                    for out_ap, in_ap in (
                        (halo[1:66, 0:8:2, 1:257], ghl[0:65, :, :]),
                        (halo[0:65, 1:8:2, 1:257], ghl[63:128, :, :]),
                        (halo[65:66, 1:8:4, 1:257], ghl[0:1, 1:4:2, :]),
                        (halo[0:1, 2:8:4, 1:257], ghl[127:128, 0:4:2, :]),
                    ):
                        sp.dma_start(out_ap.bitcast(f32), in_ap.bitcast(f32)).then_inc(halo_loaded, 16)
                if has(d):
                    sp.wait_ge(h2_done, d + 1)
                    for hf in range(2):
                        sp.dma_start(out[bass.ds(d * S + 1 + 128 * hf, 128), :], h2[:, hf, :]).then_inc(h2_out, 16)
                    sp.wait_ge(xf_done, d + 1)
                    for hf in range(2):
                        sp.dma_start(token_rows[bass.ds(2 * d * P + hf * P, P), 0:D], xf[:, hf, :]).then_inc(xf_out, 16)
                if has(e):
                    sp.wait_ge(pre_done, e + 1)
                    sp.dma_start(pre_dram[bass.ds(e, 1), :, :].rearrange("o p t -> (o p) t"), pre[:, :]).then_inc(pre_out, 16)
                if has(c):
                    sp.wait_ge(crow_done, c + 1)
                    sp.dma_start(cls_av[bass.ds(c, 1), :], crow[0:1, :]).then_inc(crow_out, 16)

            steps(sp, body)
            sp.wait_ge(h2_out, 32 * NB)
            sp.wait_ge(xf_out, 32 * NB)
            sp.wait_ge(crow_out, 16 * NB)
            sp.wait_ge(pre_out, 16 * NB)
        images.close()

        def chain(eng, s):
            tally = [0]

            def link(ins, value=None):
                tally[0] += 1
                assert value is None or value == tally[0], (value, tally[0])
                ins.then_inc(s, 1)
                eng.wait_ge(s, tally[0])
            link.tally = tally
            return link

        TI = 2 * JN
        NQ = NT + 1
        hid = [at_all[:, 0:2].rearrange("p i a k q -> p (i a k q)"), at_all[:, 2:4].rearrange("p i a k q -> p (i a k q)"),
               h0b_all[:, :, :, :].rearrange("p i a q -> p (i a q)"), uv_all[:, :, :, :].rearrange("p i a q -> p (i a q)")]
        hid_load = [sem(f"hid_load{c}") for c in range(4)]
        hid_act = sem("hid_act")

        def tiles(k, n):
            return ps_s[k][:, :, :, :].rearrange("p a k q -> p (a k q)")[:, 0:n * NE].rearrange("p (t e) -> p t e", e=NE)

        classes = ExitStack()
        block = classes.enter_context(nc.Block())
        cls_load, ct_dve, ct_pe, ct_pool, ct_act, cls_var, cls_out = (sem(n) for n in ("cls_load", "ct_dve", "ct_pe", "ct_pool", "ct_act", "cls_var", "cls_out"))
        B = slice(0, NB)
        clsr = h0[:, 0, :]
        Z_, ZT_, VH_, XF_, SQ_, ST_, XT_, PRE_ = 6, 8, 11, 12, 16, 19, 21, 22

        @block.sync
        def _(sp):
            sp.dma_start(y[B, 0, :], cls_av).then_inc(cls_load, 16)
            sp.dma_start(h0[:, 1, :], cls_rows).then_inc(cls_load, 16)
            for c in range(4):
                sp.dma_start(hid[c][:, 0:TI * P].rearrange("p (m t) -> p m t", t=R),
                             pre_dram[c * JN:(c + 1) * JN].rearrange("m p t -> p m t")).then_inc(hid_load[c], 16)
            sp.wait_ge(ct_dve, VH_)
            sp.dma_start(out[0:NTOK, :].rearrange("(b s) w -> b s w", s=S)[:, 0, :], h2[B, 0, :]).then_inc(cls_out, 16)
            sp.wait_ge(ct_dve, XF_)
            sp.dma_start(token_rows[NT * P:NT * P + P, 0:D], xf[:, 0, :]).then_inc(cls_out, 16)
            sp.wait_ge(cls_out, 32)

        @block.vector
        def _(dve):
            link = chain(dve, ct_dve)
            nc.vector.memset(z[:, 0, :], 0.0)
            nc.vector.memset(xf[:, 0, :], 0.0)
            nc.vector.memset(stats8[:, 0, :], 0.0)
            dve.wait_ge(cls_load, 32)
            nc.vector.tensor_tensor(clsr, h0[:, 1, :], bias2[:, :], ALU.add)
            link(nc.vector.tensor_tensor(y[B, 0, :], y[B, 0, :], ccv[B, :], ALU.add))
            link(nc.vector.tensor_tensor(y[B, 0, :], y[B, 0, :], uvc[B, 0:256], ALU.mult))
            link(nc.vector.bn_stats(bn["z"][B, 0, :], y[B, 0, :]))
            link(nc.vector.bn_aggr(mv["z"][B, 0, :], bn["z"][B, 0, :]))
            link(nc.vector.tensor_scalar(ve["z"][B, 0:1], mv["z"][B, 0, 1:2], LN_EPS * S * S, None, ALU.add), 5)
            dve.wait_ge(ct_pool, 1)
            link(nc.vector.tensor_scalar(z[B, 0, :], y[B, 0, :], mv["z"][B, 0, 0:1], rs["z"][B, 0:1], ALU.subtract, ALU.mult), Z_)
            dve.wait_ge(ct_pe, 1)
            zps = ps_f[0][:, 0:256].rearrange("p (k t) -> p k t", k=2)
            link(nc.vector.tensor_copy(zt[:, 0, :, 0:128], zps))
            link(nc.vector.tensor_tensor(zt[:, 1, :, 0:128], zps, zt[:, 0, :, 0:128].bitcast(f32), ALU.subtract), ZT_)
            dve.wait_ge(ct_pe, 2)
            link(nc.vector.tensor_tensor(h2[B, 0, :], ps_f[1][B, 0:256], clsr[B, :], ALU.add))
            link(nc.vector.bn_stats(bn["h"][B, 0, :], h2[B, 0, :]))
            link(nc.vector.bn_aggr(mv["h"][B, 0, :], bn["h"][B, 0, :]), VH_)
            dve.wait_ge(ct_pool, 2)
            link(nc.vector.tensor_scalar(xf[B, 0, :], h2[B, 0, :], mv["h"][B, 0, 0:1], rs["h"][B, 0:1], ALU.subtract, ALU.mult), XF_)
            link(nc.vector.bn_stats(bn["x"][B, 0, :], xf[B, 0, :]))
            link(nc.vector.bn_aggr(mv["x"][B, 0, :], bn["x"][B, 0, :]))
            nc.vector.tensor_copy(stats8[B, 0, 0:1], mv["x"][B, 0, 0:1])
            nc.vector.tensor_reduce(stats8[B, 0, 2:3], xf[B, 0, :], AX.X, ALU.min)
            nc.vector.tensor_reduce(stats8[B, 0, 3:4], xf[B, 0, :], AX.X, ALU.max)
            nc.vector.tensor_scalar(sq[B, 0, 0:1], mv["x"][B, 0, 1:2], float(D) / (D - 1), None, ALU.mult)
            link(nc.vector.tensor_tensor(sq[B, 0, 1:2], mv["x"][B, 0, 0:1], mv["x"][B, 0, 0:1], ALU.mult))
            link(nc.vector.tensor_tensor(sq[B, 0, 1:2], sq[B, 0, 1:2], mv["x"][B, 0, 1:2], ALU.add), SQ_)
            dve.wait_ge(ct_act, 1)
            link(nc.vector.tensor_scalar(axf[B, 0, :], axf[B, 0, :], 1e-6, None, ALU.is_lt, ALU.add, accum_out=stats8[B, 0, 5:6]))
            dve.wait_ge(ct_pool, 3)
            link(nc.vector.tensor_copy(stats8[B, 0, 1:2], sq[B, 0, 0:1]))
            link(nc.vector.tensor_scalar(stats8[B, 0, 4:5], sq[B, 0, 1:2], float(D) ** 0.5, None, ALU.mult), ST_)
            dve.wait_ge(ct_pe, 3)
            link(nc.vector.tensor_copy(xft[:, 0, :, 0:128], zps))
            dve.wait_ge(ct_pe, 4)
            nc.vector.tensor_tensor(xft[:, 1, :, 0:128], zps, xft[:, 0, :, 0:128].bitcast(f32), ALU.subtract)
            link(nc.vector.tensor_copy(stt[0:NST, 0:128], ps_av[0][0:NST, 0:128]), XT_)
            dve.wait_ge(ct_pe, 5)
            link(nc.vector.tensor_copy(pre_cls[:, :], ps_f[1][:, 256:384]), PRE_)

        @block.gpsimd
        def _(pool):
            pool.wait_ge(ct_dve, 5)
            nc.gpsimd.tensor_tensor(rs["z"][B, 0:1], ve["z"][B, 0:1], n05[B, 0:1], ALU.pow).then_inc(ct_pool, 1)
            pool.wait_ge(ct_dve, VH_)
            nc.gpsimd.tensor_scalar(ve["h"][B, 0:1], mv["h"][B, 0, 1:2], LN_EPS, None, ALU.add).then_inc(cls_var, 1)
            pool.wait_ge(cls_var, 1)
            nc.gpsimd.tensor_tensor(rs["h"][B, 0:1], ve["h"][B, 0:1], n05[B, 0:1], ALU.pow).then_inc(ct_pool, 1)
            pool.wait_ge(ct_dve, SQ_)
            nc.gpsimd.tensor_tensor(sq[B, 0, :], sq[B, 0, :], n05[B, 2:4], ALU.pow).then_inc(ct_pool, 1)

        @block.scalar
        def _(act):
            def gelu(c):
                act.wait_ge(hid_load[c], 16)
                nc.scalar.activation(hid[c][:, 0:TI * P], hid[c][:, 0:TI * P], ACT.Gelu, bias=r1b_c[:, 0:1]).then_inc(hid_act, 1)

            gelu(0)
            gelu(1)
            act.wait_ge(ct_dve, XF_)
            nc.scalar.activation(axf[B, 0, :], xf[B, 0, :], ACT.Abs).then_inc(ct_act, 1)
            gelu(2)
            gelu(3)
            act.wait_ge(ct_dve, PRE_)
            nc.scalar.activation(pre_cls[:, :], pre_cls[:, :], ACT.Gelu, bias=r1b_c[:, 0:1]).then_inc(hid_act, 1)

        @block.tensor
        def _(pe):
            def logits(c):
                pe.wait_ge(hid_act, c + 1)
                for i in range(TI):
                    q = 4 * i + c
                    nc.tensor.matmul(tiles(q // 32, 32)[:, q % 32, :], hid[c][:, i * P:(i + 1) * P], r2w_sb[:, :], start=True, stop=True)

            pe.wait_ge(ct_dve, Z_)
            for kt in range(2):
                last = nc.tensor.transpose(ps_f[0][:, 128 * kt:128 * kt + 128], z[:, 0, kt * 128:kt * 128 + 128], ident)
            last.then_inc(ct_pe, 1)
            logits(0)
            pe.wait_ge(ct_dve, ZT_)
            for kt in range(2):
                last = mm3(ps_f[1][:, 0:256], (zt[:, 0, kt, 0:128], zt[:, 1, kt, 0:128]), (w2s[:, 0, kt, :], w2s[:, 1, kt, :]), kt == 0, kt == 1)
            last.then_inc(ct_pe, 1)
            logits(1)
            pe.wait_ge(ct_dve, XF_)
            for kt in range(2):
                last = nc.tensor.transpose(ps_f[0][:, 128 * kt:128 * kt + 128], xf[:, 0, kt * 128:kt * 128 + 128], ident)
            last.then_inc(ct_pe, 1)
            pe.wait_ge(ct_dve, ST_)
            nc.tensor.transpose(ps_av[0][0:NST, 0:128], stats8[:, 0, :], ident).then_inc(ct_pe, 1)
            logits(2)
            pe.wait_ge(ct_dve, XT_)
            for kt in range(2):
                mm3(ps_f[1][:, 256:384], (r1ws[:, 0, kt, :], r1ws[:, 1, kt, :]), (xft[:, 0, kt, 0:128], xft[:, 1, kt, 0:128]), kt == 0, False)
            nc.tensor.matmul(ps_f[1][:, 256:384], r1st[:, :], stt[:, 0:128], start=False, stop=True).then_inc(ct_pe, 1)
            logits(3)
            pe.wait_ge(hid_act, 5)
            nc.tensor.matmul(ps_av[1][:, 0:NE], pre_cls[:, :], r2w_sb[:, :], start=True, stop=True)
        classes.close()
        ph1.close()

        WAU = 2 * 2 * INTER
        WDN = WAU + 2 * 2 * AINTER
        WCOL = WDN + 5 * D
        WMID = WDN // 2
        raw_stack = ExitStack()
        raw = [raw_stack.enter_context(nc.sbuf_tensor(f"raw{i}", [P, WCOL], f32)) for i in range(2)]
        up_load = [sem("up_load0"), sem("up_load1")]
        down_load = [sem("down_load0"), sem("down_load1")]

        router = ExitStack()

        def s2(name, shape, dt=f32):
            return router.enter_context(nc.sbuf_tensor(name, shape, dt))

        prob = s2("prob", [P, NQ, NE])
        work = s2("work", [P, NQ, NE])
        first = s2("first", [P, NQ, NE])
        second = s2("second", [P, NQ, NE])
        score_t = s2("score_t", [P, NQ, NE])
        top = s2("top", [P, NQ])
        den = s2("den", [P, NQ])
        v1 = s2("v1", [P, NQ])
        v2 = s2("v2", [P, NQ])
        e0m = s2("e0m", [P, NQ])
        e1m = s2("e1m", [P, NQ])
        slot_f = [s2(f"slot_f{k}", [P, NQ]) for k in range(2)]
        slot_i = [s2(f"slot_i{k}", [P, NQ], i32) for k in range(2)]
        hi_i = [s2(f"hi_i{k}", [P, NQ], i32) for k in range(2)]
        lo_i = [s2(f"lo_i{k}", [P, NQ], i32) for k in range(2)]
        at_lo = [s2(f"at_lo{k}", [P, NQ, P], bf16) for k in range(2)]
        at_hi = [s2(f"at_hi{k}", [P, NQ, 3 * NE], bf16) for k in range(2)]
        hi_t = [s2(f"hi_t{k}", [P, NQ, 3 * NE], bf16) for k in range(2)]
        by_expert = s2("by_expert", [P, 4 * CH])
        HW = NQ * 3 * NE // 2
        hi_p = [by_expert[:, k * HW:k * HW + HW].bitcast(bf16).rearrange("p (q h) -> p q h", q=NQ) for k in range(2)]
        vacant = s2("vacant", [P, 3 * NE])
        source = s2("source", [P, 3 * NE])
        meta = s2("meta", [P, NQ, ROW - D])
        slot_hi = [s2(f"slot_hi{k}", [P, NQ]) for k in range(2)]
        slot_lo = [s2(f"slot_lo{k}", [P, NQ]) for k in range(2)]
        score_e, above, level, rank = (by_expert[:, k * CH:k * CH + CH] for k in range(4))
        clsk = s2("clsk", [P, P])
        cut = s2("cut", [P, 1], i32)
        cand = s2("cand", [P, 1], i32)
        bitf = s2("bitf", [P, 1])
        biti = s2("biti", [P, 1], i32)
        base = s2("base", [P, 1], i32)
        halves = s2("halves", [P, 1])
        sgn = s2("sgn", [P, CH * 3 // 8])
        cnt_act = s2("cnt_act", [P, 1])
        takei = s2("takei", [P, 1], i32)
        cnt = s2("cnt", [P, 4])
        lim = s2("lim", [P, 4])
        groups = [(k, min(32, NT - 32 * k)) for k in range((NT + 31) // 32)]
        banks = [ps_av[0], ps_av[1], ps_f[0], ps_f[1]]
        iota_m = cst[:, CIE:CIE + NE].unsqueeze(1).to_broadcast([P, NQ, NE])

        def wide(t):
            return t[:, :].unsqueeze(2).to_broadcast([P, NQ, NE])

        def flat(t):
            return t[:, :, :].rearrange("p t e -> p (t e)")

        block_stack = ExitStack()
        block = block_stack.enter_context(nc.Block())
        rt_act, rt_pe, rt_dve, rt_pool, sign_done, signs, meta_out = (sem(n) for n in ("rt_act", "rt_pe", "rt_dve", "rt_pool", "sign_done", "signs", "meta_out"))
        SCALE = float(1 << 60)
        BITS = 31
        BODY = 5
        SCA = CH * 3 // 8
        SCV = CH - SCA
        D_PRE, D_LOG, D_SCO, D_SE, D_SEA = 1, 3, 21, 22, 24
        PER = 6
        D_CNT = D_SEA + PER * BITS + 1
        D_SEL, D_V = D_CNT + 4, D_CNT + 8
        D_HOT = D_V + 6
        P_SE, P_SEC = 1, 2
        P_CNT, P_SEL, P_V, P_INV = (P_SEC + BITS + k for k in (1, 2, 3, 4))

        @block.sync
        def _(sp):
            for m in range(2):
                sp.dma_start(raw[m][:, 0:WDN], wexp[m, :, 0:WDN]).then_inc(up_load[m], 16)
            sp.dma_start(raw[0][:, WDN:WCOL], wexp[0, :, WDN:WCOL]).then_inc(down_load[0], 16)
            sp.wait_ge(rt_dve, D_SCO)
            for c in range(4):
                sp.dma_start(token_rows[c * TI * P:(c + 1) * TI * P, D:ROW].rearrange("(i p) w -> p i w", p=P), meta[:, c:NT:4, :]).then_inc(meta_out, 16)
            sp.dma_start(token_rows[NT * P:NQ * P, D:ROW], meta[:, NT, :]).then_inc(meta_out, 16)
            sp.wait_ge(meta_out, 80)

        @block.scalar
        def _(act):
            act.wait_ge(rt_dve, D_LOG)
            nc.scalar.activation(prob[:, :, :], work[:, :, :], ACT.Exp).then_inc(rt_act, 1)

            def sign(b):
                act.wait_ge(rt_dve, b * PER + D_SEA)
                nc.scalar.activation(sgn[:, :], score_e[:, SCV:CH], ACT.Sign, bias=cand[:, 0:1].bitcast(f32), scale=-1.0).then_inc(sign_done, 1)
                act.wait_ge(sign_done, b + 1)
                nc.scalar.activation(above[:, SCV:CH], sgn[:, :], ACT.Sign, bias=halves[:, 0:1], scale=-1.0,
                                     accum_out=cnt_act[:, 0:1]).then_inc(signs, 1)

            sign(0)
            with act.Fori(0, (BITS - 1) // BODY) as i:
                for k in range(BODY):
                    sign(i * BODY + (1 + k))
            for k in range(2):
                act.wait_ge(rt_dve, D_HOT + 2 * k + 1)
                nc.scalar.activation(hi_p[k][:, :, :], at_hi[k][:, :, :], ACT.Copy, scale=cst[:, CP1:CP1 + 1]).then_inc(rt_act, 1)

        @block.tensor
        def _(pe):
            pe.wait_ge(rt_dve, D_SCO)
            for i in range(TI):
                last = nc.tensor.transpose(banks[i // 4][:, 128 * (i % 4):128 * (i % 4) + 128],
                                           score_t[:, 4 * i:4 * i + 4, :].rearrange("p c e -> p (c e)"), ident)
            last.then_inc(rt_pe, 1)
            pe.wait_ge(rt_dve, D_SE)
            nc.tensor.matmul(ps_s[0][:, 0, 0, 0:JN], clsk[0:32, :], cst[0:32, CTJ:CTJ + JN], start=True, stop=True).then_inc(rt_pe, 1)
            def total(b):
                pe.wait_ge(rt_dve, b * PER + (D_SEA + 1))
                nc.tensor.matmul(ps_s[1][:, 0, 0, 0:1], cst[:, CBE:CBE + 128], cnt[:, 0:1], start=True, stop=False)
                pe.wait_ge(signs, b + 1)
                nc.tensor.matmul(ps_s[1][:, 0, 0, 0:1], cst[:, CBH:CBH + 128], cnt_act[:, 0:1], start=False, stop=True).then_inc(rt_pe, 1)

            total(0)
            with pe.Fori(0, (BITS - 1) // BODY) as i:
                for k in range(BODY):
                    total(i * BODY + (1 + k))
            pe.wait_ge(rt_dve, D_CNT)
            nc.tensor.matmul(ps_s[1][:, 0, 0, 0:1], cst[:, CBE:CBE + 128], cnt[:, 1:2], start=True, stop=True)
            nc.tensor.matmul(ps_s[1][:, 0, 0, 1:2], cst[:, CLE:CLE + 128], cnt[:, 2:3], start=True, stop=True).then_inc(rt_pe, 1)
            pe.wait_ge(rt_dve, D_SEL)
            nc.tensor.matmul(ps_s[1][:, 0, 0, 2:3], cst[:, CLE:CLE + 128], cnt[:, 3:4], start=True, stop=True).then_inc(rt_pe, 1)
            pe.wait_ge(rt_dve, D_V)
            for i in range(TI):
                at_ = S * (i // 2) + 1 + 128 * (i % 2)
                nc.tensor.transpose(tiles((4 * i) // 32, 32)[:, (4 * i) % 32:(4 * i) % 32 + 4, :].rearrange("p c e -> p (c e)"),
                                    level[:, at_:at_ + 128], ident)
            nc.tensor.matmul(ps_av[0][0:NB, 0:NE], clsk[:, 0:NB], cst[:, CBE:CBE + NE], start=True, stop=True).then_inc(rt_pe, 1)
            for k in range(2):
                pe.wait_ge(rt_dve, D_HOT + 2 * k + 2)
                for half, (rhs, ready, count) in enumerate(((hi_p[k], rt_act, 2 + k), (hi_t[k], rt_pool, k + 1))):
                    pe.wait_ge(ready, count)
                    for q in range(NQ):
                        last = nc.tensor.matmul(ps_f[half][:, 0:3 * NE], at_lo[k][:, q, :], rhs[:, q, :],
                                                start=k == 0 and q == 0, stop=k == 1 and q == NQ - 1)
            last.then_inc(rt_pe, 1)

        @block.vector
        def _(dve):
            link = chain(dve, rt_dve)
            for k in range(2):
                nc.vector.memset(slot_f[k][:, NT:NQ], float(OOB))
            nc.vector.memset(cut[:, :], 0)
            nc.vector.memset(cand[:, :], 1 << (BITS - 1))
            nc.vector.memset(halves[:, :], 0.5)
            link(nc.vector.memset(bitf[:, :], float(1 << (BITS - 1))), D_PRE)
            for k, n in groups:
                nc.vector.tensor_reduce(top[:, 32 * k:32 * k + n], tiles(k, n), AX.X, ALU.max)
            link(nc.vector.tensor_reduce(top[:, NT:NQ], ps_av[1][:, 0:NE], AX.X, ALU.max))
            for k, n in groups:
                nc.vector.tensor_tensor(work[:, 32 * k:32 * k + n, :], tiles(k, n),
                                        top[:, 32 * k:32 * k + n].unsqueeze(2).to_broadcast([P, n, NE]), ALU.subtract)
            link(nc.vector.tensor_tensor(work[:, NT, :], ps_av[1][:, 0:NE], top[:, NT:NQ].to_broadcast([P, NE]), ALU.subtract), D_LOG)
            dve.wait_ge(rt_act, 1)
            link(nc.vector.tensor_reduce(den[:, :], prob[:, :, :], AX.X, ALU.add))
            link(nc.vector.reciprocal(den[:, :], den[:, :]))
            link(nc.vector.tensor_tensor(prob[:, :, :], prob[:, :, :], wide(den), ALU.mult))
            link(nc.vector.tensor_reduce(v1[:, :], prob[:, :, :], AX.X, ALU.max))
            link(nc.vector.tensor_tensor(work[:, :, :], prob[:, :, :], wide(v1), ALU.is_equal))
            link(nc.vector.tensor_tensor(work[:, :, :], work[:, :, :], iota_m, ALU.mult))
            link(nc.vector.tensor_reduce(e0m[:, :], work[:, :, :], AX.X, ALU.min))
            link(nc.vector.tensor_tensor(first[:, :, :], iota_m, wide(e0m), ALU.is_equal))
            link(nc.vector.scalar_tensor_tensor(flat(score_t), flat(first), -2.0, flat(prob), ALU.mult, ALU.add))
            link(nc.vector.tensor_reduce(v2[:, :], score_t[:, :, :], AX.X, ALU.max))
            link(nc.vector.tensor_tensor(work[:, :, :], score_t[:, :, :], wide(v2), ALU.is_equal))
            link(nc.vector.tensor_tensor(work[:, :, :], work[:, :, :], iota_m, ALU.mult))
            link(nc.vector.tensor_reduce(e1m[:, :], work[:, :, :], AX.X, ALU.min))
            link(nc.vector.tensor_tensor(second[:, :, :], iota_m, wide(e1m), ALU.is_equal))
            link(nc.vector.tensor_tensor(work[:, :, :], first[:, :, :], second[:, :, :], ALU.add))
            nc.vector.tensor_tensor(den[:, :], v1[:, :], v2[:, :], ALU.add)
            link(nc.vector.tensor_tensor(prob[:, :, :], prob[:, :, :], work[:, :, :], ALU.mult))
            nc.vector.reciprocal(top[:, :], den[:, :])
            link(nc.vector.scalar_tensor_tensor(flat(score_t), flat(work), -1.0, flat(prob), ALU.add, ALU.add))
            nc.vector.tensor_copy(meta[:, :, 3].bitcast(i32), cst[:, CTI:CTI + NQ])
            nc.vector.tensor_tensor(meta[:, :, 0], v1[:, :], top[:, :], ALU.mult)
            nc.vector.tensor_tensor(meta[:, :, 1], v2[:, :], top[:, :], ALU.mult)
            link(nc.vector.tensor_scalar(meta[:, :, 2], e0m[:, :], 64.0, None, ALU.add), D_SCO)
            link(nc.vector.tensor_tensor(clsk[0:32, :].rearrange("p (c e) -> p c e", c=4),
                                         score_t[0:32, NT, :].unsqueeze(1).to_broadcast([32, 4, NE]),
                                         cst[0:32, CTK:CTK + 4].unsqueeze(2).to_broadcast([32, 4, NE]), ALU.mult), D_SE)
            dve.wait_ge(rt_pe, P_SE)
            se = score_e[:, :].rearrange("p (j s) -> p j s", s=S)
            for b in range((TI + 3) // 4):
                last = nc.vector.tensor_scalar(se[:, 2 * b:2 * b + 2, 1:S], banks[b][:, :].rearrange("p (j s) -> p j s", j=2),
                                               SCALE, None, ALU.mult)
            link(last)
            dve.wait_ge(rt_pe, P_SEC)
            link(nc.vector.tensor_scalar(se[:, :, 0], ps_s[0][:, 0, 0, 0:JN], SCALE, None, ALU.mult), D_SEA)
            def search(b):
                n = b * PER + D_SEA

                def step(ins, k):
                    ins.then_inc(rt_dve, 1)
                    dve.wait_ge(rt_dve, n + k)

                nc.vector.tensor_scalar(above[:, 0:SCV], score_e[:, 0:SCV], cand[:, 0:1].bitcast(f32), None, ALU.is_ge, ALU.add,
                                        accum_out=cnt[:, 0:1]).then_inc(rt_dve, 1)
                step(nc.vector.tensor_scalar(biti[:, :], bitf[:, :], 0.5, None, ALU.mult), 2)
                step(nc.vector.tensor_tensor(base[:, :], cut[:, :], biti[:, :], ALU.bitwise_or), 3)
                dve.wait_ge(rt_pe, b + (P_SEC + 1))
                step(nc.vector.tensor_scalar(takei[:, :], ps_s[1][:, 0, 0, 0:1], float(CAP) - 0.5 * 4 * SCA, bitf[:, 0:1],
                                             ALU.is_ge, ALU.mult), 4)
                nc.vector.tensor_tensor(cand[:, :], base[:, :], takei[:, :], ALU.bitwise_or).then_inc(rt_dve, 1)
                nc.vector.tensor_tensor(cut[:, :], cut[:, :], takei[:, :], ALU.bitwise_or)
                step(nc.vector.tensor_scalar(bitf[:, :], bitf[:, :], 0.5, None, ALU.mult), 6)

            search(0)
            with dve.Fori(0, (BITS - 1) // BODY) as i:
                for k in range(BODY):
                    search(i * BODY + (1 + k))
            link.tally[0] += PER * BITS
            nc.vector.tensor_scalar(above[:, :], score_e[:, :], cut[:, 0:1].bitcast(f32), None, ALU.is_gt, ALU.add, accum_out=cnt[:, 1:2])
            link(nc.vector.tensor_scalar(level[:, :], score_e[:, :], cut[:, 0:1].bitcast(f32), None, ALU.is_equal, ALU.add,
                                         accum_out=cnt[:, 2:3]))
            dve.wait_ge(rt_pe, P_CNT)
            nc.vector.tensor_scalar(lim[:, 0:1], ps_s[1][:, 0, 0, 0:1], -1.0, float(CAP), ALU.mult, ALU.add)
            link(nc.vector.tensor_copy(lim[:, 1:2], ps_s[1][:, 0, 0, 1:2]))
            link(nc.vector.tensor_tensor_scan(rank[:, :], level[:, :], level[:, :], lim[:, 1:2], ALU.add, ALU.bypass))
            link(nc.vector.scalar_tensor_tensor(level[:, :], rank[:, :], lim[:, 0:1], level[:, :], ALU.is_le, ALU.mult))
            link(nc.vector.scalar_tensor_tensor(above[:, :], above[:, :], 0.0, level[:, :], ALU.add, ALU.add, accum_out=cnt[:, 3:4]), D_SEL)
            dve.wait_ge(rt_pe, P_SEL)
            link(nc.vector.tensor_copy(lim[:, 2:3], ps_s[1][:, 0, 0, 2:3]))
            link(nc.vector.tensor_tensor_scan(rank[:, :], above[:, :], above[:, :], lim[:, 2:3], ALU.add, ALU.bypass))
            link(nc.vector.scalar_tensor_tensor(level[:, :], rank[:, :], cst[:, CSB:CSB + 1], above[:, :], ALU.add, ALU.mult))
            link(nc.vector.tensor_tensor(clsk[:, 0:NB].rearrange("p (c j) -> p c j", c=4),
                                         level[:, :].rearrange("p (j s) -> p j s", s=S)[:, :, 0].unsqueeze(1).to_broadcast([P, 4, JN]),
                                         cst[:, CTM:CTM + NB].rearrange("p (c j) -> p c j", c=4), ALU.mult), D_V)
            dve.wait_ge(rt_pe, P_V)
            for onehot, wk in ((first, work), (second, prob)):
                for g_, n in groups:
                    nc.vector.tensor_tensor(wk[:, 32 * g_:32 * g_ + n, :], tiles(g_, n), onehot[:, 32 * g_:32 * g_ + n, :], ALU.mult)
                last = nc.vector.tensor_tensor(wk[0:NB, NT, :], ps_av[0][0:NB, 0:NE], onehot[0:NB, NT, :], ALU.mult)
            link(last)
            for k, wk in enumerate((work, prob)):
                nc.vector.tensor_reduce(slot_f[k][:, 0:NT], wk[:, 0:NT, :], AX.X, ALU.add)
                last = nc.vector.tensor_reduce(v1[0:NB, k:k + 1], wk[0:NB, NT, :], AX.X, ALU.add)
            link(last)
            for k in range(2):
                nc.vector.tensor_scalar(slot_f[k][:, 0:NT], slot_f[k][:, 0:NT], float(OOB), None, ALU.add)
                last = nc.vector.tensor_scalar(slot_f[k][0:NB, NT:NQ], v1[0:NB, k:k + 1], float(OOB), None, ALU.add)
            link(last)
            for k in range(2):
                last = nc.vector.tensor_copy(slot_i[k][:, :], slot_f[k][:, :])
            link(last)
            for k in range(2):
                nc.vector.tensor_scalar(hi_i[k][:, :], slot_i[k][:, :], 7, None, ALU.arith_shift_right)
                last = nc.vector.tensor_scalar(lo_i[k][:, :], slot_i[k][:, :], P - 1, None, ALU.bitwise_and)
            link(last)
            for k in range(2):
                nc.vector.tensor_copy(slot_hi[k][:, :], hi_i[k][:, :])
                last = nc.vector.tensor_copy(slot_lo[k][:, :], lo_i[k][:, :])
            link(last, D_HOT)
            for k in range(2):
                link(nc.vector.tensor_tensor(at_hi[k][:, :, :], cst[:, CIO:CIO + 3 * NE].unsqueeze(1).to_broadcast([P, NQ, 3 * NE]),
                                             slot_hi[k][:, :].unsqueeze(2).to_broadcast([P, NQ, 3 * NE]), ALU.is_equal))
                link(nc.vector.tensor_tensor(at_lo[k][:, :, :], cst[:, CIO:CIO + P].unsqueeze(1).to_broadcast([P, NQ, P]),
                                             slot_lo[k][:, :].unsqueeze(2).to_broadcast([P, NQ, P]), ALU.is_equal))
            dve.wait_ge(rt_pe, P_INV)
            nc.vector.tensor_scalar(vacant[:, :], ps_f[0][:, 0:3 * NE], 0.0, None, ALU.is_equal)
            link(nc.vector.tensor_scalar(source[:, :], ps_f[1][:, 0:3 * NE], float(P), -1.0, ALU.mult, ALU.add))
            nc.vector.tensor_tensor(vacant[:, :], vacant[:, :], cst[:, CEM:CEM + 3 * NE], ALU.mult)
            link(nc.vector.tensor_tensor(source[:, :], source[:, :], ps_f[0][:, 0:3 * NE], ALU.add))
            link(nc.vector.tensor_tensor(slot_token[:, :], source[:, :], vacant[:, :], ALU.add))

        @block.gpsimd
        def _(pool):
            for k in range(2):
                pool.wait_ge(rt_dve, D_HOT + 2 * k + 1)
                nc.gpsimd.tensor_tensor(hi_t[k][:, :, :], at_hi[k][:, :, :],
                                        cst[:, CTN:CTN + NQ].unsqueeze(2).to_broadcast([P, NQ, 3 * NE]), ALU.mult).then_inc(rt_pool, 1)
        block_stack.close()
        router.close()

        CW = CAP + CAP % 2
        slot_tiles = [(s0, min(P, CW - s0)) for s0 in range(0, CW, P)]
        ST = len(slot_tiles)
        experts = ExitStack()

        def s3(name, shape, dt=f32):
            return experts.enter_context(nc.sbuf_tensor(name, shape, dt))

        whi = [s3(f"whi{i}", [P, WCOL], f32r) for i in range(2)]
        wlo = [s3(f"wlo{i}", [P, WCOL], f32r) for i in range(2)]
        xe = [s3(f"xe{i}", [P, ST, ROW]) for i in range(2)]
        xet = [s3(f"xet{i}", [P, 2, 2, CW], f32r) for i in range(2)]
        hs = [s3(f"hs{i}", [P, 2, 5, CW], f32r) for i in range(2)]
        sg = [s3(f"sg{i}", [P, CW]) for i in range(2)]
        hm = [s3(f"hm{i}", [P, CW]) for i in range(2)]
        ye = [s3(f"ye{i}", [P, ST, D]) for i in range(2)]
        weight = [s3(f"weight{i}", [P, ST]) for i in range(2)]
        is0 = [s3(f"is0{i}", [P, ST]) for i in range(2)]
        wd = [s3(f"wd{i}", [P, ST]) for i in range(2)]
        which = [s3(f"which{i}", [P, ST], i32) for i in range(2)]
        tok = [s3(f"tok{i}", [P, ST], i32) for i in range(2)]
        spare = s3("spare_pool", [1, 1])
        enum = s3("enum", [P, 1])
        xe_load = [sem("xe_load0"), sem("xe_load1")]
        w_hi_up, w_hi_dn, w_lo_up, w_lo_dn, xet_ps, xet_hi, xet_done = (sem(n) for n in ("w_hi_up", "w_hi_dn", "w_lo_up", "w_lo_dn", "xet_ps", "xet_hi", "xet_done"))
        up_ps, gate_act, h_done, h_hi, h_lo, down_ps, ye_done = (sem(n) for n in ("up_ps", "gate_act", "h_done", "h_hi", "h_lo", "down_ps", "ye_done"))
        is_first, w_diff, w_part, w_ready, tok_ready, added = (sem(n) for n in ("is_first", "w_diff", "w_part", "w_ready", "tok_ready", "added"))
        enum_set, carried, which_ready = sem("enum_set"), sem("carried"), sem("which_ready")

        def there(m):
            return not isinstance(m, int) or 0 <= m < NE

        def expert_steps(eng, body):
            for n in range(-1, 4):
                body(n, n % 2)
            with eng.Fori(0, (NE - 8) // 2) as i:
                for k in range(2):
                    body(i * 2 + (4 + k), k)
            for n in range(NE - 4, NE + 1):
                body(n, n % 2)

        block_stack = ExitStack()
        block = block_stack.enter_context(nc.Block())

        def load_count(m, r, per):
            return (m // 2 + 1) * per if isinstance(m, int) else (m + (2 - r)) * (per // 2)

        @block.sync
        def _(sp):
            def load_up(m, r):
                if there(m):
                    wait(sp, w_lo_up, 2 * (m - 1))
                    sp.dma_start(raw[r][:, 0:WDN], wexp[bass.ds(m, 1), :, 0:WDN].rearrange("o p w -> (o p) w")).then_inc(up_load[r], 16)

            def load_down(m, r):
                if there(m):
                    wait(sp, w_lo_dn, m - 1)
                    sp.dma_start(raw[r][:, WDN:WCOL], wexp[bass.ds(m, 1), :, WDN:WCOL].rearrange("o p w -> (o p) w")).then_inc(down_load[r], 16)

            def body(n, r):
                if not isinstance(n, int) or n >= 0:
                    load_down(n + 1, 1 - r)
                load_up(n + 3, 1 - r)

            expert_steps(sp, body)

        @block.tensor
        def _(pe):
            def up(n, r, j):
                if j == 0:
                    pe.wait_ge(w_hi_up, 2 * n + 2)
                    pe.wait_ge(w_lo_up, 2 * n + 2)
                    pe.wait_ge(xet_done, n + 1)
                b = (5 * r + j) % 2
                wait(pe, h_done, 5 * n + j - 1)
                for part in range(2):
                    for kt in range(2):
                        if j < 4:
                            col = kt * 1024 + part * INTER + j * 128
                        else:
                            col = WAU + kt * 2 * AINTER + part * AINTER
                        last = mm3(ps_s[b][:, part, :, :].rearrange("p k q -> p (k q)")[:, 0:CW],
                                   (whi[r][:, col:col + 128], wlo[r][:, col:col + 128]),
                                   (xet[r][:, 0, kt, :], xet[r][:, 1, kt, :]), kt == 0, kt == 1)
                last.then_inc(up_ps, 1)

            def down(m, r):
                pe.wait_ge(h_lo, 5 * m + 5)
                pe.wait_ge(w_hi_dn, m + 1)
                pe.wait_ge(w_lo_dn, m + 1)
                for st, (s0, w) in enumerate(slot_tiles):
                    wait(pe, ye_done, ST * m + st - 1)
                    for j in range(5):
                        col = WDN + j * D
                        last = mm3(ps_av[(ST * r + st) % 2][0:w, 0:D], (hs[r][:, 0, j, s0:s0 + w], hs[r][:, 1, j, s0:s0 + w]),
                                   (whi[r][:, col:col + D], wlo[r][:, col:col + D]), j == 0, j == 4)
                    last.then_inc(down_ps, 1)

            def body(n, r):
                if there(n):
                    up(n, r, 0)
                    up(n, r, 1)
                if there(n + 1):
                    pe.wait_ge(xe_load[1 - r], load_count(n + 1, 1 - r, 16 * ST))
                    wait(pe, xet_done, n + 1)
                    for kt in range(2):
                        for st, (s0, w) in enumerate(slot_tiles):
                            last = nc.tensor.transpose(ps_f[kt][:, s0:s0 + w], xe[1 - r][0:w, st, kt * 128:kt * 128 + 128], ident[0:w, 0:w])
                    last.then_inc(xet_ps, 1)
                if there(n - 1):
                    down(n - 1, 1 - r)
                if there(n):
                    up(n, r, 2)
                    up(n, r, 3)
                if there(n):
                    up(n, r, 4)

            expert_steps(pe, body)

        @block.scalar
        def _(act):
            def gate(n, r, j):
                act.wait_ge(up_ps, 5 * n + j + 1)
                wait(act, h_done, 5 * n + j - 1)
                b = (5 * r + j) % 2
                nc.scalar.activation(sg[b][:, :], ps_s[b][:, 0, :, :].rearrange("p k q -> p (k q)")[:, 0:CW], ACT.Silu).then_inc(gate_act, 1)

            def split(m, r, part):
                if not there(m):
                    return
                if part == 0:
                    act.wait_ge(up_load[r], load_count(m, r, 16))
                    wait(act, up_ps, 5 * (m - 1))
                if part == 2:
                    act.wait_ge(down_load[r], load_count(m, r, 16))
                    wait(act, down_ps, ST * (m - 1))
                lo, hi = ((0, WMID), (WMID, WDN), (WDN, WCOL))[part]
                nc.scalar.activation(whi[r][:, lo:hi], raw[r][:, lo:hi], ACT.Copy).then_inc(w_hi_dn if part == 2 else w_hi_up, 1)

            def body(n, r):
                split(n + 1, 1 - r, 0)
                if there(n):
                    gate(n, r, 0)
                split(n + 1, 1 - r, 1)
                if there(n):
                    gate(n, r, 1)
                split(n, r, 2)
                if there(n - 1):
                    act.wait_ge(w_ready, n)
                    wait(act, added, 16 * ST * (n - 2))
                    for st, (s0, w) in enumerate(slot_tiles):
                        act.wait_ge(down_ps, ST * (n - 1) + st + 1)
                        nc.scalar.activation(ye[1 - r][0:w, st, :], ps_av[(ST * (1 - r) + st) % 2][0:w, 0:D], ACT.Copy,
                                             scale=weight[1 - r][0:w, st:st + 1]).then_inc(ye_done, 1)
                if there(n):
                    gate(n, r, 2)
                if there(n):
                    gate(n, r, 3)
                    gate(n, r, 4)

            expert_steps(act, body)

        @block.vector
        def _(dve):
            def hidden(n, r, j):
                b = (5 * r + j) % 2
                dve.wait_ge(gate_act, 5 * n + j + 1)
                wait(dve, down_ps, ST * (n - 1))
                o = ps_s[b][:, 1, :, :].rearrange("p k q -> p (k q)")[:, 0:CW]
                wait(dve, h_lo, 5 * n + j - 1)
                if j < 4:
                    nc.vector.tensor_tensor(hm[b][:, :], o, sg[b][:, :], ALU.mult).then_inc(h_done, 1)
                else:
                    nc.vector.scalar_tensor_tensor(hm[b][:, :], o, 0.05, sg[b][:, :], ALU.mult, ALU.mult).then_inc(h_done, 1)
                dve.wait_ge(h_done, 5 * n + j + 1)
                nc.vector.tensor_copy(hs[r][:, 0, j, :], hm[b][:, :]).then_inc(h_hi, 1)
                dve.wait_ge(h_hi, 5 * n + j + 1)
                nc.vector.tensor_tensor(hs[r][:, 1, j, :], hm[b][:, :], hs[r][:, 0, j, :].bitcast(f32), ALU.subtract).then_inc(h_lo, 1)

            def row_weight(m, r):
                dve.wait_ge(xe_load[r], load_count(m, r, 16 * ST))
                if not isinstance(m, int) or m > 0:
                    wait(dve, w_ready, m)
                    nc.vector.tensor_scalar(enum[:, :], enum[:, :], 1.0, None, ALU.add).then_inc(enum_set, 1)
                else:
                    nc.vector.memset(enum[:, :], 0.0).then_inc(enum_set, 1)
                dve.wait_ge(enum_set, m + 1)
                wait(dve, ye_done, ST * (m - 1))
                nc.vector.tensor_scalar(is0[r][:, :], xe[r][:, :, D + 2], enum[:, 0:1], None, ALU.is_equal).then_inc(is_first, 1)
                dve.wait_ge(is_first, m + 1)
                nc.vector.tensor_scalar(wd[r][:, :], is0[r][:, :], -1.0, 1.0, ALU.mult, ALU.add).then_inc(w_diff, 1)
                dve.wait_ge(w_diff, m + 1)
                nc.vector.tensor_tensor(is0[r][:, :], is0[r][:, :], xe[r][:, :, D], ALU.mult)
                nc.vector.tensor_tensor(wd[r][:, :], wd[r][:, :], xe[r][:, :, D + 1], ALU.mult).then_inc(w_part, 1)
                dve.wait_ge(w_part, m + 1)
                nc.vector.tensor_tensor(weight[r][:, :], is0[r][:, :], wd[r][:, :], ALU.add).then_inc(w_ready, 1)

            def body(n, r):
                if there(n):
                    hidden(n, r, 0)
                    hidden(n, r, 1)
                if there(n + 1):
                    dve.wait_ge(xet_ps, n + 2)
                    for kt in range(2):
                        last = nc.vector.tensor_copy(xet[1 - r][:, 0, kt, :], ps_f[kt][:, 0:CW])
                    last.then_inc(xet_hi, 1)
                    dve.wait_ge(xet_hi, n + 2)
                    for kt in range(2):
                        last = nc.vector.tensor_tensor(xet[1 - r][:, 1, kt, :], ps_f[kt][:, 0:CW], xet[1 - r][:, 0, kt, :].bitcast(f32), ALU.subtract)
                    last.then_inc(xet_done, 1)
                if there(n):
                    dve.wait_ge(w_hi_dn, n + 1)
                    nc.vector.tensor_tensor(wlo[r][:, WDN:WCOL], raw[r][:, WDN:WCOL], whi[r][:, WDN:WCOL].bitcast(f32),
                                            ALU.subtract).then_inc(w_lo_dn, 1)
                    hidden(n, r, 2)
                if there(n + 1):
                    row_weight(n + 1, 1 - r)
                if there(n):
                    hidden(n, r, 3)
                if there(n + 1):
                    wait(dve, added, 16 * ST * n)
                    nc.vector.tensor_copy(tok[1 - r][:, :], xe[1 - r][:, :, D + 3].bitcast(i32)).then_inc(tok_ready, 1)
                if there(n):
                    hidden(n, r, 4)

            expert_steps(dve, body)

        @block.gpsimd
        def _(pool):
            last_row = pool.to_reg(NTOK + SLOTS - 1)
            last_token = pool.to_reg(NQ * P + SLOTS - 1)

            def carry(count):
                wait(pool, carried, count)
                nc.gpsimd.tensor_tensor(spare[:, :], ident[0:1, 0:1], ident[0:1, 0:1], ALU.add).then_inc(carried, 1)

            def adds_before(n):
                return max(0, n) if isinstance(n, int) else n

            def gathers_before(n):
                return min(NE, n + 2) if isinstance(n, int) else n + 2

            def gather(m, r):
                first = 3 * m if isinstance(m, int) else bass.ds(3 * m, ST)
                places = slot_token[:, first:first + ST] if isinstance(m, int) else slot_token[:, first]
                nc.gpsimd.tensor_copy(which[r][:, :], places).then_inc(which_ready, 1)
                pool.wait_ge(which_ready, m + 1)
                wait(pool, xet_ps, m - 1)
                wait(pool, w_ready, m - 1)
                wait(pool, tok_ready, m - 1)
                carry(m if isinstance(m, int) and m < 2 else m + ST * adds_before(m - 2))
                for st in range(ST):
                    nc.gpsimd.indirect_dma_start(
                        out=xe[r][:, st, :], out_offset=None, in_=token_rows,
                        in_offset=bass.IndirectOffsetOnAxis(ap=which[r][:, st:st + 1], axis=0),
                        bounds_check=last_token, oob_is_err=True).then_inc(xe_load[r], 16)

            def body(n, r):
                if isinstance(n, int) and n == -1:
                    gather(0, 0)
                    gather(1, 1)
                if there(n + 1):
                    for part, (lo, hi) in enumerate(((0, WMID), (WMID, WDN))):
                        pool.wait_ge(w_hi_up, 2 * (n + 1) + part + 1)
                        nc.gpsimd.tensor_tensor(wlo[1 - r][:, lo:hi], raw[1 - r][:, lo:hi], whi[1 - r][:, lo:hi].bitcast(f32),
                                                ALU.subtract).then_inc(w_lo_up, 1)
                if there(n - 1):
                    pool.wait_ge(tok_ready, n)
                    wait(pool, added, 16 * ST * (n - 1))
                    for st, (s0, w) in enumerate(slot_tiles):
                        pool.wait_ge(ye_done, ST * (n - 1) + st + 1)
                        carry(ST * (n - 1) + st + gathers_before(n))
                        nc.gpsimd.indirect_dma_start(
                            out=out, out_offset=bass.IndirectOffsetOnAxis(ap=tok[1 - r][0:w, st:st + 1], axis=0),
                            in_=ye[1 - r][0:w, st, :], in_offset=None, bounds_check=last_row, oob_is_err=True,
                            compute_op=ALU.add).then_inc(added, 16)
                if there(n + 2) and (not isinstance(n, int) or n >= 0):
                    gather(n + 2, r)

            expert_steps(pool, body)
            pool.wait_ge(added, 16 * ST * NE)
        block_stack.close()
        experts.close()
        raw_stack.close()


def layouts(x, cls_tok, scharr, W1, b1, W2, b2, gamma, beta, r1_w, r1_b, r2_w, w_up, w_down, a_up, a_down):
    def by_lane(t):
        return t.reshape(t.shape[:-1] + (2, H // 2, DH)).swapaxes(-1, -2).reshape(t.shape[:-1] + (D,))

    def spread(t):
        return np.broadcast_to(t.reshape(1, -1), (P, t.size))

    def k_tiles(t):
        e, o, i = t.shape
        return t.transpose(0, 2, 1).reshape(e, i // P, P, o).transpose(0, 2, 1, 3).reshape(e, P, i // P * o)

    def two(t):
        return np.repeat(t, NE // NG, 0)

    arrays = dict(
        x=x, cls_rows=spread(cls_tok),
        w1=np.concatenate([W1[:, 0:2 * D], by_lane(W1[:, 2 * D:3 * D]), by_lane(W1[:, 3 * D:4 * D])], 1),
        b1uv=spread(b1[0:2 * D]),
        b1qk=np.concatenate([by_lane(b1[2 * D:3 * D]), by_lane(b1[3 * D:4 * D])]).reshape(4, P).T,
        w2=W2, b2=spread(b2),
        gb=np.concatenate([gamma.reshape(2, P).T, beta.reshape(2, P).T], 1),
        taps=spread(scharr), r1w=r1_w.T[0:D], r1s=r1_w.T[D:], r1b=r1_b.reshape(HID, 1), r2w=r2_w.T,
        wexp=np.concatenate([k_tiles(w_up), two(k_tiles(a_up)), k_tiles(w_down), two(k_tiles(a_down))], 2),
        consts=constants(x.shape[0]))
    return {k: np.ascontiguousarray(v) for k, v in arrays.items()}


def kernel(x, cls_tok, L0_tok_scharr, L0_attn_W1, L0_attn_b1, L0_attn_W2, L0_attn_b2, L0_attn_gamma, L0_attn_beta,
           L0_ffn_r1_w, L0_ffn_r1_b, L0_ffn_r2_w, L0_ffn_w_up, L0_ffn_w_down, L0_ffn_a_up, L0_ffn_a_down):
    import concourse.bacc as bacc
    from concourse.bass_utils import run_bass_kernel_spmd

    given = (x, cls_tok, L0_tok_scharr, L0_attn_W1, L0_attn_b1, L0_attn_W2, L0_attn_b2, L0_attn_gamma, L0_attn_beta,
             L0_ffn_r1_w, L0_ffn_r1_b, L0_ffn_r2_w, L0_ffn_w_up, L0_ffn_w_down, L0_ffn_a_up, L0_ffn_a_down)
    laid = layouts(*[np.asarray(t) for t in given])
    nb = laid["x"].shape[0]
    nc = bacc.Bacc("TRN2", target_bir_lowering=False, num_devices=1)
    arrays, args = {}, []
    for name, a in laid.items():
        arrays[f"in_{name}"] = a
        args.append(nc.dram_tensor(f"in_{name}", a.shape, mybir.dt.from_np(a.dtype), kind="ExternalInput").ap())
    args.append(nc.dram_tensor("out_rows", [nb * S + SLOTS, D], mybir.dt.float32, kind="ExternalOutput").ap())
    build(nc, *args, NB=nb, CAP=int(CAP_FACTOR * nb * S / NE))
    r = run_bass_kernel_spmd(nc, [arrays], core_ids=[0])
    return r.results[0]["out_rows"][0:nb * S].reshape(nb, S, D)
```
